# Optimizing a Trainium2 kernel written in Bass

```python
import numpy as np
import jax
import jax.numpy as jnp

def _softmax(x, axis=-1):
    return jax.nn.softmax(x, axis=axis)

def _gelu(x):
    return jax.nn.gelu(x, approximate=True)

def _silu(x):
    return jax.nn.silu(x)

def _sigmoid(x):
    return jax.nn.sigmoid(x)

def _layernorm(x, axis=-1, eps=1e-05):
    m = jnp.mean(x, axis=axis, keepdims=True)
    v = jnp.var(x, axis=axis, keepdims=True)
    return (x - m) / jnp.sqrt(v + eps)

def _scatter_add(tgt, idx, src, axis=0):
    return tgt.at[idx].add(src)

def _segment_sum(src, seg, n):
    return jax.ops.segment_sum(src, seg, n)
kernel_name = 'mk_flamingo_gated_d2_seqx_r8_d5ba0e'

def setup_inputs(seed: int=0):
    np.random.seed(seed)
    _w = jnp.asarray

    def _rec_inputs():
        import jax
        import jax.numpy as jnp
        _rk = jax.random.key(seed)
        x = 7.22e-05 + 1 * jax.random.normal(jax.random.fold_in(_rk, 1), (32, 64, 512), jnp.float32)
        _lenS = 64 - jax.random.randint(jax.random.fold_in(_rk, 7), (32,), 0, max(1, 64 // 4) + 1, jnp.int32)
        _lenS2 = 64 - jax.random.randint(jax.random.fold_in(_rk, 8), (32,), 0, max(1, 64 // 4) + 1, jnp.int32)
        _ctx_4096P = jax.random.normal(jax.random.fold_in(_rk, 11), (32, 16, 512), jnp.float32)
        _ctx_4096c = jax.random.dirichlet(jax.random.fold_in(_rk, 511), 0.3 * jnp.ones((16,), jnp.float32), (32, 64))
        _ctx_4096t = jnp.einsum('bsk,bkd->bsd', _ctx_4096c, _ctx_4096P)
        _ctx_4096t = _ctx_4096t * jax.lax.rsqrt(jnp.mean(jnp.square(_ctx_4096t)) + 1e-12) * 0.953939
        ctx_4096 = 4.13588e-05 + 0.999923 * (_ctx_4096t + 0.3 * jax.random.normal(jax.random.fold_in(_rk, 611), (32, 64, 512), jnp.float32))
        _g = jax.random.normal(jax.random.fold_in(_rk, 9001), (2, 2), jnp.float32)
        _g = jnp.sign(_g) * jnp.maximum(jnp.abs(_g), 1.0) + (_g == 0) * 1.0
        g_xattn = _g[0]
        g_ffn = _g[1]
        return (x, ctx_4096, g_xattn, g_ffn)
    x, ctx_4096, g_xattn, g_ffn = _rec_inputs()

    def _L0_xattn_setup():
        import jax, jax.numpy as jnp
        import numpy as np
        HEADS = 8
        WINDOW = 16

        def _pointwise(W, b, t):
            return jnp.einsum('oc,bct->bot', W, t) + b[None, :, None]
        key = jax.random.key(seed)
        ks = jax.random.split(key, 10)
        B, C, T = (4, 64, 512)
        s = 0.02
        return {'x': jax.random.normal(ks[0], (B, C, T), jnp.float32), 'cond': jax.random.normal(ks[1], (B, C, T), jnp.float32), 'Wq': jax.random.normal(ks[2], (C, C), jnp.float32) * s, 'bq': jnp.zeros((C,), jnp.float32), 'Wk': jax.random.normal(ks[3], (C, C), jnp.float32) * s, 'bk': jnp.zeros((C,), jnp.float32), 'Wv': jax.random.normal(ks[4], (C, C), jnp.float32) * s, 'bv': jnp.zeros((C,), jnp.float32), 'Wo': jax.random.normal(ks[5], (C, C), jnp.float32) * s, 'bo': jnp.zeros((C,), jnp.float32)}
    _L0_xattn_all = _L0_xattn_setup()
    _L0_xattn_in = {k: v for k, v in _L0_xattn_all.items() if k in ('Wq', 'bq', 'Wk', 'bk', 'Wv', 'bv', 'Wo', 'bo')}
    del _L0_xattn_all

    def _L0_ffn_setup():
        import jax, jax.numpy as jnp
        import numpy as np
        R = 16
        LORA_ALPHA = 16
        SCALING = LORA_ALPHA / R
        key = jax.random.key(seed)
        kx, kr, ka = jax.random.split(key, 3)
        B, S, D, DO, E = (4, 256, 512, 512, 8)
        x = jax.random.normal(kx, (B, S, D), dtype=jnp.float32)
        bound_r = 1.0 / np.sqrt(D)
        route_w = jax.random.uniform(kr, (E, D), jnp.float32, -bound_r, bound_r)
        bound_a = 1.0 / np.sqrt(D)
        A = jax.random.uniform(ka, (E, R, D), jnp.float32, -bound_a, bound_a)
        kb = jax.random.fold_in(key, 7)
        Bw = jax.random.normal(kb, (E, DO, R), dtype=jnp.float32) * 0.02
        return {'x': x, 'route_w': route_w, 'A': A, 'Bw': Bw}
    _L0_ffn_all = _L0_ffn_setup()
    _L0_ffn_in = {k: v for k, v in _L0_ffn_all.items() if k in ('route_w', 'A', 'Bw')}
    del _L0_ffn_all

    def _L1_xattn_setup():
        import jax, jax.numpy as jnp
        import numpy as np
        B, Q, D = (8, 64, 512)
        CTX = 512
        H, KV, HD = (16, 4, 96)
        G = H // KV
        key = jax.random.key(seed)
        ks = jax.random.split(key, 6)
        s = 0.02
        return {'latents': jax.random.normal(ks[0], (B, Q, D), jnp.float32), 'context': jax.random.normal(ks[1], (B, CTX, D), jnp.float32), 'Wq': jax.random.normal(ks[2], (H * HD, D), jnp.float32) * s, 'Wk': jax.random.normal(ks[3], (KV * HD, D), jnp.float32) * s, 'Wv': jax.random.normal(ks[4], (KV * HD, D), jnp.float32) * s, 'Wo': jax.random.normal(ks[5], (D, H * HD), jnp.float32) * s}
    _L1_xattn_all = _L1_xattn_setup()
    _L1_xattn_in = {k: v for k, v in _L1_xattn_all.items() if k in ('Wq', 'Wk', 'Wv', 'Wo')}
    del _L1_xattn_all

    def _L1_ffn_setup():
        import jax, jax.numpy as jnp
        import numpy as np
        DIM = 512
        INTER = 128
        E = 16
        GROUPS = 4
        LIM = 2
        K = 2
        SHARED_INTER = 2 * INTER
        SCALE = 1.0
        key = jax.random.key(seed)
        ks = jax.random.split(key, 16)

        def n(k, shape, s=0.02):
            return jax.random.normal(k, shape, jnp.float32) * s
        return {'x': jax.random.normal(ks[0], (1, 256, DIM), jnp.float32), 'router_w': n(ks[1], (DIM, E)), 'router_b': n(ks[2], (E,)), 'router_bias': n(ks[3], (E,), 1.0), 'ew1': n(ks[4], (E, DIM, INTER)), 'eb1': n(ks[5], (E, INTER)), 'ew2': n(ks[6], (E, DIM, INTER)), 'eb2': n(ks[7], (E, INTER)), 'ew3': n(ks[8], (E, INTER, DIM)), 'eb3': n(ks[9], (E, DIM)), 'sw1': n(ks[10], (DIM, SHARED_INTER)), 'sb1': n(ks[11], (SHARED_INTER,)), 'sw2': n(ks[12], (DIM, SHARED_INTER)), 'sb2': n(ks[13], (SHARED_INTER,)), 'sw3': n(ks[14], (SHARED_INTER, DIM)), 'sb3': n(ks[15], (DIM,))}
    _L1_ffn_all = _L1_ffn_setup()
    _L1_ffn_in = {k: v for k, v in _L1_ffn_all.items() if k in ('router_w', 'router_b', 'router_bias', 'ew1', 'eb1', 'ew2', 'eb2', 'ew3', 'eb3', 'sw1', 'sb1', 'sw2', 'sb2', 'sw3', 'sb3')}
    del _L1_ffn_all
    return {'x': x, 'ctx_4096': ctx_4096, 'g_xattn': g_xattn, 'g_ffn': g_ffn, 'L0_xattn_Wq': _L0_xattn_in['Wq'], 'L0_xattn_bq': _L0_xattn_in['bq'], 'L0_xattn_Wk': _L0_xattn_in['Wk'], 'L0_xattn_bk': _L0_xattn_in['bk'], 'L0_xattn_Wv': _L0_xattn_in['Wv'], 'L0_xattn_bv': _L0_xattn_in['bv'], 'L0_xattn_Wo': _L0_xattn_in['Wo'], 'L0_xattn_bo': _L0_xattn_in['bo'], 'L0_ffn_route_w': _L0_ffn_in['route_w'], 'L0_ffn_A': _L0_ffn_in['A'], 'L0_ffn_Bw': _L0_ffn_in['Bw'], 'L1_xattn_Wq': _L1_xattn_in['Wq'], 'L1_xattn_Wk': _L1_xattn_in['Wk'], 'L1_xattn_Wv': _L1_xattn_in['Wv'], 'L1_xattn_Wo': _L1_xattn_in['Wo'], 'L1_ffn_router_w': _L1_ffn_in['router_w'], 'L1_ffn_router_b': _L1_ffn_in['router_b'], 'L1_ffn_router_bias': _L1_ffn_in['router_bias'], 'L1_ffn_ew1': _L1_ffn_in['ew1'], 'L1_ffn_eb1': _L1_ffn_in['eb1'], 'L1_ffn_ew2': _L1_ffn_in['ew2'], 'L1_ffn_eb2': _L1_ffn_in['eb2'], 'L1_ffn_ew3': _L1_ffn_in['ew3'], 'L1_ffn_eb3': _L1_ffn_in['eb3'], 'L1_ffn_sw1': _L1_ffn_in['sw1'], 'L1_ffn_sb1': _L1_ffn_in['sb1'], 'L1_ffn_sw2': _L1_ffn_in['sw2'], 'L1_ffn_sb2': _L1_ffn_in['sb2'], 'L1_ffn_sw3': _L1_ffn_in['sw3'], 'L1_ffn_sb3': _L1_ffn_in['sb3']}

def reference(x, ctx_4096, g_xattn, g_ffn, L0_xattn_Wq, L0_xattn_bq, L0_xattn_Wk, L0_xattn_bk, L0_xattn_Wv, L0_xattn_bv, L0_xattn_Wo, L0_xattn_bo, L0_ffn_route_w, L0_ffn_A, L0_ffn_Bw, L1_xattn_Wq, L1_xattn_Wk, L1_xattn_Wv, L1_xattn_Wo, L1_ffn_router_w, L1_ffn_router_b, L1_ffn_router_bias, L1_ffn_ew1, L1_ffn_eb1, L1_ffn_ew2, L1_ffn_eb2, L1_ffn_ew3, L1_ffn_eb3, L1_ffn_sw1, L1_ffn_sb1, L1_ffn_sw2, L1_ffn_sb2, L1_ffn_sw3, L1_ffn_sb3):
    import jax
    import jax.numpy as jnp

    def _L0_xattn_ref(x, cond, Wq, bq, Wk, bk, Wv, bv, Wo, bo):
        import jax, jax.numpy as jnp
        import numpy as np
        HEADS = 8
        WINDOW = 16

        def _pointwise(W, b, t):
            return jnp.einsum('oc,bct->bot', W, t) + b[None, :, None]
        B, C, T = x.shape
        H, W = (HEADS, WINDOW)
        hd = C // H
        scale = hd ** (-0.5)
        pad_left = W // 2
        pad_right = W - pad_left - 1
        q = _pointwise(Wq, bq, x)
        k = _pointwise(Wk, bk, cond)
        v = _pointwise(Wv, bv, cond)
        k = jnp.pad(k, ((0, 0), (0, 0), (pad_left, pad_right)))
        v = jnp.pad(v, ((0, 0), (0, 0), (pad_left, pad_right)))
        idx = jnp.arange(T)[:, None] + jnp.arange(W)[None, :]
        k_win = k[:, :, idx].reshape(B, H, hd, T, W)
        v_win = v[:, :, idx].reshape(B, H, hd, T, W)
        qh = q.reshape(B, H, hd, T)
        dots = jnp.einsum('bhdt,bhdtw->bhtw', qh, k_win) * scale
        attn = jax.nn.softmax(dots, axis=-1)
        out = jnp.einsum('bhtw,bhdtw->bhdt', attn, v_win)
        out = out.reshape(B, C, T)
        return _pointwise(Wo, bo, out)

    def _L0_ffn_ref(x, route_w, A, Bw):
        import jax, jax.numpy as jnp
        import numpy as np
        R = 16
        LORA_ALPHA = 16
        SCALING = LORA_ALPHA / R
        logits = jnp.einsum('bsd,ed->bse', x, route_w)
        topk_v, topk_idx = jax.lax.top_k(logits, 1)
        E = logits.shape[-1]
        route_weight = jax.nn.one_hot(topk_idx[..., 0], E, dtype=logits.dtype) * topk_v
        h = jnp.einsum('bsd,erd->bser', x, A)
        wh = route_weight[..., None] * h
        out = jnp.einsum('bser,eor->bso', wh, Bw) * SCALING
        return out

    def _L1_xattn_ref(latents, context, Wq, Wk, Wv, Wo):
        import jax, jax.numpy as jnp
        import numpy as np
        B, Q, D = (8, 64, 512)
        CTX = 512
        H, KV, HD = (16, 4, 96)
        G = H // KV
        b, q_len, _ = latents.shape
        hidden = jnp.concatenate([context, latents], axis=1)
        s_len = hidden.shape[1]
        q = (latents @ Wq.T).reshape(b, q_len, H, HD)
        k = (hidden @ Wk.T).reshape(b, s_len, KV, HD)
        v = (hidden @ Wv.T).reshape(b, s_len, KV, HD)
        q = q.transpose(0, 2, 1, 3).reshape(b, KV, G, q_len, HD)
        k = k.transpose(0, 2, 1, 3)
        v = v.transpose(0, 2, 1, 3)
        scale = 1.0 / jnp.sqrt(jnp.asarray(HD, q.dtype))
        scores = jnp.einsum('bkgqd,bksd->bkgqs', q, k) * scale
        attn = jax.nn.softmax(scores.astype(jnp.float32), axis=-1).astype(q.dtype)
        out = jnp.einsum('bkgqs,bksd->bkgqd', attn, v)
        out = out.reshape(b, H, q_len, HD).transpose(0, 2, 1, 3).reshape(b, q_len, H * HD)
        return out @ Wo.T

    def _L1_ffn_ref(x, router_w, router_b, router_bias, ew1, eb1, ew2, eb2, ew3, eb3, sw1, sb1, sw2, sb2, sw3, sb3):
        import jax, jax.numpy as jnp
        import numpy as np
        DIM = 512
        INTER = 128
        E = 16
        GROUPS = 4
        LIM = 2
        K = 2
        SHARED_INTER = 2 * INTER
        SCALE = 1.0
        shape = x.shape
        xt = x.reshape(-1, DIM)
        T = xt.shape[0]
        logits = xt @ router_w + router_b
        scores = jax.nn.softmax(logits.astype(jnp.float32), axis=-1) + router_bias
        g = scores.reshape(T, GROUPS, E // GROUPS)
        _, gidx = jax.lax.top_k(g.max(axis=-1), LIM)
        keep = jnp.zeros((T, GROUPS), bool).at[jnp.arange(T)[:, None], gidx].set(True)
        masked = jnp.where(keep[:, :, None], g, -jnp.inf).reshape(T, E)
        _, idx = jax.lax.top_k(masked, K)
        vals = (jnp.take_along_axis(scores, idx, axis=1) * SCALE).astype(x.dtype)
        gate = jnp.zeros((T, E), x.dtype).at[jnp.arange(T)[:, None], idx].add(vals)

        def step(y, p):
            w1, b1, w2, b2, w3, b3, ge = p
            h = jax.nn.silu(xt @ w1 + b1) * (xt @ w2 + b2)
            return (y + ge[:, None] * (h @ w3 + b3), None)
        y, _ = jax.lax.scan(step, jnp.zeros_like(xt), (ew1, eb1, ew2, eb2, ew3, eb3, gate.T))
        z = jax.nn.silu(xt @ sw1 + sb1) * (xt @ sw2 + sb2) @ sw3 + sb3
        return (y + z).reshape(shape)
    x = x + jnp.tanh(g_xattn[0]) * _L0_xattn_ref(_layernorm(x, axis=-1), ctx_4096, L0_xattn_Wq, L0_xattn_bq, L0_xattn_Wk, L0_xattn_bk, L0_xattn_Wv, L0_xattn_bv, L0_xattn_Wo, L0_xattn_bo)
    x = x + jnp.tanh(g_ffn[0]) * _L0_ffn_ref(_layernorm(x, axis=-1), L0_ffn_route_w, L0_ffn_A, L0_ffn_Bw)
    x = x + jnp.tanh(g_xattn[1]) * _L1_xattn_ref(_layernorm(x, axis=-1), ctx_4096, L1_xattn_Wq, L1_xattn_Wk, L1_xattn_Wv, L1_xattn_Wo)
    x = x + jnp.tanh(g_ffn[1]) * _L1_ffn_ref(_layernorm(x, axis=-1), L1_ffn_router_w, L1_ffn_router_b, L1_ffn_router_bias, L1_ffn_ew1, L1_ffn_eb1, L1_ffn_ew2, L1_ffn_eb2, L1_ffn_ew3, L1_ffn_eb3, L1_ffn_sw1, L1_ffn_sb1, L1_ffn_sw2, L1_ffn_sb2, L1_ffn_sw3, L1_ffn_sb3)
    return x

_drawn_inputs = setup_inputs


def setup_inputs(seed=0):
    import zlib

    import numpy as np

    out = dict(_drawn_inputs(seed))
    spreads = {'g_ffn': (-1.0, 0.6),
     'L0_xattn_bq': (0.0, 0.8),
     'L0_xattn_bk': (0.0, 2.0),
     'L0_xattn_bv': (0.0, 0.703),
     'L0_xattn_bo': (0.0, 0.1)}
    factors = {'L0_xattn_Wq': 8.0,
     'L0_xattn_Wk': 8.0,
     'L0_xattn_Wv': 8.0,
     'L0_xattn_Wo': 3.884,
     'L1_xattn_Wq': 5.824,
     'L1_xattn_Wk': 5.817,
     'L1_ffn_router_w': 8.0,
     'L1_ffn_router_b': 64.0,
     'L1_ffn_eb1': 8.0,
     'L1_ffn_eb2': 8.0,
     'L1_ffn_sb1': 42.687,
     'L1_ffn_sb2': 41.432,
     'L1_ffn_sb3': 3.486}
    for name, (base, spread) in spreads.items():
        noise = np.random.default_rng([zlib.crc32(name.encode()), seed]).standard_normal(out[name].shape)
        drawn = base * np.exp(spread * noise) if base else spread * noise
        out[name] = jnp.asarray(drawn.astype(out[name].dtype))
    for name, factor in factors.items():
        out[name] = (out[name] * factor).astype(out[name].dtype)
    return out
```

```python
from contextlib import ExitStack

import concourse.bass as bass
from concourse import mybir

F32 = mybir.dt.float32
ALU = mybir.AluOpType
ACT = mybir.ActivationFunctionType
AX_X = mybir.AxisListType.X

P = 128
BATCH, TOK, DIM = 32, 64, 512
TILES = BATCH * TOK // P
CH = DIM // P
EPS = 1e-5

HEADS, HD, WINDOW = 8, TOK // 8, 16
LEFT = WINDOW // 2
GROUPS = 2
PAIRS = TILES // GROUPS
TPAD = DIM + WINDOW
UNIT = 8

LORA_E, RANK = 8, 16

QH, KV, HD1 = 16, 4, 96
G = QH // KV
OCTETS = 4
OB = BATCH // OCTETS
OT_TILES = TILES // OCTETS

E1, INTER = 16, 128
SHARED = 2
EXPERTS = E1 + SHARED
EGROUPS = 4
W3 = CH * 2 * INTER
B1, B2, W_COLS = W3 + DIM, W3 + DIM + 1, W3 + DIM + 2


class Own:

    def __init__(self, engine, semaphore):
        self.engine, self.semaphore = engine, semaphore
        self.base, self.n = 0, 0

    def mark(self, instruction):
        instruction.then_inc(self.semaphore, 1)
        self.n += 1

    def wait(self):
        self.engine.wait_ge(self.semaphore, self.base + self.n)

    def done(self, instruction):
        self.mark(instruction)
        self.wait()

    def enter(self, i, each):
        self.start, self.each = self.base + self.n, each
        self.base, self.n = i * each + self.start, 0

    def leave(self, rounds):
        assert self.n == self.each, (self.n, self.each)
        self.base, self.n = self.start + rounds * self.each, 0


def norm_stats(nc, dve, own, X, bn, mv, rstd, var_ready, std_ready, std_count):
    for t in range(TILES):
        own.mark(nc.vector.bn_stats(bn[:, t, :], X[:, t, :]))
    own.wait()
    for t in range(TILES):
        own.mark(nc.vector.bn_aggr(mv[:, t, :], bn[:, t, :]))
    own.wait()
    nc.vector.tensor_scalar_add(rstd[:, :], mv[:, :, 1], EPS).then_inc(var_ready, 1)
    dve.wait_ge(std_ready, std_count)
    own.done(nc.vector.reciprocal(rstd[:, :], rstd[:, :]))


def normalise(nc, out, X, t, mv, rstd):
    return nc.vector.tensor_scalar(out, X[:, t, :], mv[:, t, 0:1], rstd[:, t:t + 1], ALU.subtract, ALU.mult)


def window_attention(nc, X, x, ctx, w_qkvo, b_qkvo, gates, ident_in, tg, ident, bn, mv, rstd):
    stack = ExitStack()
    with stack:
        def sb(name, shape):
            return stack.enter_context(nc.sbuf_tensor(name, shape, F32))

        def sem(name):
            return stack.enter_context(nc.semaphore(name))

        w_sb = sb("w0", [P, 4, P])
        b_sb = sb("b0", [P, 4])
        xn = sb("xn0", [P, 2, DIM])
        cond = sb("cond", [P, 2, DIM])
        stage = sb("stage", [P, 2, 3, DIM])
        q_h = sb("q_h", [P, HD, DIM])
        k_h = sb("k_h", [P, HD, TPAD])
        v_h = sb("v_h", [P, HD, TPAD])
        dots = sb("dots", [P, WINDOW, DIM])
        prod = sb("prod", [P, UNIT, DIM])
        gprod = sb("gprod", [P, 2, UNIT, DIM])
        peak = sb("peak", [P, DIM])
        total = sb("total", [P, DIM])
        o_h = q_h
        back = sb("back", [P, 2, DIM])
        proj = sb("proj", [P, 2, DIM])
        qkv_ps = [[stack.enter_context(nc.psum_tensor(f"qkv_ps{s}{k}", [P, DIM], F32)) for k in range(3)]
                  for s in range(2)]
        sum_ps = [stack.enter_context(nc.psum_tensor(f"sum_ps{s}", [P, DIM], F32)) for s in range(2)]

        w_in, x_in, cond_in = sem("w_in"), sem("x_in"), [sem("cond_in0"), sem("cond_in1")]
        pads, tanh_done = sem("pads"), sem("tanh_done")
        var_ready, std_ready, dve_own, act_own = sem("var0"), sem("std0"), sem("own0"), sem("act_own0")
        xn_ready, qkv_done, staged = sem("xn_ready"), sem("qkv_done"), sem("staged")
        rows_out, heads_in, outputs_out = [sem("rows_out0"), sem("rows_out1")], sem("heads_in"), sem("outputs_out")
        multiplied, consumed = sem("multiplied"), sem("consumed")
        copied = sem("copied")
        shifted, exp_done, outputs = sem("shifted"), sem("exp_done"), sem("outputs")
        back_in, wo_done = [sem("back_in0"), sem("back_in1")], sem("wo_done")
        proj_ready, added = sem("proj_ready"), sem("added")
        block = stack.enter_context(nc.Block())

        by_row = nc.dram_tensor("by_row", (4, TILES, P, DIM), F32, kind="Internal").ap()

        def by_head(k, g):
            return by_row[k, g * PAIRS:(g + 1) * PAIRS].rearrange("j (r f) n -> (j r) f n", f=HD)

        def window(row, half):
            a = v_h[:, row, half * 256:half * 256 + 256]
            return bass.AP(a.tensor, a.offset, [list(a.ap[0]), [1, WINDOW], [1, 256]])

        @block.sync
        def _(sp):
            sp.dma_start(w_sb[:], w_qkvo).then_inc(w_in, 16)
            sp.dma_start(b_sb[:], b_qkvo).then_inc(w_in, 16)
            sp.dma_start(tg[:], gates).then_inc(w_in, 16)
            sp.dma_start(ident[:], ident_in).then_inc(w_in, 16)
            for part in range(4):
                sp.dma_start(X[:, 4 * part:4 * part + 4, :],
                             x[4 * part:4 * part + 4].rearrange("t p d -> p t d")).then_inc(x_in, 16)
            for g in range(GROUPS):
                for j in range(PAIRS):
                    n, s = g * PAIRS + j, j % 2
                    if n >= 2:
                        sp.wait_ge(qkv_done, 3 * (n - 1))
                    sp.dma_start(cond[:, s, :], ctx[n]).then_inc(cond_in[s], 16)
                if g == 0:
                    sp.wait_ge(pads, 2)
                for s in range(2):
                    sp.wait_ge(rows_out[s], 16 * (PAIRS // 2) * (g + 1))
                if g > 0:
                    sp.wait_ge(outputs_out, 16 * g)
                for k, dst in enumerate((q_h[:, :, :], k_h[:, :, LEFT:LEFT + DIM], v_h[:, :, LEFT:LEFT + DIM])):
                    sp.dma_start(dst, by_head(k, g)).then_inc(heads_in, 16)
                sp.wait_ge(outputs, g + 1)
                sp.dma_start(by_head(3, g), o_h[:, :, :]).then_inc(outputs_out, 16)
                sp.wait_ge(outputs_out, 16 * (g + 1))
                for j in range(PAIRS):
                    n, s = g * PAIRS + j, j % 2
                    if n >= 2:
                        sp.wait_ge(wo_done, n - 1)
                    sp.dma_start(back[:, s, :], by_row[3, n]).then_inc(back_in[s], 16)

        @block.gpsimd
        def _(pool):
            nc.gpsimd.memset(k_h[:, :, :], 0.0).then_inc(pads, 1)
            nc.gpsimd.memset(v_h[:, :, :], 0.0).then_inc(pads, 1)
            for g in range(GROUPS):
                pool.wait_ge(heads_in, 48 * (g + 1))
                with pool.Fori(0, WINDOW // 4) as i:
                    for s in range(2):
                        pool.wait_ge(consumed, 2 * i + (s + 16 * g + 1))
                        nc.gpsimd.tensor_tensor(gprod[:, s], q_h[:, :, :],
                                                k_h[:, :, bass.ds(4 * i + (2 * s + 1), DIM)],
                                                ALU.mult).then_inc(multiplied, 1)
                pool.wait_ge(exp_done, g + 1)
                for i in range(HD // 2):
                    for s in range(2):
                        pool.wait_ge(consumed, 2 * i + s + 16 * g + 9)
                        a = v_h[:, 2 * i + 1, 8 * s:8 * s + DIM]
                        shifted_v = bass.AP(a.tensor, a.offset, [list(a.ap[0]), [1, UNIT], [1, DIM]])
                        nc.gpsimd.tensor_tensor(gprod[:, s], dots[:, 8 * s:8 * s + 8, :], shifted_v,
                                                ALU.mult).then_inc(multiplied, 1)

        @block.scalar
        def _(act):
            act.sem_inc(copied, 2)
            act.wait_ge(w_in, 64)
            nc.scalar.activation(tg[:, :], tg[:, :], ACT.Tanh).then_inc(tanh_done, 1)
            act.wait_ge(var_ready, 1)
            nc.scalar.activation(rstd[:, :], rstd[:, :], ACT.Sqrt).then_inc(std_ready, 1)
            for g in range(GROUPS):
                for j in range(PAIRS):
                    n, s = g * PAIRS + j, j % 2
                    if n >= 2:
                        act.wait_ge(rows_out[s], 16 * (n // 2))
                    for k in range(3):
                        act.wait_ge(qkv_done, 3 * n + k + 1)
                        nc.scalar.activation(stage[:, s, k, :], qkv_ps[s][k][:, :], ACT.Identity,
                                             bias=b_sb[:, k:k + 1]).then_inc(staged, 1)
                    act.wait_ge(staged, 3 * n + 3)
                    act.dma_start(by_row[0:3, n].rearrange("k p d -> p k d"), stage[:, s]).then_inc(rows_out[s], 16)
                with act.Fori(0, WINDOW // 4) as i:
                    for s in range(2):
                        act.wait_ge(consumed, 2 * i + (s + 16 * g + 3))
                        nc.scalar.copy(dots[:, 4 * i + (2 * s + 1), :], sum_ps[s][:, :]).then_inc(copied, 1)
                act.wait_ge(shifted, g + 1)
                nc.scalar.activation(dots[:, :, :], dots[:, :, :], ACT.Exp, scale=HD ** -0.5).then_inc(exp_done, 1)
                for i in range(HD // 2):
                    act.wait_ge(consumed, 16 * g + 12 + 2 * i)
                    nc.scalar.copy(o_h[:, 2 * i + 1, :], sum_ps[i % 2][:, :]).then_inc(copied, 1)
                for j in range(PAIRS):
                    n, s = g * PAIRS + j, j % 2
                    act.wait_ge(wo_done, n + 1)
                    if n >= 2:
                        act.wait_ge(added, n - 1)
                    nc.scalar.activation(proj[:, s, :], qkv_ps[s][0][:, :], ACT.Identity,
                                         bias=b_sb[:, 3:4]).then_inc(proj_ready, 1)

        @block.tensor
        def _(pe):
            pe.sem_inc(consumed, 2)
            pe.wait_ge(w_in, 64)
            for g in range(GROUPS):
                if g > 0:
                    pe.wait_ge(proj_ready, PAIRS * g)
                for j in range(PAIRS):
                    n, s = g * PAIRS + j, j % 2
                    if j >= 2:
                        pe.wait_ge(staged, 3 * (n - 1))
                    pe.wait_ge(xn_ready, n + 1)
                    pe.wait_ge(cond_in[s], 16 * (n // 2 + 1))
                    for k, rhs in enumerate((xn[:, s, :], cond[:, s, :], cond[:, s, :])):
                        nc.tensor.matmul(qkv_ps[s][k][:, :], w_sb[:, k, :], rhs, start=True, stop=True)\
                          .then_inc(qkv_done, 1)
                with pe.Fori(0, WINDOW // 4) as i:
                    for s in range(2):
                        pe.wait_ge(multiplied, 2 * i + (s + 16 * g + 1))
                        pe.wait_ge(copied, 2 * i + (s + 12 * g + 1))
                        for r in range(UNIT):
                            last = nc.tensor.matmul(sum_ps[s][:, :], ident[:, :], gprod[:, s, r, :],
                                                    start=(r == 0), stop=(r == UNIT - 1))
                        last.then_inc(consumed, 1)
                for i in range(HD // 2):
                    pe.wait_ge(copied, 12 * g + 9 + i)
                    for s in range(2):
                        pe.wait_ge(multiplied, 16 * g + 9 + 2 * i + s)
                        for r in range(UNIT):
                            last = nc.tensor.matmul(sum_ps[i % 2][:, :], ident[:, :], gprod[:, s, r, :],
                                                    start=(s == 0 and r == 0), stop=(s == 1 and r == UNIT - 1))
                        last.then_inc(consumed, 1)
                for j in range(PAIRS):
                    n, s = g * PAIRS + j, j % 2
                    if j >= 2:
                        pe.wait_ge(proj_ready, n - 1)
                    pe.wait_ge(back_in[s], 16 * (n // 2 + 1))
                    nc.tensor.matmul(qkv_ps[s][0][:, :], w_sb[:, 3, :], back[:, s, :], start=True, stop=True)\
                      .then_inc(wo_done, 1)

        @block.vector
        def _(dve):
            own = Own(dve, dve_own)
            dve.wait_ge(x_in, 64)
            norm_stats(nc, dve, own, X, bn, mv, rstd, var_ready, std_ready, 1)
            dve.wait_ge(tanh_done, 1)
            for g in range(GROUPS):
                for j in range(PAIRS):
                    n, s = g * PAIRS + j, j % 2
                    if n >= 2:
                        dve.wait_ge(qkv_done, 3 * (n - 2) + 1)
                    normalise(nc, xn[:, s, :], X, n, mv, rstd).then_inc(xn_ready, 1)
                dve.wait_ge(heads_in, 48 * (g + 1))
                with dve.Fori(0, WINDOW // 2) as i:
                    own.enter(i, 2)
                    own.done(nc.vector.tensor_tensor(prod[:], q_h[:, :, :], k_h[:, :, bass.ds(2 * i, DIM)], ALU.mult))
                    own.done(nc.vector.tensor_reduce(dots[:, 2 * i, :], prod[:].rearrange("p d t -> p t d"),
                                                     AX_X, ALU.add))
                    own.leave(WINDOW // 2)
                dve.wait_ge(copied, 12 * g + 10)
                own.done(nc.vector.tensor_reduce(peak[:, :], dots[:].rearrange("p w t -> p t w"), AX_X, ALU.max))
                nc.vector.tensor_tensor(dots[:], dots[:], peak[:].unsqueeze(1).to_broadcast([P, WINDOW, DIM]),
                                        ALU.subtract).then_inc(shifted, 1)
                dve.wait_ge(exp_done, g + 1)
                own.done(nc.vector.tensor_reduce(total[:, :], dots[:].rearrange("p w t -> p t w"), AX_X, ALU.add))
                own.done(nc.vector.reciprocal(total[:, :], total[:, :]))
                for d in range(0, HD, 2):
                    for half in range(2):
                        t = slice(256 * half, 256 * half + 256)
                        halved = prod[:].rearrange("p a b -> p (a b)").rearrange("p (w t) -> p w t", w=WINDOW)
                        own.done(nc.vector.tensor_tensor(halved, dots[:, :, t], window(d, half), ALU.mult))
                        own.done(nc.vector.tensor_reduce(o_h[:, d, t], halved.rearrange("p w t -> p t w"),
                                                         AX_X, ALU.add))
                dve.wait_ge(copied, 12 * g + 14)
                nc.vector.tensor_tensor(o_h[:, :, :], o_h[:, :, :], total[:].unsqueeze(1).to_broadcast([P, HD, DIM]),
                                        ALU.mult).then_inc(outputs, 1)
                for j in range(PAIRS):
                    n, s = g * PAIRS + j, j % 2
                    dve.wait_ge(proj_ready, n + 1)
                    nc.vector.scalar_tensor_tensor(X[:, n, :], proj[:, s, :], tg[:, 0:1], X[:, n, :],
                                                   ALU.mult, ALU.add).then_inc(added, 1)


def top1_lora(nc, X, route_a, bw, desc_in, tg, ident, bn, mv, rstd):
    W = LORA_E + LORA_E * RANK
    stack = ExitStack()
    with stack:
        def sb(name, shape):
            return stack.enter_context(nc.sbuf_tensor(name, shape, F32))

        def sem(name):
            return stack.enter_context(nc.semaphore(name))

        def banks(name):
            return [stack.enter_context(nc.psum_tensor(f"{name}{s}", [P, DIM], F32)) for s in range(2)]

        ra_sb = sb("ra_sb", [P, CH, W])
        bw_sb = sb("bw_sb", [P, DIM])
        desc = sb("desc8", [P, LORA_E])
        xn = sb("xn1", [P, 2, DIM])
        xt = sb("xt1", [P, 2, CH, P])
        wh = sb("wh", [P, 2, P])
        wht = sb("wht", [P, 2, P])
        best, among, first, weight = (sb(n, s) for n, s in (("best", [P, 1]), ("among", [P, LORA_E]),
                                                            ("first", [P, 1]), ("weight", [P, LORA_E])))
        t_ps, h_ps, w_ps, o_ps = banks("t_ps"), banks("h_ps"), banks("w_ps"), banks("o_ps")
        w_in, var_ready, std_ready, dve_own = sem("w1_in"), sem("var1"), sem("std1"), sem("own1")
        xn_ready, turned, xt_ready, h_done = sem("xn1_ready"), sem("turned"), sem("xt_ready"), sem("h_done")
        wh_ready, wh_turned, wht_ready = sem("wh_ready"), sem("wh_turned"), sem("wht_ready")
        o_done, added = sem("o_done"), sem("added1")
        block = stack.enter_context(nc.Block())

        @block.sync
        def _(sp):
            sp.dma_start(ra_sb[:], route_a).then_inc(w_in, 16)
            sp.dma_start(bw_sb[:], bw).then_inc(w_in, 16)
            sp.dma_start(desc[:], desc_in).then_inc(w_in, 16)

        @block.scalar
        def _(act):
            act.wait_ge(var_ready, 1)
            nc.scalar.activation(rstd[:, :], rstd[:, :], ACT.Sqrt).then_inc(std_ready, 1)
            for n in range(TILES + 2):
                if n < TILES:
                    act.wait_ge(turned, n + 1)
                    if n >= 2:
                        act.wait_ge(h_done, n - 1)
                    nc.scalar.copy(xt[:, n % 2], t_ps[n % 2][:, :]).then_inc(xt_ready, 1)
                if n >= 2:
                    m = n - 2
                    act.wait_ge(wh_turned, m + 1)
                    if m >= 2:
                        act.wait_ge(o_done, m - 1)
                    nc.scalar.copy(wht[:, m % 2], w_ps[m % 2][:, 0:P]).then_inc(wht_ready, 1)

        @block.tensor
        def _(pe):
            pe.wait_ge(w_in, 48)
            for n in range(TILES + 3):
                s = n % 2
                if n < TILES:
                    pe.wait_ge(xn_ready, n + 1)
                    if n >= 2:
                        pe.wait_ge(xt_ready, n - 1)
                    for c in range(CH):
                        last = nc.tensor.transpose(t_ps[s][:, c * P:(c + 1) * P], xn[:, s, c * P:(c + 1) * P], ident[:, :])
                    last.then_inc(turned, 1)
                if 1 <= n <= TILES:
                    m = n - 1
                    pe.wait_ge(xt_ready, m + 1)
                    if m >= 2:
                        pe.wait_ge(wh_ready, m - 1)
                    for c in range(CH):
                        last = nc.tensor.matmul(h_ps[m % 2][:, 0:W], xt[:, m % 2, c, :], ra_sb[:, c, :],
                                                start=(c == 0), stop=(c == CH - 1))
                    last.then_inc(h_done, 1)
                if 2 <= n <= TILES + 1:
                    m = n - 2
                    pe.wait_ge(wh_ready, m + 1)
                    if m >= 2:
                        pe.wait_ge(wht_ready, m - 1)
                    nc.tensor.transpose(w_ps[m % 2][:, 0:P], wh[:, m % 2, :], ident[:, :]).then_inc(wh_turned, 1)
                if n >= 3:
                    m = n - 3
                    pe.wait_ge(wht_ready, m + 1)
                    if m >= 2:
                        pe.wait_ge(added, m - 1)
                    nc.tensor.matmul(o_ps[m % 2][:, :], wht[:, m % 2, :], bw_sb[:, :], start=True, stop=True)\
                      .then_inc(o_done, 1)

        @block.vector
        def _(dve):
            own = Own(dve, dve_own)
            norm_stats(nc, dve, own, X, bn, mv, rstd, var_ready, std_ready, 1)
            dve.wait_ge(w_in, 48)
            for n in range(TILES + 3):
                if n < TILES:
                    if n >= 2:
                        dve.wait_ge(turned, n - 1)
                    normalise(nc, xn[:, n % 2, :], X, n, mv, rstd).then_inc(xn_ready, 1)
                if 1 <= n <= TILES:
                    m = n - 1
                    logits = h_ps[m % 2][:, 0:LORA_E]
                    dve.wait_ge(h_done, m + 1)
                    own.done(nc.vector.tensor_reduce(best[:], logits, AX_X, ALU.max))
                    own.done(nc.vector.scalar_tensor_tensor(among[:], logits, best[:, 0:1], desc[:],
                                                            ALU.is_equal, ALU.mult))
                    own.done(nc.vector.tensor_reduce(first[:], among[:], AX_X, ALU.max))
                    own.done(nc.vector.tensor_scalar(weight[:], among[:], first[:, 0:1], best[:, 0:1],
                                                     ALU.is_equal, ALU.mult))
                    if m >= 2:
                        dve.wait_ge(wh_turned, m - 1)
                    nc.vector.tensor_tensor(wh[:, m % 2, :].rearrange("p (e r) -> p e r", e=LORA_E),
                                            h_ps[m % 2][:, LORA_E:W].rearrange("p (e r) -> p e r", e=LORA_E),
                                            weight[:].unsqueeze(2).to_broadcast([P, LORA_E, RANK]),
                                            ALU.mult).then_inc(wh_ready, 1)
                if n >= 3:
                    m = n - 3
                    dve.wait_ge(o_done, m + 1)
                    nc.vector.scalar_tensor_tensor(X[:, m, :], o_ps[m % 2][:, :], tg[:, 1:2], X[:, m, :],
                                                   ALU.mult, ALU.add).then_inc(added, 1)


def latent_attention(nc, X, ctx_t, wq, wk, wv, wo, tg, ident, bn, mv, rstd):
    stack = ExitStack()
    with stack:
        def sb(name, shape):
            return stack.enter_context(nc.sbuf_tensor(name, shape, F32))

        def sem(name):
            return stack.enter_context(nc.semaphore(name))

        def banks(name):
            return [stack.enter_context(nc.psum_tensor(f"{name}{s}", [P, DIM], F32)) for s in range(2)]

        wq_sb = sb("wq_sb", [P, CH, QH * HD1])
        wk_sb = sb("wk_sb", [P, CH, KV * HD1])
        wv_sb = sb("wv_sb", [P, CH, KV * HD1])
        wo_sb = sb("wo_sb", [HD1, QH, DIM])
        xn = sb("xn2", [P, 2, DIM])
        ht = sb("ht", [P, CH, OB, 2, TOK])
        kt = sb("kt", [HD1, KV, OB, 2 * TOK])
        v = sb("v", [P, OB, KV * HD1])
        qt = sb("qt", [HD1, 2, OB, G, TOK])
        ot = sb("ot", [HD1, 2, G, DIM])
        probs = sb("probs", [P, 2, 2, P])
        probs_t = sb("probs_t", [P, 2, 2 * P])
        npeak = sb("npeak", [P, 2, 2])
        total = sb("total2", [P, 2, 2])
        big_ps, s_ps, p_ps, o_ps = banks("big_ps"), banks("s_ps"), banks("p_ps"), banks("o2_ps")

        uses = [("T", k) for k in range(OT_TILES)] + [("K", k) for k in range(2 * KV)] + [("V", b) for b in range(OB)]
        uses += [("Q", 0, h) for h in range(G)]
        OUT_AT = {3: (0,), 5: (1,), 7: (2, 3)}
        for a in range(KV):
            for b in range(OB):
                if b % 2 == 0 and a + 1 < KV:
                    uses.append(("Q", a + 1, b // 2))
                if a > 0:
                    uses += [("Y", a - 1, k) for k in OUT_AT.get(b, ())]
        uses += [("Y", KV - 1, k) for k in range(OT_TILES)]
        at = {use: n for n, use in enumerate(uses)}
        USES, UNITS = len(uses), KV * OB

        w_in, ctx_in = sem("w2_in"), sem("ctx_in")
        var_ready, std_ready, dve_own = sem("var2"), sem("std2"), sem("own2")
        xn_ready = sem("xn2_ready")
        big_done = sem("big_done")
        big_free = [sem("big_free0"), sem("big_free1")]
        ht_ready, kt_ready, v_ready, q_ready = sem("ht_ready"), sem("kt_ready"), sem("v_ready"), sem("q_ready")
        scored, peaked, exp_done, normed = sem("scored"), sem("peaked"), sem("exp2_done"), sem("normed")
        p_turned, pt_ready, pv_done, o_ready, added = sem("p_turned"), sem("pt_ready"), sem("pv2_done"), sem("o_ready"), sem("added2")
        block = stack.enter_context(nc.Block())

        @block.sync
        def _(sp):
            for dst, src in ((wk_sb, wk), (wv_sb, wv), (wq_sb, wq), (wo_sb, wo)):
                sp.dma_start(dst[:], src).then_inc(w_in, 16)
            with sp.Fori(0, OCTETS) as o:
                sp.wait_ge(big_done, o * USES + 1)
                for c in range(CH):
                    sp.dma_start(ht[:, c, :, 0, :], ctx_t[bass.ds(o, 1), :, c].rearrange("o p (b t) -> (o p) b t", b=OB))\
                      .then_inc(ctx_in, 16)

        @block.scalar
        def _(act):
            act.wait_ge(var_ready, 1)
            nc.scalar.activation(rstd[:, :], rstd[:, :], ACT.Sqrt).then_inc(std_ready, 1)

            def big(o, use):
                n = at[use]
                act.wait_ge(big_done, o * USES + n + 1)
                return big_ps[n % 2], big_free[n % 2]

            with act.Fori(0, OCTETS) as o:
                for k in range(OT_TILES):
                    ps, free = big(o, ("T", k))
                    nc.scalar.copy(ht[:, :, 2 * k:2 * k + 2, 1, :], ps[:, :].rearrange("p (c b t) -> p c b t", c=CH, b=2)).then_inc(free, 1)
                for k in range(2 * KV):
                    ps, free = big(o, ("K", k))
                    nc.scalar.copy(kt[:, k // 2, k % 2 * 4:k % 2 * 4 + 4, :], ps[0:HD1, :]).then_inc(free, 1)
                for h in range(G):
                    ps, free = big(o, ("Q", 0, h))
                    nc.scalar.activation(qt[:, 0, :, h, :], ps[0:HD1, :], ACT.Copy, scale=HD1 ** -0.5).then_inc(free, 1)
                for u in range(UNITS + 2):
                    a, b = u // OB, u % OB
                    if u < UNITS:
                        if b % 2 == 0 and a + 1 < KV:
                            ps, free = big(o, ("Q", a + 1, b // 2))
                            nc.scalar.activation(qt[:, (a + 1) % 2, :, b // 2, :], ps[0:HD1, :], ACT.Copy,
                                                 scale=HD1 ** -0.5).then_inc(free, 1)
                        act.wait_ge(peaked, o * UNITS + u + 1)
                        if u >= 2:
                            act.wait_ge(p_turned, o * UNITS + u - 1)
                        for g2 in range(2):
                            nc.scalar.activation(probs[:, u % 2, g2, :], s_ps[u % 2][:, g2 * P:(g2 + 1) * P], ACT.Exp,
                                                 bias=npeak[:, u % 2, g2:g2 + 1],
                                                 accum_out=total[:, u % 2, g2:g2 + 1]).then_inc(exp_done, 1)
                    if u >= 2:
                        w = u - 2
                        act.wait_ge(p_turned, o * UNITS + w + 1)
                        if w >= 2:
                            act.wait_ge(pv_done, o * UNITS + w - 1)
                        nc.scalar.copy(probs_t[:, w % 2, :], p_ps[w % 2][:, 0:2 * P]).then_inc(pt_ready, 1)

        @block.tensor
        def _(pe):
            pe.sem_inc(big_free[0], 1)
            pe.sem_inc(big_free[1], 1)
            pe.wait_ge(w_in, 64)

            def big(o, use):
                n = at[use]
                pe.wait_ge(big_free[n % 2], o * (USES // 2) + (n // 2 + 1))
                return big_ps[n % 2]

            def queries(o, a, h):
                ps = big(o, ("Q", a, h))
                head = a * G + h
                for c in range(CH):
                    last = nc.tensor.matmul(ps[0:HD1, :], wq_sb[:, c, head * HD1:(head + 1) * HD1], ht[:, c, :, 1, :],
                                            start=(c == 0), stop=(c == CH - 1))
                last.then_inc(big_done, 1)

            def project(o, a, k):
                if k == 0:
                    pe.wait_ge(o_ready, o * UNITS + OB * (a + 1))
                ps = big(o, ("Y", a, k))
                for h in range(G):
                    last = nc.tensor.matmul(ps[:, :], ot[:, a % 2, h, k * P:(k + 1) * P], wo_sb[:, a * G + h, :],
                                            start=(h == 0), stop=(h == G - 1))
                last.then_inc(big_done, 1)

            with pe.Fori(0, OCTETS) as o:
                for k in range(OT_TILES):
                    pe.wait_ge(xn_ready, o * OT_TILES + k + 1)
                    ps = big(o, ("T", k))
                    for c in range(CH):
                        last = nc.tensor.transpose(ps[:, c * P:(c + 1) * P], xn[:, k % 2, c * P:(c + 1) * P], ident[:, :])
                    last.then_inc(big_done, 1)
                pe.wait_ge(ctx_in, o * (16 * CH) + 16 * CH)
                for k in range(2 * KV):
                    ps = big(o, ("K", k))
                    if k == 0:
                        pe.wait_ge(big_free[1], o * (USES // 2) + 3)
                    for c in range(CH):
                        last = nc.tensor.matmul(ps[0:HD1, :], wk_sb[:, c, k // 2 * HD1:(k // 2 + 1) * HD1],
                                                ht[:, c, k % 2 * 4:k % 2 * 4 + 4], start=(c == 0), stop=(c == CH - 1))
                    last.then_inc(big_done, 1)
                for b in range(OB):
                    ps = big(o, ("V", b))
                    for c in range(CH):
                        last = nc.tensor.matmul(ps[:, 0:KV * HD1], ht[:, c, b], wv_sb[:, c, :],
                                                start=(c == 0), stop=(c == CH - 1))
                    last.then_inc(big_done, 1)
                for h in range(G):
                    queries(o, 0, h)
                for u in range(UNITS + 3):
                    a, b = u // OB, u % OB
                    if u < UNITS:
                        if b == 0:
                            first = at[("Q", a, G - 2)], at[("Q", a, G - 1)]
                            for n in first:
                                pe.wait_ge(big_free[n % 2], o * (USES // 2) + n // 2 + 2)
                        if u >= 2:
                            pe.wait_ge(exp_done, o * (2 * UNITS) + 2 * (u - 1))
                        for g2 in range(2):
                            last = nc.tensor.matmul(s_ps[u % 2][:, g2 * P:(g2 + 1) * P],
                                                    qt[:, a % 2, b, 2 * g2:2 * g2 + 2],
                                                    kt[:, a, b], start=True, stop=True)
                        last.then_inc(scored, 1)
                        if b % 2 == 0 and a + 1 < KV:
                            queries(o, a + 1, b // 2)
                    if u >= 2 and u - 2 < UNITS:
                        w = u - 2
                        pe.wait_ge(normed, o * UNITS + w + 1)
                        if w >= 2:
                            pe.wait_ge(pt_ready, o * UNITS + w - 1)
                        for g2 in range(2):
                            last = nc.tensor.transpose(p_ps[w % 2][:, g2 * P:(g2 + 1) * P], probs[:, w % 2, g2, :], ident[:, :])
                        last.then_inc(p_turned, 1)
                    if u >= 3:
                        w = u - 3
                        pe.wait_ge(pt_ready, o * UNITS + w + 1)
                        if w >= 2:
                            pe.wait_ge(o_ready, o * UNITS + w - 1)
                        nc.tensor.matmul(o_ps[w % 2][0:HD1, 0:2 * P], v[:, w % OB, w // OB * HD1:(w // OB + 1) * HD1],
                                         probs_t[:, w % 2, :], start=True, stop=True).then_inc(pv_done, 1)
                    if OB < u < UNITS:
                        for k in OUT_AT.get(b, ()):
                            project(o, a - 1, k)
                for k in range(OT_TILES):
                    project(o, KV - 1, k)

        @block.vector
        def _(dve):
            own = Own(dve, dve_own)
            norm_stats(nc, dve, own, X, bn, mv, rstd, var_ready, std_ready, 1)

            def big(o, use):
                n = at[use]
                dve.wait_ge(big_done, o * USES + n + 1)
                return big_ps[n % 2], big_free[n % 2]

            def add(o, a, k):
                ps, free = big(o, ("Y", a, k))
                row = X[:, bass.ds(o * OT_TILES + k, 1), :].rearrange("p o d -> p (o d)")
                nc.vector.scalar_tensor_tensor(row, ps[:, :], tg[:, 2:3], row, ALU.mult, ALU.add).then_inc(free, 1)

            with dve.Fori(0, OCTETS) as o:
                own.enter(o, UNITS)
                for k in range(OT_TILES):
                    if k >= 2:
                        dve.wait_ge(big_done, o * USES + k - 1)
                    t = o * OT_TILES + k
                    nc.vector.tensor_scalar(xn[:, k % 2, :], X[:, bass.ds(t, 1), :].rearrange("p o d -> p (o d)"),
                                            mv[:, bass.ds(t, 1), 0:1].rearrange("p o d -> p (o d)"),
                                            rstd[:, bass.ds(t, 1)], ALU.subtract, ALU.mult).then_inc(xn_ready, 1)
                for b in range(OB):
                    ps, free = big(o, ("V", b))
                    nc.vector.tensor_copy(v[:, b, :], ps[:, 0:KV * HD1]).then_inc(free, 1)
                for u in range(UNITS + 3):
                    if u < UNITS:
                        dve.wait_ge(scored, o * UNITS + u + 1)
                        nc.vector.tensor_reduce(npeak[:, u % 2, :], s_ps[u % 2][:, 0:2 * P].rearrange("p (g s) -> p g s", g=2),
                                                AX_X, ALU.max, negate=True).then_inc(peaked, 1)
                    if 1 <= u <= UNITS:
                        w = u - 1
                        dve.wait_ge(exp_done, o * (2 * UNITS) + 2 * (w + 1))
                        own.done(nc.vector.reciprocal(total[:, w % 2, :], total[:, w % 2, :]))
                        nc.vector.tensor_tensor(probs[:, w % 2], probs[:, w % 2],
                                                total[:, w % 2, :].unsqueeze(2).to_broadcast([P, 2, P]),
                                                ALU.mult).then_inc(normed, 1)
                    if u >= 3:
                        w = u - 3
                        a, b = w // OB, w % OB
                        dve.wait_ge(pv_done, o * UNITS + w + 1)
                        if b == 0 and a >= 2:
                            dve.wait_ge(big_done, o * USES + at[("Y", a - 2, G - 1)] + 1)
                        nc.vector.tensor_copy(ot[:, a % 2, :, b * TOK:(b + 1) * TOK],
                                              o_ps[w % 2][0:HD1, 0:2 * P].rearrange("p (g q) -> p g q", g=G)).then_inc(o_ready, 1)
                    if OB < u < UNITS:
                        for k in OUT_AT.get(u % OB, ()):
                            add(o, u // OB - 1, k)
                for k in range(OT_TILES):
                    add(o, KV - 1, k)
                own.leave(OCTETS)


def route(nc, X, xt, gates, gs, gt, rw, rows, tg, ident, bn, mv, rstd):
    stack = ExitStack()
    with stack:
        def sb(name, shape):
            return stack.enter_context(nc.sbuf_tensor(name, shape, F32))

        def sem(name):
            return stack.enter_context(nc.semaphore(name))

        def banks(name):
            return [stack.enter_context(nc.psum_tensor(f"{name}{s}", [P, DIM], F32)) for s in range(2)]

        T, E, GS = TILES, E1, E1 // EGROUPS
        rw_sb = sb("rw_sb", [P, CH, E])
        rows_sb = sb("rows_sb", [P, 3 * E + EGROUPS])
        xn = sb("xn3", [P, 2, DIM])
        slot = sb("slot", [P, 2, CH, P])
        scores, work, among, picked, left = (sb(n, [P, T, E]) for n in ("scores", "work", "among3", "picked", "left"))
        top, gtop, gwork, gamong, keep = sb("top3", [P, T]), sb("gtop", [P, T, EGROUPS]), sb("gwork", [P, T, EGROUPS]), \
            sb("gamong", [P, T, EGROUPS]), sb("keep", [P, T, EGROUPS])
        t_ps, l_ps, g_ps = banks("t3_ps"), banks("l_ps"), banks("g_ps")
        w_in, var_ready, std_ready, dve_own = sem("w3_in"), sem("var3"), sem("std3"), sem("own3")
        xn_ready, turned, slot_ready, xt_ready = sem("xn3_ready"), sem("turned3"), sem("slot_ready"), sem("xt3_ready")
        logits_done, logits_out, shifted, exp_done = sem("logits_done"), sem("logits_out"), sem("shifted3"), sem("exp3")
        gates_ready, gates_turned, gt_ready = sem("gates_ready"), sem("gates_turned"), sem("gt_ready")
        block = stack.enter_context(nc.Block())

        @block.sync
        def _(sp):
            sp.dma_start(rw_sb[:], rw).then_inc(w_in, 16)
            sp.dma_start(rows_sb[:], rows).then_inc(w_in, 16)

        @block.scalar
        def _(act):
            act.wait_ge(var_ready, 1)
            nc.scalar.activation(rstd[:, :], rstd[:, :], ACT.Sqrt).then_inc(std_ready, 1)
            for n in range(TILES):
                s = n % 2
                act.wait_ge(turned, n + 1)
                if n >= 2:
                    act.wait_ge(logits_done, n - 1)
                    act.wait_ge(xt_ready, n - 1)
                nc.scalar.copy(slot[:, s], t_ps[s][:, :]).then_inc(slot_ready, 1)
            act.wait_ge(shifted, 1)
            nc.scalar.activation(work[:], work[:], ACT.Exp).then_inc(exp_done, 1)
            for n in range(TILES):
                act.wait_ge(gates_turned, n + 1)
                nc.scalar.copy(gt[0:E, n, :], g_ps[n % 2][0:E, 0:P]).then_inc(gt_ready, 1)

        @block.gpsimd
        def _(pool):
            for n in range(TILES):
                pool.wait_ge(slot_ready, n + 1)
                nc.gpsimd.tensor_copy(xt[:, :, n * P:(n + 1) * P], slot[:, n % 2]).then_inc(xt_ready, 1)

        @block.tensor
        def _(pe):
            pe.wait_ge(w_in, 32)
            for n in range(TILES + 1):
                s = n % 2
                if n < TILES:
                    pe.wait_ge(xn_ready, n + 1)
                    if n >= 2:
                        pe.wait_ge(slot_ready, n - 1)
                    for c in range(CH):
                        last = nc.tensor.transpose(t_ps[s][:, c * P:(c + 1) * P], xn[:, s, c * P:(c + 1) * P], ident[:, :])
                    last.then_inc(turned, 1)
                if n >= 1:
                    m = n - 1
                    pe.wait_ge(slot_ready, m + 1)
                    if m >= 2:
                        pe.wait_ge(logits_out, m - 1)
                    for c in range(CH):
                        last = nc.tensor.matmul(l_ps[m % 2][:, 0:E], slot[:, m % 2, c, :], rw_sb[:, c, :],
                                                start=(c == 0), stop=(c == CH - 1))
                    last.then_inc(logits_done, 1)
            pe.wait_ge(gates_ready, 1)
            for n in range(TILES):
                if n >= 2:
                    pe.wait_ge(gt_ready, n - 1)
                nc.tensor.transpose(g_ps[n % 2][0:E, 0:P], gates[:, n, :], ident[:, :]).then_inc(gates_turned, 1)

        @block.vector
        def _(dve):
            own = Own(dve, dve_own)
            V = nc.vector

            def over(a, n):
                return a.unsqueeze(2).to_broadcast([P, a.shape[1], n])

            def pick(out, values, mark, best, order, n):
                own.done(V.tensor_reduce(best, values, AX_X, ALU.max))
                own.done(V.tensor_tensor(mark, values, over(best, n), ALU.is_equal))
                own.done(V.tensor_tensor(mark, mark, order.unsqueeze(1).to_broadcast([P, T, n]), ALU.mult))
                own.done(V.tensor_reduce(best, mark, AX_X, ALU.max))
                own.done(V.tensor_tensor(out, mark, over(best, n), ALU.is_equal))

            own.done(V.memset(gt[:], 1.0))
            norm_stats(nc, dve, own, X, bn, mv, rstd, var_ready, std_ready, 1)
            dve.wait_ge(w_in, 32)
            for n in range(TILES + 1):
                if n < TILES:
                    if n >= 2:
                        dve.wait_ge(turned, n - 1)
                    normalise(nc, xn[:, n % 2, :], X, n, mv, rstd).then_inc(xn_ready, 1)
                if n >= 1:
                    m = n - 1
                    dve.wait_ge(logits_done, m + 1)
                    V.tensor_tensor(work[:, m, :], l_ps[m % 2][:, 0:E], rows_sb[:, 0:E], ALU.add).then_inc(logits_out, 1)
            dve.wait_ge(logits_out, TILES)
            own.done(V.tensor_reduce(top[:], work[:], AX_X, ALU.max))
            V.tensor_tensor(work[:], work[:], over(top[:], E), ALU.subtract).then_inc(shifted, 1)
            dve.wait_ge(exp_done, 1)
            own.done(V.tensor_reduce(top[:], work[:], AX_X, ALU.add))
            own.done(V.reciprocal(top[:], top[:]))
            own.done(V.tensor_tensor(work[:], work[:], over(top[:], E), ALU.mult))
            own.done(V.tensor_tensor(scores[:], work[:], rows_sb[:, E:2 * E].unsqueeze(1).to_broadcast([P, T, E]), ALU.add))
            own.done(V.tensor_reduce(gwork[:], scores[:].rearrange("p t (g e) -> p t g e", g=EGROUPS), AX_X, ALU.max))
            order, gorder = rows_sb[:, 2 * E:3 * E], rows_sb[:, 3 * E:3 * E + EGROUPS]
            pick(keep[:], gwork[:], gamong[:], top[:], gorder, EGROUPS)
            own.done(V.scalar_tensor_tensor(gwork[:], keep[:], -1e30, gwork[:], ALU.mult, ALU.add))
            pick(gtop[:], gwork[:], gamong[:], top[:], gorder, EGROUPS)
            own.done(V.tensor_tensor(keep[:], keep[:], gtop[:], ALU.add))
            own.done(V.tensor_scalar(gwork[:], keep[:], 1.0, 1e30, ALU.subtract, ALU.mult))
            four = lambda a: a.rearrange("p t (g e) -> p (t g) e", g=EGROUPS)
            flat = lambda a: over(a.rearrange("p t g -> p (t g)"), GS)
            own.done(V.tensor_tensor(four(left[:]), four(scores[:]), flat(keep[:]), ALU.mult))
            own.done(V.tensor_tensor(four(left[:]), four(left[:]), flat(gwork[:]), ALU.add))
            pick(picked[:], left[:], among[:], top[:], order, E)
            own.done(V.scalar_tensor_tensor(left[:], picked[:], -2e30, left[:], ALU.mult, ALU.add))
            pick(work[:], left[:], among[:], top[:], order, E)
            own.done(V.tensor_tensor(picked[:], picked[:], work[:], ALU.add))
            own.done(V.tensor_tensor(gates[:], picked[:], scores[:], ALU.mult))
            own.done(V.tensor_scalar(gs[:, :, 0:E], gates[:], tg[:, 3:4], None, ALU.mult))
            own.done(V.memset(gs[:, :, E:EXPERTS], 1.0))
            V.tensor_scalar(gs[:, :, E:EXPERTS], gs[:, :, E:EXPERTS], tg[:, 3:4], None, ALU.mult).then_inc(gates_ready, 1)


def experts(nc, X, out, xt, gs, gt, w, b3, tg):
    stack = ExitStack()
    with stack:
        def sb(name, shape):
            return stack.enter_context(nc.sbuf_tensor(name, shape, F32))

        def sem(name):
            return stack.enter_context(nc.semaphore(name))

        def banks(name, n=2):
            return [stack.enter_context(nc.psum_tensor(f"{name}{s}", [P, DIM], F32)) for s in range(n)]

        QUARTERS = OCTETS
        w_sb = sb("w_sb", [P, 2, W_COLS])
        w12_sb = w_sb[:, :, 0:W3].rearrange("p s (c k n) -> p s c k n", c=CH, k=2)
        b3_sb = sb("b3_sb", [E1 + 1, DIM])
        act_sb = sb("act_sb", [P, 2, DIM])
        h_sb = sb("h_sb", [P, 2, DIM])
        a_ps, b_ps, y_ps = banks("a_ps"), banks("b_ps"), banks("y_ps", 4)
        w_in, b_in = [sem("w4_in0"), sem("w4_in1")], sem("b4_in")
        up_done, silu_done, h_ready = sem("up_done"), sem("silu_done"), sem("h4_ready")
        y_done, added, stored = sem("y4_done"), sem("added4"), sem("stored")
        bias_done, bias_added = sem("bias_done"), sem("bias_added")
        ROUNDS = EXPERTS // 2
        block = stack.enter_context(nc.Block())

        STEPS = 2 * QUARTERS

        @block.sync
        def _(sp):
            sp.dma_start(b3_sb[:], b3).then_inc(b_in, 16)

            def load(r, s):
                e = 2 * r + s
                sp.dma_start(w_sb[:, s], w[bass.ds(e, 1)].rearrange("e p n -> (e p) n")).then_inc(w_in[s], 16)

            for s in range(2):
                load(0, s)
            with sp.Fori(1, ROUNDS) as r:
                for s in range(2):
                    sp.wait_ge(y_done, r * (4 * STEPS) + (16 * s - 8))
                    load(r, s)
            for q in range(QUARTERS):
                sp.wait_ge(added, 4 + 4 * (QUARTERS * (EXPERTS - 1) + q + 1))
                sp.dma_start(out[4 * q:4 * q + 4].rearrange("t p d -> p t d"), X[:, 4 * q:4 * q + 4, :]).then_inc(stored, 16)
            sp.wait_ge(stored, 16 * QUARTERS)

        @block.tensor
        def _(pe):
            pe.sem_inc(y_done, 8)
            pe.wait_ge(b_in, 16)
            for n in range(TILES):
                if n >= 4:
                    pe.wait_ge(bias_added, n - 3)
                nc.tensor.matmul(y_ps[n % 4][:, :], gt[:, n, :], b3_sb[:, :], start=True, stop=True).then_inc(bias_done, 1)
            pe.wait_ge(bias_added, TILES)

            def up(r, k):
                s, q = k // QUARTERS % 2, k % QUARTERS
                if q == 0:
                    pe.wait_ge(w_in[s], r * 16 + (16 if k < STEPS else 32))
                pe.wait_ge(h_ready, r * STEPS + (k + 1))
                for half, banks_of in enumerate((a_ps, b_ps)):
                    for c in range(CH):
                        last = nc.tensor.matmul(banks_of[k % 2][:, :], w12_sb[:, s, c, half, :],
                                                xt[:, c, q * DIM:(q + 1) * DIM], start=(c == 0), stop=(c == CH - 1))
                    last.then_inc(up_done, 1)

            def down(r, k):
                pe.wait_ge(h_ready, r * STEPS + (k + 3))
                for j in range(4):
                    pe.wait_ge(added, r * (4 * STEPS) + (4 * k + j + 1))
                    nc.tensor.matmul(y_ps[j][:, :], h_sb[:, k % 2, j * P:(j + 1) * P], w_sb[:, k // QUARTERS, W3:B1],
                                     start=True, stop=True).then_inc(y_done, 1)

            up(0, 0)
            with pe.Fori(0, ROUNDS - 1) as r:
                for k in range(STEPS):
                    up(r, k + 1)
                    down(r, k)
            for k in range(STEPS):
                if k + 1 < STEPS:
                    up(ROUNDS - 1, k + 1)
                down(ROUNDS - 1, k)

        @block.scalar
        def _(act):
            with act.Fori(0, ROUNDS) as r:
                for k in range(STEPS):
                    act.wait_ge(up_done, r * (2 * STEPS) + (2 * k + 1))
                    act.wait_ge(h_ready, r * STEPS + (k + 1))
                    nc.scalar.activation(act_sb[:, k % 2, :], a_ps[k % 2][:, :], ACT.Silu,
                                         bias=w_sb[:, k // QUARTERS % 2, B1:B1 + 1]).then_inc(silu_done, 1)

        @block.vector
        def _(dve):
            dve.sem_inc(h_ready, 2)
            dve.sem_inc(added, 4)
            for n in range(TILES):
                dve.wait_ge(bias_done, n + 1)
                nc.vector.scalar_tensor_tensor(X[:, n, :], y_ps[n % 4][:, :], tg[:, 3:4], X[:, n, :],
                                               ALU.mult, ALU.add).then_inc(bias_added, 1)

            def hidden(r, k):
                dve.wait_ge(silu_done, r * STEPS + (k + 1))
                dve.wait_ge(up_done, r * (2 * STEPS) + (2 * k + 2))
                dve.wait_ge(y_done, r * (4 * STEPS) + (4 * k + 4))
                nc.vector.scalar_tensor_tensor(h_sb[:, k % 2, :], b_ps[k % 2][:, :],
                                               w_sb[:, k // QUARTERS % 2, B2:B2 + 1], act_sb[:, k % 2, :],
                                               ALU.add, ALU.mult).then_inc(h_ready, 1)

            def gather(r, k):
                for j in range(4):
                    tile = k % QUARTERS * 4 + j
                    dve.wait_ge(y_done, r * (4 * STEPS) + (4 * k + j + 9))
                    nc.vector.scalar_tensor_tensor(X[:, tile, :], y_ps[j][:, :],
                                                   gs[:, tile, bass.ds(2 * r + k // QUARTERS, 1)], X[:, tile, :],
                                                   ALU.mult, ALU.add).then_inc(added, 1)

            hidden(0, 0)
            with dve.Fori(0, ROUNDS - 1) as r:
                for k in range(STEPS):
                    hidden(r, k + 1)
                    gather(r, k)
            for k in range(STEPS):
                if k + 1 < STEPS:
                    hidden(ROUNDS - 1, k + 1)
                gather(ROUNDS - 1, k)


def flamingo_gated_kernel(nc, x, ctx, ctx_t, gates4, w_qkvo, b_qkvo, ident_in, route_a, bw, desc, wq, wk, wv, wo,
                          rw, rows, w, b3, out):
    with ExitStack() as stack:
        def sb(name, shape):
            return stack.enter_context(nc.sbuf_tensor(name, shape, F32))

        X = sb("X", [P, TILES, DIM])
        tg = sb("tg", [P, 4])
        ident = sb("ident", [P, P])
        bn, mv, rstd = sb("bn", [P, TILES, 6]), sb("mv", [P, TILES, 2]), sb("rstd", [P, TILES])
        window_attention(nc, X, x, ctx, w_qkvo, b_qkvo, gates4, ident_in, tg, ident, bn, mv, rstd)
        top1_lora(nc, X, route_a, bw, desc, tg, ident, bn, mv, rstd)
        latent_attention(nc, X, ctx_t, wq, wk, wv, wo, tg, ident, bn, mv, rstd)
        xt = sb("xt", [P, CH, TILES * P])
        gates, gs, gt = sb("gates", [P, TILES, E1]), sb("gs", [P, TILES, EXPERTS]), sb("gt", [E1 + 1, TILES, P])
        route(nc, X, xt, gates, gs, gt, rw, rows, tg, ident, bn, mv, rstd)
        experts(nc, X, out, xt, gs, gt, w, b3, tg)


def laid_out(i):
    import numpy as np
    a = {k: np.asarray(v) for k, v in i.items()}

    def by_chunk(w):
        return w.reshape(CH, P, -1).transpose(1, 0, 2)

    def twice(w):
        z = np.zeros((P, P), np.float32)
        z[:TOK, :TOK] = z[TOK:, TOK:] = w.T
        return z

    o = {}
    o["x"] = a["x"].reshape(TILES, P, DIM)
    o["ctx"] = a["ctx_4096"].reshape(TILES, P, DIM)
    o["ctx_t"] = a["ctx_4096"].reshape(OCTETS, DIM, CH, P).transpose(0, 3, 2, 1)
    g = np.stack([a["g_xattn"][0], a["g_ffn"][0], a["g_xattn"][1], a["g_ffn"][1]])
    o["gates4"] = np.broadcast_to(g, (P, 4))
    o["w_qkvo"] = np.stack([twice(a[f"L0_xattn_W{k}"]) for k in "qkvo"], axis=1)
    o["b_qkvo"] = np.stack([np.tile(a[f"L0_xattn_b{k}"], 2) for k in "qkvo"], axis=1)
    o["ident_in"] = np.eye(P, dtype=np.float32)
    o["route_a"] = by_chunk(np.concatenate([a["L0_ffn_route_w"], a["L0_ffn_A"].reshape(-1, DIM)]).T)
    o["bw"] = a["L0_ffn_Bw"].transpose(0, 2, 1).reshape(P, DIM)
    o["desc"] = np.broadcast_to(np.arange(LORA_E, 0, -1, dtype=np.float32), (P, LORA_E))
    o["wq"], o["wk"], o["wv"] = (by_chunk(a[f"L1_xattn_W{k}"].T) for k in "qkv")
    o["wo"] = a["L1_xattn_Wo"].reshape(DIM, QH, HD1).transpose(2, 1, 0)
    o["rw"] = by_chunk(a["L1_ffn_router_w"])
    rows = [a["L1_ffn_router_b"], a["L1_ffn_router_bias"], np.arange(E1, 0, -1), np.arange(EGROUPS, 0, -1)]
    o["rows"] = np.broadcast_to(np.concatenate([r.astype(np.float32) for r in rows]), (P, 3 * E1 + EGROUPS))

    def up(k):
        routed = a[f"L1_ffn_ew{k}"].reshape(E1, CH, P, INTER).transpose(0, 2, 1, 3)
        shared = a[f"L1_ffn_sw{k}"].reshape(CH, P, SHARED, INTER).transpose(2, 1, 0, 3)
        return np.concatenate([routed, shared])

    w12 = np.stack([up(1), up(2)], axis=3).reshape(EXPERTS, P, W3)
    w3 = np.concatenate([a["L1_ffn_ew3"], a["L1_ffn_sw3"].reshape(SHARED, INTER, DIM)])
    b12 = np.stack([np.concatenate([a[f"L1_ffn_eb{k}"], a[f"L1_ffn_sb{k}"].reshape(SHARED, INTER)])
                    for k in (1, 2)], axis=2)
    o["w"] = np.concatenate([w12, w3, b12], axis=2)
    o["b3"] = np.concatenate([a["L1_ffn_eb3"], a["L1_ffn_sb3"][None]])
    return {k: np.ascontiguousarray(v) for k, v in o.items()}


def kernel(**inputs):
    import concourse.bacc as bacc
    from concourse.bass_utils import run_bass_kernel_spmd

    arrays = laid_out(inputs)
    nc = bacc.Bacc("TRN2", target_bir_lowering=False, num_devices=1)
    args = {k: nc.dram_tensor(f"in_{k}", v.shape, mybir.dt.from_np(v.dtype), kind="ExternalInput").ap()
            for k, v in arrays.items()}
    out = nc.dram_tensor("out_0", (TILES, P, DIM), F32, kind="ExternalOutput").ap()
    flamingo_gated_kernel(nc, out=out, **args)
    got = run_bass_kernel_spmd(nc, [{f"in_{k}": v for k, v in arrays.items()}], core_ids=[0])
    return got.results[0]["out_0"].reshape(BATCH, TOK, DIM)
```

```python
from contextlib import ExitStack

import concourse.bass as bass
from concourse import mybir

F32 = mybir.dt.float32
U32 = mybir.dt.uint32
ALU = mybir.AluOpType
ACT = mybir.ActivationFunctionType
AX_X = mybir.AxisListType.X

P = 128
BATCH, TOK, DIM = 32, 64, 512
TILES = BATCH * TOK // P
CH = DIM // P
EPS = 1e-5

HEADS, HD, WINDOW = 8, TOK // 8, 16
LEFT = WINDOW // 2
GROUPS = 2
PAIRS = TILES // GROUPS
TPAD = DIM + WINDOW
UNIT = 8

LORA_E, RANK = 8, 16

QH, KV, HD1 = 16, 4, 96
G = QH // KV
OCTETS = 4
OB = BATCH // OCTETS
OT_TILES = TILES // OCTETS

E1, INTER = 16, 128
SHARED = 2
EXPERTS = E1 + SHARED
EGROUPS = 4
W3 = CH * 2 * INTER
B1, B2, W_COLS = W3 + DIM, W3 + DIM + 1, W3 + DIM + 2
MAX_TILES = (2 * BATCH * TOK + E1 * (P - 1)) // P // 2 * 2 + 2
ROW_PARTS = (("router_b", E1), ("router_bias", E1), ("order", E1), ("order_g", EGROUPS), ("steps", E1),
             ("upto", E1 * E1), ("tile", MAX_TILES))
ROWS = sum(n for _, n in ROW_PARTS)


class Own:

    def __init__(self, engine, semaphore):
        self.engine, self.semaphore = engine, semaphore
        self.base, self.n = 0, 0

    def mark(self, instruction):
        instruction.then_inc(self.semaphore, 1)
        self.n += 1

    def wait(self):
        self.engine.wait_ge(self.semaphore, self.base + self.n)

    def done(self, instruction):
        self.mark(instruction)
        self.wait()

    def enter(self, i, each):
        self.start, self.each = self.base + self.n, each
        self.base, self.n = i * each + self.start, 0

    def leave(self, rounds):
        assert self.n == self.each, (self.n, self.each)
        self.base, self.n = self.start + rounds * self.each, 0


def norm_stats(nc, dve, own, X, bn, mv, rstd, var_ready, std_ready, std_count):
    for t in range(TILES):
        own.mark(nc.vector.bn_stats(bn[:, t, :], X[:, t, :]))
    own.wait()
    for t in range(TILES):
        own.mark(nc.vector.bn_aggr(mv[:, t, :], bn[:, t, :]))
    own.wait()
    nc.vector.tensor_scalar_add(rstd[:, :], mv[:, :, 1], EPS).then_inc(var_ready, 1)
    dve.wait_ge(std_ready, std_count)
    own.done(nc.vector.reciprocal(rstd[:, :], rstd[:, :]))


def normalise(nc, out, X, t, mv, rstd):
    return nc.vector.tensor_scalar(out, X[:, t, :], mv[:, t, 0:1], rstd[:, t:t + 1], ALU.subtract, ALU.mult)


def window_attention(nc, X, x, ctx, w_qkvo, b_qkvo, gates, ident_in, tg, ident, bn, mv, rstd):
    stack = ExitStack()
    with stack:
        def sb(name, shape):
            return stack.enter_context(nc.sbuf_tensor(name, shape, F32))

        def sem(name):
            return stack.enter_context(nc.semaphore(name))

        w_sb = sb("w0", [P, 4, P])
        b_sb = sb("b0", [P, 4])
        xn = sb("xn0", [P, 2, DIM])
        cond = sb("cond", [P, 2, DIM])
        stage = sb("stage", [P, 2, 3, DIM])
        q_h = sb("q_h", [P, HD, DIM])
        k_h = sb("k_h", [P, HD, TPAD])
        v_h = sb("v_h", [P, HD, TPAD])
        dots = sb("dots", [P, WINDOW, DIM])
        prod = sb("prod", [P, UNIT, DIM])
        gprod = sb("gprod", [P, 2, UNIT, DIM])
        peak = sb("peak", [P, DIM])
        total = sb("total", [P, DIM])
        o_h = q_h
        back = sb("back", [P, 2, DIM])
        proj = sb("proj", [P, 2, DIM])
        qkv_ps = [[stack.enter_context(nc.psum_tensor(f"qkv_ps{s}{k}", [P, DIM], F32)) for k in range(3)]
                  for s in range(2)]
        sum_ps = [stack.enter_context(nc.psum_tensor(f"sum_ps{s}", [P, DIM], F32)) for s in range(2)]

        w_in, x_in, cond_in = sem("w_in"), sem("x_in"), [sem("cond_in0"), sem("cond_in1")]
        pads, tanh_done = sem("pads"), sem("tanh_done")
        var_ready, std_ready, dve_own, act_own = sem("var0"), sem("std0"), sem("own0"), sem("act_own0")
        xn_ready, qkv_done, staged = sem("xn_ready"), sem("qkv_done"), sem("staged")
        rows_out, heads_in, outputs_out = [sem("rows_out0"), sem("rows_out1")], sem("heads_in"), sem("outputs_out")
        multiplied, consumed = sem("multiplied"), sem("consumed")
        copied = sem("copied")
        shifted, exp_done, outputs = sem("shifted"), sem("exp_done"), sem("outputs")
        back_in, wo_done = [sem("back_in0"), sem("back_in1")], sem("wo_done")
        proj_ready, added = sem("proj_ready"), sem("added")
        block = stack.enter_context(nc.Block())

        by_row = nc.dram_tensor("by_row", (4, TILES, P, DIM), F32, kind="Internal").ap()

        def by_head(k, g):
            return by_row[k, g * PAIRS:(g + 1) * PAIRS].rearrange("j (r f) n -> (j r) f n", f=HD)

        def window(row, half):
            a = v_h[:, row, half * 256:half * 256 + 256]
            return bass.AP(a.tensor, a.offset, [list(a.ap[0]), [1, WINDOW], [1, 256]])

        @block.sync
        def _(sp):
            sp.dma_start(w_sb[:], w_qkvo).then_inc(w_in, 16)
            sp.dma_start(b_sb[:], b_qkvo).then_inc(w_in, 16)
            sp.dma_start(tg[:], gates).then_inc(w_in, 16)
            sp.dma_start(ident[:], ident_in).then_inc(w_in, 16)
            for part in range(4):
                sp.dma_start(X[:, 4 * part:4 * part + 4, :],
                             x[4 * part:4 * part + 4].rearrange("t p d -> p t d")).then_inc(x_in, 16)
            for g in range(GROUPS):
                for j in range(PAIRS):
                    n, s = g * PAIRS + j, j % 2
                    if n >= 2:
                        sp.wait_ge(qkv_done, 3 * (n - 1))
                    sp.dma_start(cond[:, s, :], ctx[n]).then_inc(cond_in[s], 16)
                if g == 0:
                    sp.wait_ge(pads, 2)
                for s in range(2):
                    sp.wait_ge(rows_out[s], 16 * (PAIRS // 2) * (g + 1))
                if g > 0:
                    sp.wait_ge(outputs_out, 16 * g)
                for k, dst in enumerate((q_h[:, :, :], k_h[:, :, LEFT:LEFT + DIM], v_h[:, :, LEFT:LEFT + DIM])):
                    sp.dma_start(dst, by_head(k, g)).then_inc(heads_in, 16)
                sp.wait_ge(outputs, g + 1)
                sp.dma_start(by_head(3, g), o_h[:, :, :]).then_inc(outputs_out, 16)
                sp.wait_ge(outputs_out, 16 * (g + 1))
                for j in range(PAIRS):
                    n, s = g * PAIRS + j, j % 2
                    if n >= 2:
                        sp.wait_ge(wo_done, n - 1)
                    sp.dma_start(back[:, s, :], by_row[3, n]).then_inc(back_in[s], 16)

        @block.gpsimd
        def _(pool):
            nc.gpsimd.memset(k_h[:, :, :], 0.0).then_inc(pads, 1)
            nc.gpsimd.memset(v_h[:, :, :], 0.0).then_inc(pads, 1)
            for g in range(GROUPS):
                pool.wait_ge(heads_in, 48 * (g + 1))
                with pool.Fori(0, WINDOW // 4) as i:
                    for s in range(2):
                        pool.wait_ge(consumed, 2 * i + (s + 16 * g + 1))
                        nc.gpsimd.tensor_tensor(gprod[:, s], q_h[:, :, :],
                                                k_h[:, :, bass.ds(4 * i + (2 * s + 1), DIM)],
                                                ALU.mult).then_inc(multiplied, 1)
                pool.wait_ge(exp_done, g + 1)
                for i in range(HD // 2):
                    for s in range(2):
                        pool.wait_ge(consumed, 2 * i + s + 16 * g + 9)
                        a = v_h[:, 2 * i + 1, 8 * s:8 * s + DIM]
                        shifted_v = bass.AP(a.tensor, a.offset, [list(a.ap[0]), [1, UNIT], [1, DIM]])
                        nc.gpsimd.tensor_tensor(gprod[:, s], dots[:, 8 * s:8 * s + 8, :], shifted_v,
                                                ALU.mult).then_inc(multiplied, 1)

        @block.scalar
        def _(act):
            act.sem_inc(copied, 2)
            act.wait_ge(w_in, 64)
            nc.scalar.activation(tg[:, :], tg[:, :], ACT.Tanh).then_inc(tanh_done, 1)
            act.wait_ge(var_ready, 1)
            nc.scalar.activation(rstd[:, :], rstd[:, :], ACT.Sqrt).then_inc(std_ready, 1)
            for g in range(GROUPS):
                for j in range(PAIRS):
                    n, s = g * PAIRS + j, j % 2
                    if n >= 2:
                        act.wait_ge(rows_out[s], 16 * (n // 2))
                    for k in range(3):
                        act.wait_ge(qkv_done, 3 * n + k + 1)
                        nc.scalar.activation(stage[:, s, k, :], qkv_ps[s][k][:, :], ACT.Identity,
                                             bias=b_sb[:, k:k + 1]).then_inc(staged, 1)
                    act.wait_ge(staged, 3 * n + 3)
                    act.dma_start(by_row[0:3, n].rearrange("k p d -> p k d"), stage[:, s]).then_inc(rows_out[s], 16)
                with act.Fori(0, WINDOW // 4) as i:
                    for s in range(2):
                        act.wait_ge(consumed, 2 * i + (s + 16 * g + 3))
                        nc.scalar.copy(dots[:, 4 * i + (2 * s + 1), :], sum_ps[s][:, :]).then_inc(copied, 1)
                act.wait_ge(shifted, g + 1)
                nc.scalar.activation(dots[:, :, :], dots[:, :, :], ACT.Exp, scale=HD ** -0.5).then_inc(exp_done, 1)
                for i in range(HD // 2):
                    act.wait_ge(consumed, 16 * g + 12 + 2 * i)
                    nc.scalar.copy(o_h[:, 2 * i + 1, :], sum_ps[i % 2][:, :]).then_inc(copied, 1)
                for j in range(PAIRS):
                    n, s = g * PAIRS + j, j % 2
                    act.wait_ge(wo_done, n + 1)
                    if n >= 2:
                        act.wait_ge(added, n - 1)
                    nc.scalar.activation(proj[:, s, :], qkv_ps[s][0][:, :], ACT.Identity,
                                         bias=b_sb[:, 3:4]).then_inc(proj_ready, 1)

        @block.tensor
        def _(pe):
            pe.sem_inc(consumed, 2)
            pe.wait_ge(w_in, 64)
            for g in range(GROUPS):
                if g > 0:
                    pe.wait_ge(proj_ready, PAIRS * g)
                for j in range(PAIRS):
                    n, s = g * PAIRS + j, j % 2
                    if j >= 2:
                        pe.wait_ge(staged, 3 * (n - 1))
                    pe.wait_ge(xn_ready, n + 1)
                    pe.wait_ge(cond_in[s], 16 * (n // 2 + 1))
                    for k, rhs in enumerate((xn[:, s, :], cond[:, s, :], cond[:, s, :])):
                        nc.tensor.matmul(qkv_ps[s][k][:, :], w_sb[:, k, :], rhs, start=True, stop=True)\
                          .then_inc(qkv_done, 1)
                with pe.Fori(0, WINDOW // 4) as i:
                    for s in range(2):
                        pe.wait_ge(multiplied, 2 * i + (s + 16 * g + 1))
                        pe.wait_ge(copied, 2 * i + (s + 12 * g + 1))
                        for r in range(UNIT):
                            last = nc.tensor.matmul(sum_ps[s][:, :], ident[:, :], gprod[:, s, r, :],
                                                    start=(r == 0), stop=(r == UNIT - 1))
                        last.then_inc(consumed, 1)
                for i in range(HD // 2):
                    pe.wait_ge(copied, 12 * g + 9 + i)
                    for s in range(2):
                        pe.wait_ge(multiplied, 16 * g + 9 + 2 * i + s)
                        for r in range(UNIT):
                            last = nc.tensor.matmul(sum_ps[i % 2][:, :], ident[:, :], gprod[:, s, r, :],
                                                    start=(s == 0 and r == 0), stop=(s == 1 and r == UNIT - 1))
                        last.then_inc(consumed, 1)
                for j in range(PAIRS):
                    n, s = g * PAIRS + j, j % 2
                    if j >= 2:
                        pe.wait_ge(proj_ready, n - 1)
                    pe.wait_ge(back_in[s], 16 * (n // 2 + 1))
                    nc.tensor.matmul(qkv_ps[s][0][:, :], w_sb[:, 3, :], back[:, s, :], start=True, stop=True)\
                      .then_inc(wo_done, 1)

        @block.vector
        def _(dve):
            own = Own(dve, dve_own)
            dve.wait_ge(x_in, 64)
            norm_stats(nc, dve, own, X, bn, mv, rstd, var_ready, std_ready, 1)
            dve.wait_ge(tanh_done, 1)
            for g in range(GROUPS):
                for j in range(PAIRS):
                    n, s = g * PAIRS + j, j % 2
                    if n >= 2:
                        dve.wait_ge(qkv_done, 3 * (n - 2) + 1)
                    normalise(nc, xn[:, s, :], X, n, mv, rstd).then_inc(xn_ready, 1)
                dve.wait_ge(heads_in, 48 * (g + 1))
                with dve.Fori(0, WINDOW // 2) as i:
                    own.enter(i, 2)
                    own.done(nc.vector.tensor_tensor(prod[:], q_h[:, :, :], k_h[:, :, bass.ds(2 * i, DIM)], ALU.mult))
                    own.done(nc.vector.tensor_reduce(dots[:, 2 * i, :], prod[:].rearrange("p d t -> p t d"),
                                                     AX_X, ALU.add))
                    own.leave(WINDOW // 2)
                dve.wait_ge(copied, 12 * g + 10)
                own.done(nc.vector.tensor_reduce(peak[:, :], dots[:].rearrange("p w t -> p t w"), AX_X, ALU.max))
                nc.vector.tensor_tensor(dots[:], dots[:], peak[:].unsqueeze(1).to_broadcast([P, WINDOW, DIM]),
                                        ALU.subtract).then_inc(shifted, 1)
                dve.wait_ge(exp_done, g + 1)
                own.done(nc.vector.tensor_reduce(total[:, :], dots[:].rearrange("p w t -> p t w"), AX_X, ALU.add))
                own.done(nc.vector.reciprocal(total[:, :], total[:, :]))
                for d in range(0, HD, 2):
                    for half in range(2):
                        t = slice(256 * half, 256 * half + 256)
                        halved = prod[:].rearrange("p a b -> p (a b)").rearrange("p (w t) -> p w t", w=WINDOW)
                        own.done(nc.vector.tensor_tensor(halved, dots[:, :, t], window(d, half), ALU.mult))
                        own.done(nc.vector.tensor_reduce(o_h[:, d, t], halved.rearrange("p w t -> p t w"),
                                                         AX_X, ALU.add))
                dve.wait_ge(copied, 12 * g + 14)
                nc.vector.tensor_tensor(o_h[:, :, :], o_h[:, :, :], total[:].unsqueeze(1).to_broadcast([P, HD, DIM]),
                                        ALU.mult).then_inc(outputs, 1)
                for j in range(PAIRS):
                    n, s = g * PAIRS + j, j % 2
                    dve.wait_ge(proj_ready, n + 1)
                    nc.vector.scalar_tensor_tensor(X[:, n, :], proj[:, s, :], tg[:, 0:1], X[:, n, :],
                                                   ALU.mult, ALU.add).then_inc(added, 1)


def top1_lora(nc, X, route_a, bw, desc_in, tg, ident, bn, mv, rstd):
    W = LORA_E + LORA_E * RANK
    stack = ExitStack()
    with stack:
        def sb(name, shape):
            return stack.enter_context(nc.sbuf_tensor(name, shape, F32))

        def sem(name):
            return stack.enter_context(nc.semaphore(name))

        def banks(name):
            return [stack.enter_context(nc.psum_tensor(f"{name}{s}", [P, DIM], F32)) for s in range(2)]

        ra_sb = sb("ra_sb", [P, CH, W])
        bw_sb = sb("bw_sb", [P, DIM])
        desc = sb("desc8", [P, LORA_E])
        xn = sb("xn1", [P, 2, DIM])
        xt = sb("xt1", [P, 2, CH, P])
        wh = sb("wh", [P, 2, P])
        wht = sb("wht", [P, 2, P])
        best, among, first, weight = (sb(n, s) for n, s in (("best", [P, 1]), ("among", [P, LORA_E]),
                                                            ("first", [P, 1]), ("weight", [P, LORA_E])))
        t_ps, h_ps, w_ps, o_ps = banks("t_ps"), banks("h_ps"), banks("w_ps"), banks("o_ps")
        w_in, var_ready, std_ready, dve_own = sem("w1_in"), sem("var1"), sem("std1"), sem("own1")
        xn_ready, turned, xt_ready, h_done = sem("xn1_ready"), sem("turned"), sem("xt_ready"), sem("h_done")
        wh_ready, wh_turned, wht_ready = sem("wh_ready"), sem("wh_turned"), sem("wht_ready")
        o_done, added = sem("o_done"), sem("added1")
        block = stack.enter_context(nc.Block())

        @block.sync
        def _(sp):
            sp.dma_start(ra_sb[:], route_a).then_inc(w_in, 16)
            sp.dma_start(bw_sb[:], bw).then_inc(w_in, 16)
            sp.dma_start(desc[:], desc_in).then_inc(w_in, 16)

        @block.scalar
        def _(act):
            act.wait_ge(var_ready, 1)
            nc.scalar.activation(rstd[:, :], rstd[:, :], ACT.Sqrt).then_inc(std_ready, 1)
            for n in range(TILES + 2):
                if n < TILES:
                    act.wait_ge(turned, n + 1)
                    if n >= 2:
                        act.wait_ge(h_done, n - 1)
                    nc.scalar.copy(xt[:, n % 2], t_ps[n % 2][:, :]).then_inc(xt_ready, 1)
                if n >= 2:
                    m = n - 2
                    act.wait_ge(wh_turned, m + 1)
                    if m >= 2:
                        act.wait_ge(o_done, m - 1)
                    nc.scalar.copy(wht[:, m % 2], w_ps[m % 2][:, 0:P]).then_inc(wht_ready, 1)

        @block.tensor
        def _(pe):
            pe.wait_ge(w_in, 48)
            for n in range(TILES + 3):
                s = n % 2
                if n < TILES:
                    pe.wait_ge(xn_ready, n + 1)
                    if n >= 2:
                        pe.wait_ge(xt_ready, n - 1)
                    for c in range(CH):
                        last = nc.tensor.transpose(t_ps[s][:, c * P:(c + 1) * P], xn[:, s, c * P:(c + 1) * P], ident[:, :])
                    last.then_inc(turned, 1)
                if 1 <= n <= TILES:
                    m = n - 1
                    pe.wait_ge(xt_ready, m + 1)
                    if m >= 2:
                        pe.wait_ge(wh_ready, m - 1)
                    for c in range(CH):
                        last = nc.tensor.matmul(h_ps[m % 2][:, 0:W], xt[:, m % 2, c, :], ra_sb[:, c, :],
                                                start=(c == 0), stop=(c == CH - 1))
                    last.then_inc(h_done, 1)
                if 2 <= n <= TILES + 1:
                    m = n - 2
                    pe.wait_ge(wh_ready, m + 1)
                    if m >= 2:
                        pe.wait_ge(wht_ready, m - 1)
                    nc.tensor.transpose(w_ps[m % 2][:, 0:P], wh[:, m % 2, :], ident[:, :]).then_inc(wh_turned, 1)
                if n >= 3:
                    m = n - 3
                    pe.wait_ge(wht_ready, m + 1)
                    if m >= 2:
                        pe.wait_ge(added, m - 1)
                    nc.tensor.matmul(o_ps[m % 2][:, :], wht[:, m % 2, :], bw_sb[:, :], start=True, stop=True)\
                      .then_inc(o_done, 1)

        @block.vector
        def _(dve):
            own = Own(dve, dve_own)
            norm_stats(nc, dve, own, X, bn, mv, rstd, var_ready, std_ready, 1)
            dve.wait_ge(w_in, 48)
            for n in range(TILES + 3):
                if n < TILES:
                    if n >= 2:
                        dve.wait_ge(turned, n - 1)
                    normalise(nc, xn[:, n % 2, :], X, n, mv, rstd).then_inc(xn_ready, 1)
                if 1 <= n <= TILES:
                    m = n - 1
                    logits = h_ps[m % 2][:, 0:LORA_E]
                    dve.wait_ge(h_done, m + 1)
                    own.done(nc.vector.tensor_reduce(best[:], logits, AX_X, ALU.max))
                    own.done(nc.vector.scalar_tensor_tensor(among[:], logits, best[:, 0:1], desc[:],
                                                            ALU.is_equal, ALU.mult))
                    own.done(nc.vector.tensor_reduce(first[:], among[:], AX_X, ALU.max))
                    own.done(nc.vector.tensor_scalar(weight[:], among[:], first[:, 0:1], best[:, 0:1],
                                                     ALU.is_equal, ALU.mult))
                    if m >= 2:
                        dve.wait_ge(wh_turned, m - 1)
                    nc.vector.tensor_tensor(wh[:, m % 2, :].rearrange("p (e r) -> p e r", e=LORA_E),
                                            h_ps[m % 2][:, LORA_E:W].rearrange("p (e r) -> p e r", e=LORA_E),
                                            weight[:].unsqueeze(2).to_broadcast([P, LORA_E, RANK]),
                                            ALU.mult).then_inc(wh_ready, 1)
                if n >= 3:
                    m = n - 3
                    dve.wait_ge(o_done, m + 1)
                    nc.vector.scalar_tensor_tensor(X[:, m, :], o_ps[m % 2][:, :], tg[:, 1:2], X[:, m, :],
                                                   ALU.mult, ALU.add).then_inc(added, 1)


def latent_attention(nc, X, ctx_t, wq, wk, wv, wo, tg, ident, bn, mv, rstd):
    stack = ExitStack()
    with stack:
        def sb(name, shape):
            return stack.enter_context(nc.sbuf_tensor(name, shape, F32))

        def sem(name):
            return stack.enter_context(nc.semaphore(name))

        def banks(name):
            return [stack.enter_context(nc.psum_tensor(f"{name}{s}", [P, DIM], F32)) for s in range(2)]

        wq_sb = sb("wq_sb", [P, CH, QH * HD1])
        wk_sb = sb("wk_sb", [P, CH, KV * HD1])
        wv_sb = sb("wv_sb", [P, CH, KV * HD1])
        wo_sb = sb("wo_sb", [HD1, QH, DIM])
        xn = sb("xn2", [P, 2, DIM])
        ht = sb("ht", [P, CH, OB, 2, TOK])
        kt = sb("kt", [HD1, KV, OB, 2 * TOK])
        v = sb("v", [P, OB, KV * HD1])
        qt = sb("qt", [HD1, 2, OB, G, TOK])
        ot = sb("ot", [HD1, 2, G, DIM])
        probs = sb("probs", [P, 2, 2, P])
        probs_t = sb("probs_t", [P, 2, 2 * P])
        npeak = sb("npeak", [P, 2, 2])
        total = sb("total2", [P, 2, 2])
        big_ps, s_ps, p_ps, o_ps = banks("big_ps"), banks("s_ps"), banks("p_ps"), banks("o2_ps")

        uses = [("T", k) for k in range(OT_TILES)] + [("K", k) for k in range(2 * KV)] + [("V", b) for b in range(OB)]
        uses += [("Q", 0, h) for h in range(G)]
        OUT_AT = {3: (0,), 5: (1,), 7: (2, 3)}
        for a in range(KV):
            for b in range(OB):
                if b % 2 == 0 and a + 1 < KV:
                    uses.append(("Q", a + 1, b // 2))
                if a > 0:
                    uses += [("Y", a - 1, k) for k in OUT_AT.get(b, ())]
        uses += [("Y", KV - 1, k) for k in range(OT_TILES)]
        at = {use: n for n, use in enumerate(uses)}
        USES, UNITS = len(uses), KV * OB

        w_in, ctx_in = sem("w2_in"), sem("ctx_in")
        var_ready, std_ready, dve_own = sem("var2"), sem("std2"), sem("own2")
        xn_ready = sem("xn2_ready")
        big_done = sem("big_done")
        big_free = [sem("big_free0"), sem("big_free1")]
        ht_ready, kt_ready, v_ready, q_ready = sem("ht_ready"), sem("kt_ready"), sem("v_ready"), sem("q_ready")
        scored, peaked, exp_done, normed = sem("scored"), sem("peaked"), sem("exp2_done"), sem("normed")
        p_turned, pt_ready, pv_done, o_ready, added = sem("p_turned"), sem("pt_ready"), sem("pv2_done"), sem("o_ready"), sem("added2")
        block = stack.enter_context(nc.Block())

        @block.sync
        def _(sp):
            for dst, src in ((wk_sb, wk), (wv_sb, wv), (wq_sb, wq), (wo_sb, wo)):
                sp.dma_start(dst[:], src).then_inc(w_in, 16)
            with sp.Fori(0, OCTETS) as o:
                sp.wait_ge(big_done, o * USES + 1)
                for c in range(CH):
                    sp.dma_start(ht[:, c, :, 0, :], ctx_t[bass.ds(o, 1), :, c].rearrange("o p (b t) -> (o p) b t", b=OB))\
                      .then_inc(ctx_in, 16)

        @block.scalar
        def _(act):
            act.wait_ge(var_ready, 1)
            nc.scalar.activation(rstd[:, :], rstd[:, :], ACT.Sqrt).then_inc(std_ready, 1)

            def big(o, use):
                n = at[use]
                act.wait_ge(big_done, o * USES + n + 1)
                return big_ps[n % 2], big_free[n % 2]

            with act.Fori(0, OCTETS) as o:
                for k in range(OT_TILES):
                    ps, free = big(o, ("T", k))
                    nc.scalar.copy(ht[:, :, 2 * k:2 * k + 2, 1, :], ps[:, :].rearrange("p (c b t) -> p c b t", c=CH, b=2)).then_inc(free, 1)
                for k in range(2 * KV):
                    ps, free = big(o, ("K", k))
                    nc.scalar.copy(kt[:, k // 2, k % 2 * 4:k % 2 * 4 + 4, :], ps[0:HD1, :]).then_inc(free, 1)
                for h in range(G):
                    ps, free = big(o, ("Q", 0, h))
                    nc.scalar.activation(qt[:, 0, :, h, :], ps[0:HD1, :], ACT.Copy, scale=HD1 ** -0.5).then_inc(free, 1)
                for u in range(UNITS + 2):
                    a, b = u // OB, u % OB
                    if u < UNITS:
                        if b % 2 == 0 and a + 1 < KV:
                            ps, free = big(o, ("Q", a + 1, b // 2))
                            nc.scalar.activation(qt[:, (a + 1) % 2, :, b // 2, :], ps[0:HD1, :], ACT.Copy,
                                                 scale=HD1 ** -0.5).then_inc(free, 1)
                        act.wait_ge(peaked, o * UNITS + u + 1)
                        if u >= 2:
                            act.wait_ge(p_turned, o * UNITS + u - 1)
                        for g2 in range(2):
                            nc.scalar.activation(probs[:, u % 2, g2, :], s_ps[u % 2][:, g2 * P:(g2 + 1) * P], ACT.Exp,
                                                 bias=npeak[:, u % 2, g2:g2 + 1],
                                                 accum_out=total[:, u % 2, g2:g2 + 1]).then_inc(exp_done, 1)
                    if u >= 2:
                        w = u - 2
                        act.wait_ge(p_turned, o * UNITS + w + 1)
                        if w >= 2:
                            act.wait_ge(pv_done, o * UNITS + w - 1)
                        nc.scalar.copy(probs_t[:, w % 2, :], p_ps[w % 2][:, 0:2 * P]).then_inc(pt_ready, 1)

        @block.tensor
        def _(pe):
            pe.sem_inc(big_free[0], 1)
            pe.sem_inc(big_free[1], 1)
            pe.wait_ge(w_in, 64)

            def big(o, use):
                n = at[use]
                pe.wait_ge(big_free[n % 2], o * (USES // 2) + (n // 2 + 1))
                return big_ps[n % 2]

            def queries(o, a, h):
                ps = big(o, ("Q", a, h))
                head = a * G + h
                for c in range(CH):
                    last = nc.tensor.matmul(ps[0:HD1, :], wq_sb[:, c, head * HD1:(head + 1) * HD1], ht[:, c, :, 1, :],
                                            start=(c == 0), stop=(c == CH - 1))
                last.then_inc(big_done, 1)

            def project(o, a, k):
                if k == 0:
                    pe.wait_ge(o_ready, o * UNITS + OB * (a + 1))
                ps = big(o, ("Y", a, k))
                for h in range(G):
                    last = nc.tensor.matmul(ps[:, :], ot[:, a % 2, h, k * P:(k + 1) * P], wo_sb[:, a * G + h, :],
                                            start=(h == 0), stop=(h == G - 1))
                last.then_inc(big_done, 1)

            with pe.Fori(0, OCTETS) as o:
                for k in range(OT_TILES):
                    pe.wait_ge(xn_ready, o * OT_TILES + k + 1)
                    ps = big(o, ("T", k))
                    for c in range(CH):
                        last = nc.tensor.transpose(ps[:, c * P:(c + 1) * P], xn[:, k % 2, c * P:(c + 1) * P], ident[:, :])
                    last.then_inc(big_done, 1)
                pe.wait_ge(ctx_in, o * (16 * CH) + 16 * CH)
                for k in range(2 * KV):
                    ps = big(o, ("K", k))
                    if k == 0:
                        pe.wait_ge(big_free[1], o * (USES // 2) + 3)
                    for c in range(CH):
                        last = nc.tensor.matmul(ps[0:HD1, :], wk_sb[:, c, k // 2 * HD1:(k // 2 + 1) * HD1],
                                                ht[:, c, k % 2 * 4:k % 2 * 4 + 4], start=(c == 0), stop=(c == CH - 1))
                    last.then_inc(big_done, 1)
                for b in range(OB):
                    ps = big(o, ("V", b))
                    for c in range(CH):
                        last = nc.tensor.matmul(ps[:, 0:KV * HD1], ht[:, c, b], wv_sb[:, c, :],
                                                start=(c == 0), stop=(c == CH - 1))
                    last.then_inc(big_done, 1)
                for h in range(G):
                    queries(o, 0, h)
                for u in range(UNITS + 3):
                    a, b = u // OB, u % OB
                    if u < UNITS:
                        if b == 0:
                            first = at[("Q", a, G - 2)], at[("Q", a, G - 1)]
                            for n in first:
                                pe.wait_ge(big_free[n % 2], o * (USES // 2) + n // 2 + 2)
                        if u >= 2:
                            pe.wait_ge(exp_done, o * (2 * UNITS) + 2 * (u - 1))
                        for g2 in range(2):
                            last = nc.tensor.matmul(s_ps[u % 2][:, g2 * P:(g2 + 1) * P],
                                                    qt[:, a % 2, b, 2 * g2:2 * g2 + 2],
                                                    kt[:, a, b], start=True, stop=True)
                        last.then_inc(scored, 1)
                        if b % 2 == 0 and a + 1 < KV:
                            queries(o, a + 1, b // 2)
                    if u >= 2 and u - 2 < UNITS:
                        w = u - 2
                        pe.wait_ge(normed, o * UNITS + w + 1)
                        if w >= 2:
                            pe.wait_ge(pt_ready, o * UNITS + w - 1)
                        for g2 in range(2):
                            last = nc.tensor.transpose(p_ps[w % 2][:, g2 * P:(g2 + 1) * P], probs[:, w % 2, g2, :], ident[:, :])
                        last.then_inc(p_turned, 1)
                    if u >= 3:
                        w = u - 3
                        pe.wait_ge(pt_ready, o * UNITS + w + 1)
                        if w >= 2:
                            pe.wait_ge(o_ready, o * UNITS + w - 1)
                        nc.tensor.matmul(o_ps[w % 2][0:HD1, 0:2 * P], v[:, w % OB, w // OB * HD1:(w // OB + 1) * HD1],
                                         probs_t[:, w % 2, :], start=True, stop=True).then_inc(pv_done, 1)
                    if OB < u < UNITS:
                        for k in OUT_AT.get(b, ()):
                            project(o, a - 1, k)
                for k in range(OT_TILES):
                    project(o, KV - 1, k)

        @block.vector
        def _(dve):
            own = Own(dve, dve_own)
            norm_stats(nc, dve, own, X, bn, mv, rstd, var_ready, std_ready, 1)

            def big(o, use):
                n = at[use]
                dve.wait_ge(big_done, o * USES + n + 1)
                return big_ps[n % 2], big_free[n % 2]

            def add(o, a, k):
                ps, free = big(o, ("Y", a, k))
                row = X[:, bass.ds(o * OT_TILES + k, 1), :].rearrange("p o d -> p (o d)")
                nc.vector.scalar_tensor_tensor(row, ps[:, :], tg[:, 2:3], row, ALU.mult, ALU.add).then_inc(free, 1)

            with dve.Fori(0, OCTETS) as o:
                own.enter(o, UNITS)
                for k in range(OT_TILES):
                    if k >= 2:
                        dve.wait_ge(big_done, o * USES + k - 1)
                    t = o * OT_TILES + k
                    nc.vector.tensor_scalar(xn[:, k % 2, :], X[:, bass.ds(t, 1), :].rearrange("p o d -> p (o d)"),
                                            mv[:, bass.ds(t, 1), 0:1].rearrange("p o d -> p (o d)"),
                                            rstd[:, bass.ds(t, 1)], ALU.subtract, ALU.mult).then_inc(xn_ready, 1)
                for b in range(OB):
                    ps, free = big(o, ("V", b))
                    nc.vector.tensor_copy(v[:, b, :], ps[:, 0:KV * HD1]).then_inc(free, 1)
                for u in range(UNITS + 3):
                    if u < UNITS:
                        dve.wait_ge(scored, o * UNITS + u + 1)
                        nc.vector.tensor_reduce(npeak[:, u % 2, :], s_ps[u % 2][:, 0:2 * P].rearrange("p (g s) -> p g s", g=2),
                                                AX_X, ALU.max, negate=True).then_inc(peaked, 1)
                    if 1 <= u <= UNITS:
                        w = u - 1
                        dve.wait_ge(exp_done, o * (2 * UNITS) + 2 * (w + 1))
                        own.done(nc.vector.reciprocal(total[:, w % 2, :], total[:, w % 2, :]))
                        nc.vector.tensor_tensor(probs[:, w % 2], probs[:, w % 2],
                                                total[:, w % 2, :].unsqueeze(2).to_broadcast([P, 2, P]),
                                                ALU.mult).then_inc(normed, 1)
                    if u >= 3:
                        w = u - 3
                        a, b = w // OB, w % OB
                        dve.wait_ge(pv_done, o * UNITS + w + 1)
                        if b == 0 and a >= 2:
                            dve.wait_ge(big_done, o * USES + at[("Y", a - 2, G - 1)] + 1)
                        nc.vector.tensor_copy(ot[:, a % 2, :, b * TOK:(b + 1) * TOK],
                                              o_ps[w % 2][0:HD1, 0:2 * P].rearrange("p (g q) -> p g q", g=G)).then_inc(o_ready, 1)
                    if OB < u < UNITS:
                        for k in OUT_AT.get(u % OB, ()):
                            add(o, u // OB - 1, k)
                for k in range(OT_TILES):
                    add(o, KV - 1, k)
                own.leave(OCTETS)


def route(nc, X, tg, ident, bn, mv, rstd, wr, te, slot_of, tok_of, gs, xn_rows, table, rw, rows, tri_in, tok_ids, wr_in, w_s, b3):
    stack = ExitStack()
    with stack:
        def sb(name, shape, dtype=F32):
            return stack.enter_context(nc.sbuf_tensor(name, shape, dtype))

        def sem(name):
            return stack.enter_context(nc.semaphore(name))

        def banks(name, n=2):
            return [stack.enter_context(nc.psum_tensor(f"{name}{s}", [P, DIM], F32)) for s in range(n)]

        T, E, GS = TILES, E1, E1 // EGROUPS
        STEPS = SHARED * OCTETS
        rw_sb = sb("rw_sb", [P, CH, E])
        rows_sb = sb("rows_sb", [P, ROWS])
        row, at = {}, 0
        for name, n in ROW_PARTS:
            row[name] = rows_sb[:, at:at + n]
            at += n
        tri = sb("tri", [P, P])
        ones = sb("ones", [P, P])
        tab_sb = sb("tab_sb", [MAX_TILES, P])
        ids = sb("ids", [P, T])
        w_sb = sb("w_sb", [P, SHARED, W_COLS])
        w12_sb = w_sb[:, :, 0:W3].rearrange("p s (c k n) -> p s c k n", c=CH, k=2)
        b3_sb = sb("b3_sb", [E + 1, DIM])
        xt = sb("xt", [P, CH, T * P])
        xn = sb("xn3", [P, 2, DIM])
        slot = sb("slot", [P, 2, CH, P])
        act_sb, h_sb = sb("act_sb", [P, 2, DIM]), sb("h_sb", [P, 2, DIM])
        gates = sb("gates", [P, T, E + 1])
        gt = sb("gt", [E + 1, 2, P])
        scores, work, among, best1, best2, left, pos = (
            sb(n, [P, T, E]) for n in ("scores", "work", "among3", "best1", "best2", "left", "pos"))
        top, gtop, gwork, gamong, keep = (sb("top3", [P, T]), sb("gtop", [P, T, EGROUPS]), sb("gwork", [P, T, EGROUPS]),
                                          sb("gamong", [P, T, EGROUPS]), sb("keep", [P, T, EGROUPS]))
        before = sb("before", [P, T + 1, E])
        square = sb("square", [P, E, E])
        tiles_of, ends, starts = sb("tiles_of", [P, E]), sb("ends", [P, E]), sb("starts", [P, E])
        te_f = sb("te_f", [1, MAX_TILES])
        te_work = h_sb[0:1].rearrange("p s n -> p (s n)")[:, 0:MAX_TILES * E].rearrange("p (i e) -> p i e", e=E)
        a_ps, b_ps, y_ps = banks("a_ps"), banks("b_ps"), banks("y_ps", 4)
        t_ps, l_ps, prefix_ps, total_ps, tab_ps, gt_ps = a_ps, b_ps, y_ps[0], y_ps[1], y_ps[2], b_ps

        w_in, ids_in, ws_in = sem("w3_in"), sem("ids_in"), sem("ws_in")
        var_ready, std_ready, dve_own = sem("var3"), sem("std3"), sem("own3")
        xn_ready, rows_out = sem("xn3_ready"), [sem("xn_rows_out0"), sem("xn_rows_out1")]
        turned, slot_ready, xt_ready = sem("turned3"), sem("slot_ready"), sem("xt3_ready")
        logits_done, logits_out, shifted, exp_done = sem("logits_done"), sem("logits_out"), sem("shifted3"), sem("exp3")
        ones_ready, picks_ready, counted, gates_ready = sem("ones_ready"), sem("picks_ready"), sem("counted"), sem("gates_ready")
        zeroed, slots_ready, scattered, tab_in = sem("zeroed"), sem("slots_ready"), sem("scattered"), sem("tab_in")
        tok_ready = sem("tok_ready")
        tab_turned, gates_turned, gt_ready = sem("tab_turned"), sem("gates_turned"), sem("gt_ready")
        bias_done, bias_added = sem("bias_done"), sem("bias_added")
        up_done, silu_done, h_ready, y_done, added = sem("up_done"), sem("silu_done"), sem("h_ready"), sem("y_done"), sem("added3")
        block = stack.enter_context(nc.Block())

        @block.sync
        def _(sp):
            for dst, src in ((rw_sb, rw), (rows_sb, rows), (tri, tri_in), (b3_sb, b3)):
                sp.dma_start(dst[:], src).then_inc(w_in, 16)
            sp.dma_start(ids[:], tok_ids).then_inc(ids_in, 16)
            sp.wait_ge(ones_ready, 1)
            sp.dma_start(table.rearrange("(i p) o -> i (p o)", p=P), tab_sb[:]).then_inc(zeroed, 16)
            sp.dma_start(w_sb[:], w_s).then_inc(ws_in, 16)
            for n in range(T):
                sp.wait_ge(xn_ready, n + 1)
                sp.dma_start(xn_rows[n * P:(n + 1) * P, :], xn[:, n % 2, :]).then_inc(rows_out[n % 2], 16)
            sp.wait_ge(scattered, 16 * 2 * T)
            sp.dma_start(tab_sb[:], table.rearrange("(i p) o -> i (p o)", p=P)).then_inc(tab_in, 16)

        @block.gpsimd
        def _(pool):
            for n in range(T):
                pool.wait_ge(slot_ready, n + 1)
                nc.gpsimd.tensor_copy(xt[:, :, n * P:(n + 1) * P], slot[:, n % 2]).then_inc(xt_ready, 1)
            pool.wait_ge(zeroed, 16)
            pool.wait_ge(ids_in, 16)
            for k in range(2):
                pool.wait_ge(slots_ready, k + 1)
                for n in range(T):
                    nc.gpsimd.indirect_dma_start(
                        table, bass.IndirectOffsetOnAxis(ap=slot_of[:, k, n:n + 1], axis=0), ids[:, n:n + 1], None)\
                        .then_inc(scattered, 16)

        @block.scalar
        def _(act):
            for part in range(4):
                act.dma_start(wr[:, 4 * part:4 * part + 4, :], wr_in[4 * part:4 * part + 4].rearrange("e p n -> p e n"))\
                   .then_inc(ws_in, 16)
            act.wait_ge(var_ready, 1)
            nc.scalar.activation(rstd[:, :], rstd[:, :], ACT.Sqrt).then_inc(std_ready, 1)
            for n in range(T):
                s = n % 2
                act.wait_ge(turned, n + 1)
                if n >= 2:
                    act.wait_ge(logits_done, n - 1)
                    act.wait_ge(xt_ready, n - 1)
                nc.scalar.copy(slot[:, s], t_ps[s][:, :]).then_inc(slot_ready, 1)
            act.wait_ge(shifted, 1)
            nc.scalar.activation(work[:], work[:], ACT.Exp).then_inc(exp_done, 1)
            for n in range(T):
                act.wait_ge(gates_turned, n + 1)
                if n >= 2:
                    act.wait_ge(bias_done, n - 1)
                nc.scalar.copy(gt[:, n % 2, :], gt_ps[n % 2][0:E + 1, 0:P]).then_inc(gt_ready, 1)
            for k in range(STEPS):
                act.wait_ge(up_done, 2 * k + 1)
                if k >= 2:
                    act.wait_ge(h_ready, k - 1)
                nc.scalar.activation(act_sb[:, k % 2, :], a_ps[k % 2][:, :], ACT.Silu,
                                     bias=w_sb[:, k // OCTETS, B1:B1 + 1]).then_inc(silu_done, 1)

        @block.tensor
        def _(pe):
            pe.wait_ge(w_in, 64)
            for n in range(T + 1):
                s = n % 2
                if n < T:
                    pe.wait_ge(xn_ready, n + 1)
                    if n >= 2:
                        pe.wait_ge(slot_ready, n - 1)
                    for c in range(CH):
                        last = nc.tensor.transpose(t_ps[s][:, c * P:(c + 1) * P], xn[:, s, c * P:(c + 1) * P], ident[:, :])
                    last.then_inc(turned, 1)
                if n >= 1:
                    m = n - 1
                    pe.wait_ge(slot_ready, m + 1)
                    if m >= 2:
                        pe.wait_ge(logits_out, m - 1)
                    for c in range(CH):
                        last = nc.tensor.matmul(l_ps[m % 2][:, 0:E], slot[:, m % 2, c, :], rw_sb[:, c, :],
                                                start=(c == 0), stop=(c == CH - 1))
                    last.then_inc(logits_done, 1)
            pe.wait_ge(ones_ready, 1)
            pe.wait_ge(picks_ready, 1)
            flat = among[:].rearrange("p t e -> p (t e)")
            nc.tensor.matmul(prefix_ps[:, 0:T * E], tri[:, :], flat, start=True, stop=True).then_inc(counted, 1)
            nc.tensor.matmul(total_ps[:, 0:T * E], ones[:, :], flat, start=True, stop=True).then_inc(counted, 1)

            pe.wait_ge(gates_ready, 1)
            for n in range(T + 1):
                if n < T:
                    if n >= 2:
                        pe.wait_ge(gt_ready, n - 1)
                    nc.tensor.transpose(gt_ps[n % 2][0:E + 1, 0:P], gates[:, n, :], ident[:, :]).then_inc(gates_turned, 1)
                if n >= 1:
                    m = n - 1
                    pe.wait_ge(gt_ready, m + 1)
                    if m == 0:
                        pe.wait_ge(slots_ready, 2)
                    if m >= 4:
                        pe.wait_ge(bias_added, m - 3)
                    nc.tensor.matmul(y_ps[m % 4][:, :], gt[:, m % 2, :], b3_sb[:, :], start=True, stop=True).then_inc(bias_done, 1)
            pe.wait_ge(ws_in, 80)
            pe.wait_ge(xt_ready, T)
            pe.wait_ge(bias_added, T)

            def up(k):
                s, q = k // OCTETS, k % OCTETS
                if k >= 2:
                    pe.wait_ge(h_ready, k - 1)
                for half, banks_of in enumerate((a_ps, b_ps)):
                    for c in range(CH):
                        last = nc.tensor.matmul(banks_of[k % 2][:, :], w12_sb[:, s, c, half, :],
                                                xt[:, c, q * DIM:(q + 1) * DIM], start=(c == 0), stop=(c == CH - 1))
                    last.then_inc(up_done, 1)

            up(0)
            for k in range(STEPS):
                if k + 1 < STEPS:
                    up(k + 1)
                if k == 3:
                    pe.wait_ge(tab_in, 16)
                    pe.wait_ge(added, 4 * k - 1)
                    nc.tensor.transpose(tab_ps[:, 0:MAX_TILES], tab_sb[:, :], ident[0:MAX_TILES, 0:MAX_TILES])\
                      .then_inc(tab_turned, 1)
                pe.wait_ge(h_ready, k + 1)
                for j in range(4):
                    if k >= 1:
                        pe.wait_ge(added, 4 * (k - 1) + j + 1)
                    if k == 3 and j == 2:
                        pe.wait_ge(tok_ready, 1)
                    nc.tensor.matmul(y_ps[j][:, :], h_sb[:, k % 2, j * P:(j + 1) * P], w_sb[:, k // OCTETS, W3:B1],
                                     start=True, stop=True).then_inc(y_done, 1)

        @block.vector
        def _(dve):
            own = Own(dve, dve_own)
            V = nc.vector

            def over(a, n):
                return a.unsqueeze(2).to_broadcast([P, a.shape[1], n])

            def pick(out, values, mark, best, order, n):
                own.done(V.tensor_reduce(best, values, AX_X, ALU.max))
                own.done(V.tensor_tensor(mark, values, over(best, n), ALU.is_equal))
                own.done(V.tensor_tensor(mark, mark, order.unsqueeze(1).to_broadcast([P, T, n]), ALU.mult))
                own.done(V.tensor_reduce(best, mark, AX_X, ALU.max))
                own.done(V.tensor_tensor(out, mark, over(best, n), ALU.is_equal))

            own.mark(V.memset(gates[:], 1.0))
            own.mark(V.memset(ones[:], 1.0))
            own.mark(V.memset(before[:, 0, :], 0.0))
            V.memset(tab_sb[:], 0.0).then_inc(ones_ready, 1)
            norm_stats(nc, dve, own, X, bn, mv, rstd, var_ready, std_ready, 1)
            dve.wait_ge(w_in, 64)
            for n in range(T + 1):
                if n < T:
                    if n >= 2:
                        dve.wait_ge(turned, n - 1)
                        dve.wait_ge(rows_out[n % 2], 16 * (n // 2))
                    normalise(nc, xn[:, n % 2, :], X, n, mv, rstd).then_inc(xn_ready, 1)
                if n >= 1:
                    m = n - 1
                    dve.wait_ge(logits_done, m + 1)
                    V.tensor_tensor(work[:, m, :], l_ps[m % 2][:, 0:E], row["router_b"], ALU.add).then_inc(logits_out, 1)
            dve.wait_ge(logits_out, T)
            own.done(V.tensor_reduce(top[:], work[:], AX_X, ALU.max))
            V.tensor_tensor(work[:], work[:], over(top[:], E), ALU.subtract).then_inc(shifted, 1)
            dve.wait_ge(exp_done, 1)
            own.done(V.tensor_reduce(top[:], work[:], AX_X, ALU.add))
            own.done(V.reciprocal(top[:], top[:]))
            own.done(V.tensor_tensor(work[:], work[:], over(top[:], E), ALU.mult))
            own.done(V.tensor_tensor(scores[:], work[:], row["router_bias"].unsqueeze(1).to_broadcast([P, T, E]), ALU.add))
            own.done(V.tensor_reduce(gwork[:], scores[:].rearrange("p t (g e) -> p t g e", g=EGROUPS), AX_X, ALU.max))
            pick(keep[:], gwork[:], gamong[:], top[:], row["order_g"], EGROUPS)
            own.done(V.scalar_tensor_tensor(gwork[:], keep[:], -1e30, gwork[:], ALU.mult, ALU.add))
            pick(gtop[:], gwork[:], gamong[:], top[:], row["order_g"], EGROUPS)
            own.done(V.tensor_tensor(keep[:], keep[:], gtop[:], ALU.add))
            own.done(V.tensor_scalar(gwork[:], keep[:], 1.0, 1e30, ALU.subtract, ALU.mult))
            four = lambda a: a.rearrange("p t (g e) -> p (t g) e", g=EGROUPS)
            flat = lambda a: over(a.rearrange("p t g -> p (t g)"), GS)
            own.done(V.tensor_tensor(four(left[:]), four(scores[:]), flat(keep[:]), ALU.mult))
            own.done(V.tensor_tensor(four(left[:]), four(left[:]), flat(gwork[:]), ALU.add))
            pick(best1[:], left[:], among[:], top[:], row["order"], E)
            own.done(V.scalar_tensor_tensor(left[:], best1[:], -2e30, left[:], ALU.mult, ALU.add))
            pick(best2[:], left[:], among[:], top[:], row["order"], E)
            V.tensor_tensor(among[:], best1[:], best2[:], ALU.add).then_inc(picks_ready, 1)
            dve.wait_ge(picks_ready, 1)
            V.tensor_tensor(gates[:, :, 0:E], among[:], scores[:], ALU.mult).then_inc(gates_ready, 1)
            for k, best in enumerate((best1, best2)):
                own.done(V.tensor_tensor(work[:], best[:], scores[:], ALU.mult))
                own.done(V.tensor_reduce(top[:], work[:], AX_X, ALU.add))
                own.done(V.tensor_scalar(gs[:, k, :], top[:], tg[:, 3:4], None, ALU.mult))
            dve.wait_ge(counted, 2)
            for t in range(T):
                own.done(V.tensor_tensor(before[:, t + 1, :], total_ps[:, t * E:(t + 1) * E], before[:, t, :], ALU.add))
            own.done(V.tensor_tensor(square[:], over(before[:, T, :], E), row["steps"].unsqueeze(1).to_broadcast([P, E, E]),
                                     ALU.is_gt))
            own.done(V.tensor_reduce(tiles_of[:], square[:], AX_X, ALU.add))
            own.done(V.tensor_tensor(square[:], row["upto"].rearrange("p (a b) -> p a b", a=E),
                                     tiles_of[:].unsqueeze(1).to_broadcast([P, E, E]), ALU.mult))
            own.done(V.tensor_reduce(ends[:], square[:], AX_X, ALU.add))
            own.done(V.tensor_tensor(starts[:], ends[:], tiles_of[:], ALU.subtract))
            own.done(V.tensor_tensor(pos[:].rearrange("p t e -> p (t e)"), prefix_ps[:, 0:T * E],
                                     before[:, 0:T, :].rearrange("p t e -> p (t e)"), ALU.add))
            own.done(V.scalar_tensor_tensor(pos[:], starts[:].unsqueeze(1).to_broadcast([P, T, E]), float(P), pos[:],
                                            ALU.mult, ALU.add))
            for k, best in enumerate((best1, best2)):
                own.done(V.tensor_tensor(work[:], best[:], pos[:], ALU.mult))
                own.done(V.tensor_reduce(top[:], work[:], AX_X, ALU.add))
                V.tensor_copy(slot_of[:, k, :], top[:]).then_inc(slots_ready, 1)
                dve.wait_ge(slots_ready, k + 1)
            own.done(V.tensor_tensor(te_work, ends[0:1, :].unsqueeze(1).to_broadcast([1, MAX_TILES, E]),
                                     row["tile"][0:1, :].unsqueeze(2).to_broadcast([1, MAX_TILES, E]), ALU.is_le))
            own.done(V.tensor_reduce(te_f[:], te_work, AX_X, ALU.add))
            own.done(V.tensor_scalar(te[:], te_f[:], float(E - 1), None, ALU.min))
            for n in range(T):
                dve.wait_ge(bias_done, n + 1)
                V.scalar_tensor_tensor(X[:, n, :], y_ps[n % 4][:, :], tg[:, 3:4], X[:, n, :], ALU.mult, ALU.add)\
                 .then_inc(bias_added, 1)

            def hidden(k):
                dve.wait_ge(silu_done, k + 1)
                dve.wait_ge(up_done, 2 * k + 2)
                if k >= 2:
                    dve.wait_ge(y_done, 4 * (k - 1))
                V.scalar_tensor_tensor(h_sb[:, k % 2, :], b_ps[k % 2][:, :], w_sb[:, k // OCTETS, B2:B2 + 1],
                                       act_sb[:, k % 2, :], ALU.add, ALU.mult).then_inc(h_ready, 1)

            hidden(0)
            for k in range(STEPS):
                if k + 1 < STEPS:
                    hidden(k + 1)
                if k == 3:
                    dve.wait_ge(tab_turned, 1)
                    V.tensor_copy(tok_of[:], tab_ps[:, 0:MAX_TILES]).then_inc(tok_ready, 1)
                for j in range(4):
                    dve.wait_ge(y_done, 4 * k + j + 1)
                    tile = k % OCTETS * 4 + j
                    V.scalar_tensor_tensor(X[:, tile, :], y_ps[j][:, :], tg[:, 3:4], X[:, tile, :], ALU.mult, ALU.add)\
                     .then_inc(added, 1)


def routed(nc, X, out, ident, wr, te, slot_of, tok_of, gs, xn_rows, y_rows, b_in):
    stack = ExitStack()
    with stack:
        def sb(name, shape):
            return stack.enter_context(nc.sbuf_tensor(name, shape, F32))

        def sem(name):
            return stack.enter_context(nc.semaphore(name))

        def banks(name):
            return [stack.enter_context(nc.psum_tensor(f"{name}{s}", [P, DIM], F32)) for s in range(2)]

        DEEP = 4
        b_sb = sb("b_sb", [P, E1, 2 * INTER])
        xg = sb("xg", [P, DEEP, DIM])
        xgt = sb("xgt", [P, 2, CH, P])
        up_sb, silu_sb, h_sb = sb("up_sb", [P, 2, 2 * INTER]), sb("silu_sb", [P, 2, INTER]), sb("h5_sb", [P, 2, INTER])
        ht_sb = sb("ht5_sb", [P, 2, P])
        y_sb = sb("y_sb", [P, 4, DIM])
        back = sb("back5", [P, 4, DIM])
        t_ps, u_ps, ht_ps, y_ps = banks("t5_ps"), banks("u5_ps"), banks("ht5_ps"), banks("y5_ps")
        b_here = sem("b5_in")
        gathered = [sem(f"gathered{s}") for s in range(DEEP)]
        turned, xgt_ready, up_done, biased, silu_done = sem("turned5"), sem("xgt_ready"), sem("up5_done"), sem("biased"), sem("silu5")
        h_ready, h_turned, ht_ready, down_done, y_ready = sem("h5_ready"), sem("h5_turned"), sem("ht5_ready"), sem("down_done"), sem("y5_ready")
        y_out = [sem(f"y_out{s}") for s in range(4)]
        backed = [sem(f"backed{s}") for s in range(4)]
        combined, stored = sem("combined"), sem("stored")
        block = stack.enter_context(nc.Block())

        def in_steps(engine, step):
            for i in range(8):
                step(i, i)
            with engine.Fori(2, MAX_TILES // 4) as r:
                for j in range(4):
                    step(r * 4 + j, 8 + j)
            for i in range(MAX_TILES, MAX_TILES + 3):
                step(i, i)

        @block.sync
        def _(sp):
            sp.dma_start(b_sb[:], b_in).then_inc(b_here, 16)
            with sp.Fori(0, MAX_TILES // 4) as r:
                for s in range(4):
                    sp.wait_ge(y_ready, r * 4 + s + 1)
                    sp.dma_start(y_rows[bass.ds((r * 4 + s) * P, P), :], y_sb[:, s, :]).then_inc(y_out[s], 16)
            for n in range(TILES):
                sp.wait_ge(combined, 2 * n + 2)
                sp.dma_start(out[n], X[:, n, :]).then_inc(stored, 16)
            sp.wait_ge(stored, 16 * TILES)

        @block.gpsimd
        def _(pool):
            for i in range(MAX_TILES):
                if i >= DEEP:
                    pool.wait_ge(turned, i - DEEP + 1)
                nc.gpsimd.indirect_dma_start(xg[:, i % DEEP, :], None, xn_rows,
                                             bass.IndirectOffsetOnAxis(ap=tok_of[:, i:i + 1], axis=0))\
                    .then_inc(gathered[i % DEEP], 16)
            for s in range(4):
                pool.wait_ge(y_out[s], 16 * (MAX_TILES // 4))
            for m in range(2 * TILES):
                n, k = m // 2, m % 2
                if m >= 4:
                    pool.wait_ge(combined, m - 3)
                nc.gpsimd.indirect_dma_start(back[:, m % 4, :], None, y_rows,
                                             bass.IndirectOffsetOnAxis(ap=slot_of[:, k, n:n + 1], axis=0))\
                    .then_inc(backed[m % 4], 16)

        @block.scalar
        def _(act):
            def step(i, n):
                if n < MAX_TILES:
                    act.wait_ge(turned, i + 1)
                    if n >= 2:
                        act.wait_ge(up_done, i - 1)
                    nc.scalar.copy(xgt[:, n % 2], t_ps[n % 2][:, :]).then_inc(xgt_ready, 1)
                if 1 <= n <= MAX_TILES:
                    m = n - 1
                    act.wait_ge(biased, i)
                    if m >= 2:
                        act.wait_ge(h_ready, i - 2)
                    nc.scalar.activation(silu_sb[:, m % 2, :], up_sb[:, m % 2, 0:INTER], ACT.Silu).then_inc(silu_done, 1)
                if 2 <= n <= MAX_TILES + 1:
                    m = n - 2
                    act.wait_ge(h_turned, i - 1)
                    if m >= 2:
                        act.wait_ge(down_done, i - 3)
                    nc.scalar.copy(ht_sb[:, m % 2, :], ht_ps[m % 2][:, 0:P]).then_inc(ht_ready, 1)
                if n >= 3:
                    m = n - 3
                    act.wait_ge(down_done, i - 2)
                    if m >= 4:
                        act.wait_ge(y_out[m % 4], (i - 3 - m % 4) * 4)
                    nc.scalar.copy(y_sb[:, m % 4, :], y_ps[m % 2][:, :]).then_inc(y_ready, 1)

            in_steps(act, step)

        @block.tensor
        def _(pe):
            def expert(i):
                return pe.value_load(te[0:1, bass.ds(i, 1)], min_val=0, max_val=E1 - 1)

            def step(i, n):
                if n < MAX_TILES:
                    pe.wait_ge(gathered[n % DEEP], (i - n % DEEP) * (16 // DEEP) + 16)
                    if n >= 2:
                        pe.wait_ge(xgt_ready, i - 1)
                    for c in range(CH):
                        last = nc.tensor.transpose(t_ps[n % 2][:, c * P:(c + 1) * P], xg[:, n % DEEP, c * P:(c + 1) * P],
                                                   ident[:, :])
                    last.then_inc(turned, 1)
                if 1 <= n <= MAX_TILES:
                    m = n - 1
                    e = expert(i - 1)
                    pe.wait_ge(xgt_ready, i)
                    if m >= 2:
                        pe.wait_ge(biased, i - 2)
                    for c in range(CH):
                        last = nc.tensor.matmul(u_ps[m % 2][:, 0:2 * INTER], xgt[:, m % 2, c, :],
                                                wr[:, bass.ds(e, 1), c * 2 * INTER:(c + 1) * 2 * INTER],
                                                start=(c == 0), stop=(c == CH - 1))
                    last.then_inc(up_done, 1)
                if 2 <= n <= MAX_TILES + 1:
                    m = n - 2
                    pe.wait_ge(h_ready, i - 1)
                    if m >= 2:
                        pe.wait_ge(ht_ready, i - 3)
                    nc.tensor.transpose(ht_ps[m % 2][:, 0:P], h_sb[:, m % 2, :], ident[:, :]).then_inc(h_turned, 1)
                if n >= 3:
                    m = n - 3
                    e = expert(i - 3)
                    pe.wait_ge(ht_ready, i - 2)
                    if m >= 2:
                        pe.wait_ge(y_ready, i - 4)
                    nc.tensor.matmul(y_ps[m % 2][:, :], ht_sb[:, m % 2, :], wr[:, bass.ds(e, 1), W3:B1],
                                     start=True, stop=True).then_inc(down_done, 1)

            in_steps(pe, step)

        @block.vector
        def _(dve):
            dve.wait_ge(b_here, 16)

            def step(i, n):
                if n >= MAX_TILES:
                    return
                e = dve.value_load(te[0:1, bass.ds(i, 1)], min_val=0, max_val=E1 - 1)
                if n >= 2:
                    dve.wait_ge(silu_done, i - 1)
                dve.wait_ge(up_done, i + 1)
                nc.vector.tensor_tensor(up_sb[:, n % 2, :], u_ps[n % 2][:, 0:2 * INTER],
                                        b_sb[:, bass.ds(e, 1), :].rearrange("p e n -> p (e n)"), ALU.add).then_inc(biased, 1)
                dve.wait_ge(silu_done, i + 1)
                if n >= 2:
                    dve.wait_ge(h_turned, i - 1)
                nc.vector.tensor_tensor(h_sb[:, n % 2, :], silu_sb[:, n % 2, :], up_sb[:, n % 2, INTER:2 * INTER],
                                        ALU.mult).then_inc(h_ready, 1)

            in_steps(dve, step)
            for m in range(2 * TILES):
                n, k = m // 2, m % 2
                dve.wait_ge(backed[m % 4], 16 * (m // 4 + 1))
                nc.vector.scalar_tensor_tensor(X[:, n, :], back[:, m % 4, :], gs[:, k, n:n + 1], X[:, n, :],
                                               ALU.mult, ALU.add).then_inc(combined, 1)
                dve.wait_ge(combined, m + 1)


def flamingo_gated_kernel(nc, x, ctx, ctx_t, gates4, w_qkvo, b_qkvo, ident_in, route_a, bw, desc, wq, wk, wv, wo,
                          rw, rows, tri, tok_ids, w_routed, w_shared, b_routed, b3, out):
    with ExitStack() as stack:
        def sb(name, shape, dtype=F32):
            return stack.enter_context(nc.sbuf_tensor(name, shape, dtype))

        X = sb("X", [P, TILES, DIM])
        tg = sb("tg", [P, 4])
        ident = sb("ident", [P, P])
        bn, mv, rstd = sb("bn", [P, TILES, 6]), sb("mv", [P, TILES, 2]), sb("rstd", [P, TILES])
        window_attention(nc, X, x, ctx, w_qkvo, b_qkvo, gates4, ident_in, tg, ident, bn, mv, rstd)
        top1_lora(nc, X, route_a, bw, desc, tg, ident, bn, mv, rstd)
        latent_attention(nc, X, ctx_t, wq, wk, wv, wo, tg, ident, bn, mv, rstd)
        wr = sb("wr", [P, E1, W_COLS - 2])
        te = sb("te", [1, MAX_TILES], U32)
        slot_of = sb("slot_of", [P, 2, TILES], U32)
        tok_of = sb("tok_of", [P, MAX_TILES], U32)
        gs = sb("gs", [P, 2, TILES])
        xn_rows = nc.dram_tensor("xn_rows", (TILES * P, DIM), F32, kind="Internal").ap()
        y_rows = nc.dram_tensor("y_rows", (MAX_TILES * P, DIM), F32, kind="Internal").ap()
        table = nc.dram_tensor("table", (MAX_TILES * P, 1), F32, kind="Internal").ap()
        route(nc, X, tg, ident, bn, mv, rstd, wr, te, slot_of, tok_of, gs, xn_rows, table, rw, rows, tri, tok_ids,
              w_routed, w_shared, b3)
        routed(nc, X, out, ident, wr, te, slot_of, tok_of, gs, xn_rows, y_rows, b_routed)


def laid_out(i):
    import numpy as np
    a = {k: np.asarray(v) for k, v in i.items()}

    def by_chunk(w):
        return w.reshape(CH, P, -1).transpose(1, 0, 2)

    def twice(w):
        z = np.zeros((P, P), np.float32)
        z[:TOK, :TOK] = z[TOK:, TOK:] = w.T
        return z

    o = {}
    o["x"] = a["x"].reshape(TILES, P, DIM)
    o["ctx"] = a["ctx_4096"].reshape(TILES, P, DIM)
    o["ctx_t"] = a["ctx_4096"].reshape(OCTETS, DIM, CH, P).transpose(0, 3, 2, 1)
    g = np.stack([a["g_xattn"][0], a["g_ffn"][0], a["g_xattn"][1], a["g_ffn"][1]])
    o["gates4"] = np.broadcast_to(g, (P, 4))
    o["w_qkvo"] = np.stack([twice(a[f"L0_xattn_W{k}"]) for k in "qkvo"], axis=1)
    o["b_qkvo"] = np.stack([np.tile(a[f"L0_xattn_b{k}"], 2) for k in "qkvo"], axis=1)
    o["ident_in"] = np.eye(P, dtype=np.float32)
    o["route_a"] = by_chunk(np.concatenate([a["L0_ffn_route_w"], a["L0_ffn_A"].reshape(-1, DIM)]).T)
    o["bw"] = a["L0_ffn_Bw"].transpose(0, 2, 1).reshape(P, DIM)
    o["desc"] = np.broadcast_to(np.arange(LORA_E, 0, -1, dtype=np.float32), (P, LORA_E))
    o["wq"], o["wk"], o["wv"] = (by_chunk(a[f"L1_xattn_W{k}"].T) for k in "qkv")
    o["wo"] = a["L1_xattn_Wo"].reshape(DIM, QH, HD1).transpose(2, 1, 0)
    o["rw"] = by_chunk(a["L1_ffn_router_w"])
    parts = {"router_b": a["L1_ffn_router_b"], "router_bias": a["L1_ffn_router_bias"],
             "order": np.arange(E1, 0, -1), "order_g": np.arange(EGROUPS, 0, -1), "steps": np.arange(E1) * P,
             "upto": np.tril(np.ones((E1, E1))).ravel(), "tile": np.arange(MAX_TILES)}
    o["rows"] = np.broadcast_to(np.concatenate([parts[k].astype(np.float32) for k, _ in ROW_PARTS]), (P, ROWS))
    o["tri"] = np.triu(np.ones((P, P), np.float32), 1)
    o["tok_ids"] = np.arange(TILES * P, dtype=np.float32).reshape(TILES, P).T

    def up(k):
        routed = a[f"L1_ffn_ew{k}"].reshape(E1, CH, P, INTER).transpose(0, 2, 1, 3)
        shared = a[f"L1_ffn_sw{k}"].reshape(CH, P, SHARED, INTER).transpose(2, 1, 0, 3)
        return np.concatenate([routed, shared])

    w12 = np.stack([up(1), up(2)], axis=3).reshape(EXPERTS, P, W3)
    w3 = np.concatenate([a["L1_ffn_ew3"], a["L1_ffn_sw3"].reshape(SHARED, INTER, DIM)])
    b12 = np.stack([np.concatenate([a[f"L1_ffn_eb{k}"], a[f"L1_ffn_sb{k}"].reshape(SHARED, INTER)])
                    for k in (1, 2)], axis=2)
    o["w_routed"] = np.concatenate([w12, w3], axis=2)[:E1]
    o["w_shared"] = np.concatenate([w12, w3, b12], axis=2)[E1:].transpose(1, 0, 2)
    b_routed = np.concatenate([a["L1_ffn_eb1"], a["L1_ffn_eb2"]], axis=1)
    o["b_routed"] = np.broadcast_to(b_routed, (P, E1, 2 * INTER))
    o["b3"] = np.concatenate([a["L1_ffn_eb3"], a["L1_ffn_sb3"][None]])
    return {k: np.ascontiguousarray(v) for k, v in o.items()}


def kernel(**inputs):
    import concourse.bacc as bacc
    from concourse.bass_utils import run_bass_kernel_spmd

    arrays = laid_out(inputs)
    nc = bacc.Bacc("TRN2", target_bir_lowering=False, num_devices=1)
    args = {k: nc.dram_tensor(f"in_{k}", v.shape, mybir.dt.from_np(v.dtype), kind="ExternalInput").ap()
            for k, v in arrays.items()}
    out = nc.dram_tensor("out_0", (TILES, P, DIM), F32, kind="ExternalOutput").ap()
    flamingo_gated_kernel(nc, out=out, **args)
    got = run_bass_kernel_spmd(nc, [{f"in_{k}": v for k, v in arrays.items()}], core_ids=[0])
    return got.results[0]["out_0"].reshape(BATCH, TOK, DIM)
```

```python
from contextlib import ExitStack

import concourse.bass as bass
from concourse import mybir

F32 = mybir.dt.float32
U32 = mybir.dt.uint32
ALU = mybir.AluOpType
ACT = mybir.ActivationFunctionType
AX_X = mybir.AxisListType.X

P = 128
BATCH, TOK, DIM = 32, 64, 512
TILES = BATCH * TOK // P
CH = DIM // P
EPS = 1e-5

HEADS, HD, WINDOW = 8, TOK // 8, 16
LEFT = WINDOW // 2
GROUPS = 2
PAIRS = TILES // GROUPS
TPAD = DIM + WINDOW
UNIT = 8

LORA_E, RANK = 8, 16

QH, KV, HD1 = 16, 4, 96
G = QH // KV
HC = G * HD1 // P
PIECE = P - HD1
OCTETS = 4
OB = BATCH // OCTETS
OT_TILES = TILES // OCTETS

E1, INTER = 16, 128
SHARED = 2
EXPERTS = E1 + SHARED
EGROUPS = 4
W3 = CH * 2 * INTER
B1, B2, W_COLS = W3 + DIM, W3 + DIM + 1, W3 + DIM + 2
MAX_TILES = (2 * BATCH * TOK + E1 * (P - 1)) // P // 2 * 2 + 2
ROW_PARTS = (("router_b", E1), ("router_bias", E1), ("order", E1), ("order_g", EGROUPS), ("steps", E1),
             ("upto", E1 * E1), ("tile", MAX_TILES))
ROWS = sum(n for _, n in ROW_PARTS)


class Own:

    def __init__(self, engine, semaphore):
        self.engine, self.semaphore = engine, semaphore
        self.base, self.n = 0, 0

    def mark(self, instruction):
        instruction.then_inc(self.semaphore, 1)
        self.n += 1

    def wait(self):
        self.engine.wait_ge(self.semaphore, self.base + self.n)

    def done(self, instruction):
        self.mark(instruction)
        self.wait()

    def enter(self, i, each):
        self.start, self.each = self.base + self.n, each
        self.base, self.n = i * each + self.start, 0

    def leave(self, rounds):
        assert self.n == self.each, (self.n, self.each)
        self.base, self.n = self.start + rounds * self.each, 0


def tile_stats(nc, own, X, bn, mv, t):
    own.done(nc.vector.bn_stats(bn[:, t, :], X[:, t, :]))
    own.mark(nc.vector.bn_aggr(mv[:, t, :], bn[:, t, :]))


def deviations(nc, dve, own, mv, rstd, var_ready, std_ready):
    nc.vector.tensor_scalar_add(rstd[:, :], mv[:, :, 1], EPS).then_inc(var_ready, 1)
    dve.wait_ge(std_ready, 1)
    own.done(nc.vector.reciprocal(rstd[:, :], rstd[:, :]))


def normalise(nc, out, X, t, mv, rstd):
    return nc.vector.tensor_scalar(out, X[:, t, :], mv[:, t, 0:1], rstd[:, t:t + 1], ALU.subtract, ALU.mult)


def window_attention(nc, X, x, ctx, w_qkvo, b_qkvo, gates, ident_in, tg, ident, bn, mv, rstd):
    stack = ExitStack()
    with stack:
        def sb(name, shape):
            return stack.enter_context(nc.sbuf_tensor(name, shape, F32))

        def sem(name):
            return stack.enter_context(nc.semaphore(name))

        w_sb = sb("w0", [P, 4, P])
        b_sb = sb("b0", [P, 4])
        xn = sb("xn0", [P, 2, DIM])
        cond = sb("cond", [P, 2, DIM])
        stage = sb("stage", [P, 2, 3, DIM])
        q_h = sb("q_h", [P, HD, DIM])
        k_h = sb("k_h", [P, HD, TPAD])
        v_h = sb("v_h", [P, HD, TPAD])
        dots = sb("dots", [P, WINDOW, DIM])
        prod = sb("prod", [P, UNIT, DIM])
        gprod = sb("gprod", [P, 2, UNIT, DIM])
        v_0 = gprod[:, 1]
        peak = sb("peak", [P, DIM])
        total = sb("total", [P, DIM])
        o_h = sb("o_h", [P, HD, DIM])
        back, proj = [cond[:, s, :] for s in range(2)] + [stage[:, s, k, :] for s in range(2) for k in range(3)], xn
        qkv_ps = [[stack.enter_context(nc.psum_tensor(f"qkv_ps{s}{k}", [P, DIM], F32)) for k in range(3)]
                  for s in range(2)]
        sum_ps = [stack.enter_context(nc.psum_tensor(f"sum_ps{s}", [P, DIM], F32)) for s in range(2)]
        total_ps = qkv_ps[0][0], qkv_ps[1][0]

        w_in, x_in, cond_in = sem("w_in"), [sem(f"x_in{k}") for k in range(4)], [sem("cond_in0"), sem("cond_in1")]
        pads, tanh_done = sem("pads"), sem("tanh_done")
        var_ready, std_ready, dve_own = sem("var0"), sem("std0"), sem("own0")
        xn_ready, qkv_done, staged = sem("xn_ready"), sem("qkv_done"), sem("staged")
        rows_out, outputs_out = [sem("rows_out0"), sem("rows_out1")], sem("outputs_out")
        multiplied, consumed = sem("multiplied"), sem("consumed")
        values_out, keys_in, values_in, total_done = sem("values_out"), sem("keys_in"), sem("values_in"), sem("total_done")
        copied = sem("copied")
        shifted, exp_done, outputs = sem("shifted"), sem("exp_done"), sem("outputs")
        back_in, wo_done = [sem(f"back_in{k}") for k in range(PAIRS)], sem("wo_done")
        proj_ready, added = sem("proj_ready"), sem("added")
        block = stack.enter_context(nc.Block())

        by_row = nc.dram_tensor("by_row", (4, TILES, P, DIM), F32, kind="Internal").ap()

        def by_head(k, g, part=None):
            pairs = slice(g * PAIRS, (g + 1) * PAIRS) if part is None else slice(g * PAIRS + 4 * part, g * PAIRS + 4 * part + 4)
            return by_row[k, pairs].rearrange("j (r f) n -> (j r) f n", f=HD)

        def window(row, half):
            a = v_h[:, row, half * 256:half * 256 + 256]
            return bass.AP(a.tensor, a.offset, [list(a.ap[0]), [1, WINDOW], [1, 256]])

        def half_of(a, half):
            return a[..., half * 256:half * 256 + 256]

        def by_window(buffer):
            return buffer.rearrange("p a b -> p (a b)").rearrange("p (w t) -> p w t", w=WINDOW)

        @block.sync
        def _(sp):
            sp.dma_start(w_sb[:], w_qkvo).then_inc(w_in, 16)
            sp.dma_start(b_sb[:], b_qkvo).then_inc(w_in, 16)
            sp.dma_start(tg[:], gates).then_inc(w_in, 16)
            sp.dma_start(ident[:], ident_in).then_inc(w_in, 16)

            def store_outputs(g):
                for half in range(2):
                    sp.wait_ge(outputs, 2 * g + half + 1)
                    sp.dma_start(half_of(by_head(3, g), half), half_of(o_h, half)).then_inc(outputs_out, 16)

            for part in range(4):
                sp.dma_start(X[:, 4 * part:4 * part + 4, :],
                             x[4 * part:4 * part + 4].rearrange("t p d -> p t d")).then_inc(x_in[part], 16)
            for g in range(GROUPS):
                for j in range(PAIRS):
                    n, s = g * PAIRS + j, j % 2
                    if n >= 2:
                        sp.wait_ge(qkv_done, 3 * (n - 1))
                    sp.dma_start(cond[:, s, :], ctx[n]).then_inc(cond_in[s], 16)
                if g == 0:
                    sp.wait_ge(pads, 2)
                if g > 0:
                    sp.wait_ge(shifted, 2 * g)
                for part in range(2):
                    for s in range(2):
                        sp.wait_ge(rows_out[s], 16 * (PAIRS // 2 * g + PAIRS // 4 * (part + 1)))
                    sp.dma_start(q_h[64 * part:64 * part + 64, :, :], by_head(0, g, part)).then_inc(keys_in, 16)
                    sp.dma_start(k_h[64 * part:64 * part + 64, :, LEFT:LEFT + DIM], by_head(1, g, part)).then_inc(keys_in, 16)
                if g == 0:
                    sp.wait_ge(staged, 3 * PAIRS)
                    sp.dma_start(by_row[2, 0:PAIRS].rearrange("j p d -> p j d"), v_0).then_inc(values_out, 16)
                    sp.wait_ge(values_out, 16)
                if g > 0:
                    store_outputs(g - 1)
                sp.dma_start(v_h[:, :, LEFT:LEFT + DIM], by_head(2, g)).then_inc(values_in, 16)
            for n in range(TILES):
                if n == TILES - PAIRS:
                    store_outputs(GROUPS - 1)
                if n % PAIRS == 0:
                    sp.wait_ge(outputs_out, 32 * (n // PAIRS + 1))
                if n >= PAIRS:
                    sp.wait_ge(wo_done, n - PAIRS + 1)
                sp.dma_start(back[n % PAIRS], by_row[3, n]).then_inc(back_in[n % PAIRS], 16)

        @block.gpsimd
        def _(pool):
            nc.gpsimd.memset(k_h[:, :, :], 0.0).then_inc(pads, 1)
            nc.gpsimd.memset(v_h[:, :, :], 0.0).then_inc(pads, 1)
            for g in range(GROUPS):
                pool.wait_ge(keys_in, 64 * (g + 1))
                with pool.Fori(0, WINDOW // 4) as i:
                    for s in range(2):
                        if g == 0 and s == 1:
                            pool.wait_ge(values_out, 16)
                        pool.wait_ge(consumed, 2 * i + (s + 16 * g + 1))
                        nc.gpsimd.tensor_tensor(gprod[:, s], q_h[:, :, :],
                                                k_h[:, :, bass.ds(4 * i + (2 * s + 1), DIM)],
                                                ALU.mult).then_inc(multiplied, 1)
                pool.wait_ge(values_in, 16 * (g + 1))
                for j in range(HD):
                    half, d, s = j // 4, j % 4 * 2 + 1, j % 2
                    if j % 4 == 0:
                        pool.wait_ge(exp_done, 2 * g + half + 1)
                    pool.wait_ge(consumed, j + 16 * g + 9)
                    nc.gpsimd.tensor_tensor(by_window(gprod[:, s]), half_of(dots, half), window(d, half),
                                            ALU.mult).then_inc(multiplied, 1)

        @block.scalar
        def _(act):
            act.sem_inc(copied, 2)
            act.wait_ge(w_in, 64)
            nc.scalar.activation(tg[:, :], tg[:, :], ACT.Tanh).then_inc(tanh_done, 1)
            act.wait_ge(var_ready, 1)
            nc.scalar.activation(rstd[:, :], rstd[:, :], ACT.Sqrt).then_inc(std_ready, 1)

            def stage_tile(n, s, v_to=None):
                for k in range(3):
                    act.wait_ge(qkv_done, n * 3 + (k + 1))
                    dst = stage[:, s, k, :] if v_to is None or k < 2 else v_to
                    nc.scalar.activation(dst, qkv_ps[s][k][:, :], ACT.Identity,
                                         bias=b_sb[:, k:k + 1]).then_inc(staged, 1)
                act.wait_ge(staged, n * 3 + 3)

            for n in range(PAIRS):
                s = n % 2
                if n >= 2:
                    act.wait_ge(rows_out[s], 16 * (n // 2))
                stage_tile(n, s, v_0[:, n, :])
                act.dma_start(by_row[0:2, n].rearrange("k p d -> p k d"), stage[:, s, 0:2]).then_inc(rows_out[s], 16)
            for g in range(GROUPS):
                if g > 0:
                    act.wait_ge(outputs, 2 * g)
                with act.Fori(0, WINDOW // 4) as i:
                    for s in range(2):
                        act.wait_ge(consumed, 2 * i + (s + 16 * g + 3))
                        nc.scalar.copy(dots[:, 4 * i + (2 * s + 1), :], sum_ps[s][:, :]).then_inc(copied, 1)
                        if g + 1 < GROUPS:
                            first = (g + 1) * PAIRS + s
                            act.wait_ge(rows_out[s], i * 16 + 16 * (first // 2))
                            stage_tile(2 * i + first, s)
                            act.dma_start(by_row[0:3, bass.ds(2 * i + first, 1)].rearrange("k o p d -> (o p) k d"),
                                          stage[:, s]).then_inc(rows_out[s], 16)
                for half in range(2):
                    act.wait_ge(shifted, 2 * g + half + 1)
                    nc.scalar.activation(half_of(dots, half), half_of(dots, half), ACT.Exp,
                                         scale=HD ** -0.5).then_inc(exp_done, 1)
                if g > 0:
                    act.wait_ge(outputs_out, 32 * g)
                for j in range(HD):
                    act.wait_ge(consumed, 16 * g + 11 + j)
                    nc.scalar.copy(half_of(o_h[:, j % 4 * 2 + 1, :], j // 4), sum_ps[j % 2][:, 0:256]).then_inc(copied, 1)
            for n in range(TILES):
                act.wait_ge(wo_done, n + 1)
                if n >= 2:
                    act.wait_ge(added, n - 1)
                nc.scalar.activation(proj[:, n % 2, :], qkv_ps[n % 2][1][:, :], ACT.Identity,
                                     bias=b_sb[:, 3:4]).then_inc(proj_ready, 1)

        @block.tensor
        def _(pe):
            pe.sem_inc(consumed, 2)
            pe.wait_ge(w_in, 64)

            def project_tile(n, s, pair):
                pe.wait_ge(xn_ready, n + 1)
                pe.wait_ge(cond_in[s], pair * 16 + 16)
                for k, rhs in enumerate((xn[:, s, :], cond[:, s, :], cond[:, s, :])):
                    nc.tensor.matmul(qkv_ps[s][k][:, :], w_sb[:, k, :], rhs, start=True, stop=True)\
                      .then_inc(qkv_done, 1)

            for n in range(PAIRS):
                if n >= 2:
                    pe.wait_ge(staged, 3 * (n - 1))
                project_tile(n, n % 2, n // 2)
            for g in range(GROUPS):
                with pe.Fori(0, WINDOW // 4) as i:
                    for s in range(2):
                        pe.wait_ge(multiplied, 2 * i + (s + 16 * g + 1))
                        pe.wait_ge(copied, 2 * i + (s + 16 * g + 1))
                        for r in range(UNIT):
                            last = nc.tensor.matmul(sum_ps[s][:, :], ident[:, :], gprod[:, s, r, :],
                                                    start=(r == 0), stop=(r == UNIT - 1))
                        last.then_inc(consumed, 1)
                        if g + 1 < GROUPS:
                            first = (g + 1) * PAIRS + s
                            pe.wait_ge(staged, 6 * i + 3 * (first - 1))
                            project_tile(2 * i + first, s, i + first // 2)
                if g + 1 < GROUPS:
                    pe.wait_ge(staged, 3 * PAIRS * (g + 2))

                def job(j):
                    pe.wait_ge(copied, 16 * g + 9 + j)
                    pe.wait_ge(multiplied, 16 * g + 9 + j)
                    for w in range(WINDOW):
                        last = nc.tensor.matmul(sum_ps[j % 2][:, 0:256], ident[:, :], by_window(gprod[:, j % 2])[:, w, :],
                                                start=(w == 0), stop=(w == WINDOW - 1))
                    last.then_inc(consumed, 1)

                for half in range(2):
                    pe.wait_ge(exp_done, 2 * g + half + 1)
                    for w in range(WINDOW):
                        last = nc.tensor.matmul(total_ps[half][:, 0:256], ident[:, :], half_of(dots[:, w, :], half),
                                                start=(w == 0), stop=(w == WINDOW - 1))
                    last.then_inc(total_done, 1)
                    for j in range(4 * half, 4 * half + 4):
                        job(j)
            for n in range(TILES):
                if n >= 2:
                    pe.wait_ge(proj_ready, n - 1)
                pe.wait_ge(back_in[n % PAIRS], 16 * (n // PAIRS + 1))
                nc.tensor.matmul(qkv_ps[n % 2][1][:, :], w_sb[:, 3, :], back[n % PAIRS], start=True, stop=True)\
                  .then_inc(wo_done, 1)

        @block.vector
        def _(dve):
            own = Own(dve, dve_own)
            for t in range(TILES):
                if t % 4 == 0:
                    dve.wait_ge(x_in[t // 4], 16)
                own.mark(nc.vector.bn_stats(bn[:, t, :], X[:, t, :]))
            own.wait()
            for t in range(TILES):
                own.mark(nc.vector.bn_aggr(mv[:, t, :], bn[:, t, :]))
            own.wait()
            deviations(nc, dve, own, mv, rstd, var_ready, std_ready)
            dve.wait_ge(tanh_done, 1)
            for n in range(PAIRS):
                if n >= 2:
                    dve.wait_ge(qkv_done, 3 * (n - 2) + 1)
                normalise(nc, xn[:, n % 2, :], X, n, mv, rstd).then_inc(xn_ready, 1)
            for g in range(GROUPS):
                dve.wait_ge(keys_in, 64 * (g + 1))
                with dve.Fori(0, WINDOW // 4) as i:
                    own.enter(i, 4)
                    for s in range(2):
                        own.done(nc.vector.tensor_tensor(prod[:], q_h[:, :, :], k_h[:, :, bass.ds(4 * i + 2 * s, DIM)],
                                                         ALU.mult))
                        own.done(nc.vector.tensor_reduce(dots[:, 4 * i + 2 * s, :], prod[:].rearrange("p d t -> p t d"),
                                                         AX_X, ALU.add))
                        if g + 1 < GROUPS:
                            n = 2 * i + ((g + 1) * PAIRS + s)
                            dve.wait_ge(qkv_done, 6 * i + (3 * ((g + 1) * PAIRS + s - 2) + 1))
                            nc.vector.tensor_scalar(xn[:, s, :], X[:, bass.ds(n, 1), :].rearrange("p o d -> p (o d)"),
                                                    mv[:, bass.ds(n, 1), 0:1].rearrange("p o d -> p (o d)"),
                                                    rstd[:, bass.ds(n, 1)], ALU.subtract, ALU.mult).then_inc(xn_ready, 1)
                    own.leave(WINDOW // 4)
                dve.wait_ge(copied, 16 * g + 10)
                for half in range(2):
                    own.done(nc.vector.tensor_reduce(half_of(peak, half), half_of(dots, half).rearrange("p w t -> p t w"),
                                                     AX_X, ALU.max))
                    nc.vector.tensor_tensor(half_of(dots, half), half_of(dots, half),
                                            half_of(peak, half).unsqueeze(1).to_broadcast([P, WINDOW, 256]),
                                            ALU.subtract).then_inc(shifted, 1)
                dve.wait_ge(values_in, 16 * (g + 1))
                if g > 0:
                    dve.wait_ge(outputs_out, 32 * g)
                for half in range(2):
                    dve.wait_ge(exp_done, 2 * g + half + 1)
                    for d in range(0, HD, 2):
                        own.done(nc.vector.tensor_tensor(by_window(prod), half_of(dots, half), window(d, half), ALU.mult))
                        own.done(nc.vector.tensor_reduce(half_of(o_h[:, d, :], half),
                                                         by_window(prod).rearrange("p w t -> p t w"), AX_X, ALU.add))
                for half in range(2):
                    dve.wait_ge(total_done, 2 * g + half + 1)
                    own.done(nc.vector.reciprocal(half_of(total, half), total_ps[half][:, 0:256]))
                    dve.wait_ge(copied, 16 * g + 14 + 4 * half)
                    nc.vector.tensor_tensor(half_of(o_h, half), half_of(o_h, half),
                                            half_of(total, half).unsqueeze(1).to_broadcast([P, HD, 256]),
                                            ALU.mult).then_inc(outputs, 1)
            for n in range(TILES):
                dve.wait_ge(proj_ready, n + 1)
                nc.vector.scalar_tensor_tensor(X[:, n, :], proj[:, n % 2, :], tg[:, 0:1], X[:, n, :],
                                               ALU.mult, ALU.add).then_inc(added, 1)
                dve.wait_ge(added, n + 1)
                tile_stats(nc, own, X, bn, mv, n)


def top1_lora(nc, X, route_a, bw, desc_in, tg, ident, bn, mv, rstd, weights, weights_in, ht, ctx_t, ctx_in):
    W = LORA_E + LORA_E * RANK
    stack = ExitStack()
    with stack:
        def sb(name, shape):
            return stack.enter_context(nc.sbuf_tensor(name, shape, F32))

        def sem(name):
            return stack.enter_context(nc.semaphore(name))

        def banks(name):
            return [stack.enter_context(nc.psum_tensor(f"{name}{s}", [P, DIM], F32)) for s in range(2)]

        ra_sb = sb("ra_sb", [P, CH, W])
        bw_sb = sb("bw_sb", [P, DIM])
        desc = sb("desc8", [P, LORA_E])
        xn = sb("xn1", [P, 2, DIM])
        xt = sb("xt1", [P, 2, CH, P])
        wh = sb("wh", [P, 2, P])
        wht = sb("wht", [P, 2, P])
        best, among, first, weight = (sb(n, s) for n, s in (("best", [P, 1]), ("among", [P, LORA_E]),
                                                            ("first", [P, 1]), ("weight", [P, LORA_E])))
        t_ps, h_ps, w_ps, o_ps = banks("t_ps"), banks("h_ps"), banks("w_ps"), banks("o_ps")
        w_in, var_ready, std_ready, dve_own = sem("w1_in"), sem("var1"), sem("std1"), sem("own1")
        xn_ready, turned, xt_ready, h_done = sem("xn1_ready"), sem("turned"), sem("xt_ready"), sem("h_done")
        wh_ready, wh_turned, wht_ready = sem("wh_ready"), sem("wh_turned"), sem("wht_ready")
        o_done, added, stats_done = sem("o_done"), sem("added1"), sem("stats_done")
        block = stack.enter_context(nc.Block())

        @block.sync
        def _(sp):
            sp.dma_start(ra_sb[:], route_a).then_inc(w_in, 16)
            sp.dma_start(bw_sb[:], bw).then_inc(w_in, 16)
            sp.dma_start(desc[:], desc_in).then_inc(w_in, 16)
            for (dst, src), here in zip(weights, weights_in):
                sp.dma_start(dst[:], src).then_inc(here, 16)
            for c in range(CH):
                sp.dma_start(ht[:, c, :, 0, :], ctx_t[0, :, c].rearrange("p (b t) -> p b t", b=OB)).then_inc(ctx_in, 16)

        @block.scalar
        def _(act):
            act.wait_ge(var_ready, 1)
            nc.scalar.activation(rstd[:, :], rstd[:, :], ACT.Sqrt).then_inc(std_ready, 1)
            for n in range(TILES + 2):
                if n < TILES:
                    act.wait_ge(turned, n + 1)
                    if n >= 2:
                        act.wait_ge(h_done, n - 1)
                    nc.scalar.copy(xt[:, n % 2], t_ps[n % 2][:, :]).then_inc(xt_ready, 1)
                if n >= 2:
                    m = n - 2
                    act.wait_ge(wh_turned, m + 1)
                    if m >= 2:
                        act.wait_ge(o_done, m - 1)
                    nc.scalar.copy(wht[:, m % 2], w_ps[m % 2][:, 0:P]).then_inc(wht_ready, 1)

        @block.tensor
        def _(pe):
            pe.wait_ge(w_in, 48)
            for n in range(TILES + 3):
                s = n % 2
                if n < TILES:
                    pe.wait_ge(xn_ready, n + 1)
                    if n >= 2:
                        pe.wait_ge(xt_ready, n - 1)
                    for c in range(CH):
                        last = nc.tensor.transpose(t_ps[s][:, c * P:(c + 1) * P], xn[:, s, c * P:(c + 1) * P], ident[:, :])
                    last.then_inc(turned, 1)
                if 1 <= n <= TILES:
                    m = n - 1
                    pe.wait_ge(xt_ready, m + 1)
                    if m >= 2:
                        pe.wait_ge(wh_ready, m - 1)
                    for c in range(CH):
                        last = nc.tensor.matmul(h_ps[m % 2][:, 0:W], xt[:, m % 2, c, :], ra_sb[:, c, :],
                                                start=(c == 0), stop=(c == CH - 1))
                    last.then_inc(h_done, 1)
                if 2 <= n <= TILES + 1:
                    m = n - 2
                    pe.wait_ge(wh_ready, m + 1)
                    if m >= 2:
                        pe.wait_ge(wht_ready, m - 1)
                    nc.tensor.transpose(w_ps[m % 2][:, 0:P], wh[:, m % 2, :], ident[:, :]).then_inc(wh_turned, 1)
                if n >= 3:
                    m = n - 3
                    pe.wait_ge(wht_ready, m + 1)
                    if m >= 2:
                        pe.wait_ge(added, m - 1)
                    nc.tensor.matmul(o_ps[m % 2][:, :], wht[:, m % 2, :], bw_sb[:, :], start=True, stop=True)\
                      .then_inc(o_done, 1)

        @block.vector
        def _(dve):
            own = Own(dve, dve_own)
            deviations(nc, dve, own, mv, rstd, var_ready, std_ready)
            dve.wait_ge(w_in, 48)
            normalise(nc, xn[:, 0, :], X, 0, mv, rstd).then_inc(xn_ready, 1)
            for n in range(TILES + 4):
                m, routing = n - 1, 1 <= n <= TILES
                if routing:
                    logits = h_ps[m % 2][:, 0:LORA_E]
                    dve.wait_ge(h_done, m + 1)
                    own.mark(nc.vector.tensor_reduce(best[:], logits, AX_X, ALU.max))
                if n + 1 < TILES:
                    if n >= 1:
                        dve.wait_ge(turned, n)
                    normalise(nc, xn[:, (n + 1) % 2, :], X, n + 1, mv, rstd).then_inc(xn_ready, 1)
                if routing:
                    own.wait()
                    own.mark(nc.vector.scalar_tensor_tensor(among[:], logits, best[:, 0:1], desc[:],
                                                            ALU.is_equal, ALU.mult))
                if n >= 4:
                    dve.wait_ge(added, n - 3)
                    nc.vector.bn_stats(bn[:, n - 4, :], X[:, n - 4, :]).then_inc(stats_done, 1)
                if routing:
                    own.wait()
                    own.mark(nc.vector.tensor_reduce(first[:], among[:], AX_X, ALU.max))
                if n >= 4:
                    dve.wait_ge(stats_done, n - 3)
                    nc.vector.bn_aggr(mv[:, n - 4, :], bn[:, n - 4, :])
                if routing:
                    own.wait()
                    own.mark(nc.vector.tensor_scalar(weight[:], among[:], first[:, 0:1], best[:, 0:1],
                                                     ALU.is_equal, ALU.mult))
                if 3 <= n < TILES + 3:
                    k = n - 3
                    dve.wait_ge(o_done, k + 1)
                    nc.vector.scalar_tensor_tensor(X[:, k, :], o_ps[k % 2][:, :], tg[:, 1:2], X[:, k, :],
                                                   ALU.mult, ALU.add).then_inc(added, 1)
                if routing:
                    own.wait()
                    if m >= 2:
                        dve.wait_ge(wh_turned, m - 1)
                    nc.vector.tensor_tensor(wh[:, m % 2, :].rearrange("p (e r) -> p e r", e=LORA_E),
                                            h_ps[m % 2][:, LORA_E:W].rearrange("p (e r) -> p e r", e=LORA_E),
                                            weight[:].unsqueeze(2).to_broadcast([P, LORA_E, RANK]),
                                            ALU.mult).then_inc(wh_ready, 1)


def latent_attention(nc, X, ht, ctx_t, ctx_in, weights, weights_in, tg, ident, bn, mv, rstd):
    stack = ExitStack()
    with stack:
        def sb(name, shape):
            return stack.enter_context(nc.sbuf_tensor(name, shape, F32))

        def sem(name):
            return stack.enter_context(nc.semaphore(name))

        def banks(name):
            return [stack.enter_context(nc.psum_tensor(f"{name}{s}", [P, DIM], F32)) for s in range(2)]

        wk_sb, wv_sb, wq_sb, wo_sb = weights
        wk_in, wv_in, wq_in, wo_in = weights_in
        xn = sb("xn2", [P, 2, DIM])
        kt = sb("kt", [HD1, KV, OB, 2 * TOK])
        v = sb("v", [P, OB, KV * HD1])
        qt = sb("qt", [HD1, 2, OB, G, TOK])
        ot = sb("ot", [P, 2, HC, DIM])
        probs = sb("probs", [P, 3, 2, P])
        probs_t = sb("probs_t", [P, 2, 2 * P])
        npeak = sb("npeak", [P, 3, 2])
        total = sb("total2", [P, 3, 2])
        big_ps, s_ps, p_ps, o_ps = banks("big_ps"), banks("s_ps"), banks("p_ps"), banks("o2_ps")

        UNITS = KV * OB
        uses = [("T", k) for k in range(OT_TILES)] + [("K", k) for k in range(2 * HC)] + [("V", b) for b in range(OB - 4)]
        uses += [("Q", 0, c) for c in range(HC)]
        VALUES_AT, QUERIES_AT = (0, 1, 2, 3), {1: (4, 5, 6), 2: (8, 10, 12), 3: (16, 18, 20)}
        PROJECTIONS_AT = {0: (7, 9, 13, 14), 1: (15, 17, 19, 22), 2: (24, 26, 28, 30), 3: (31, 33, 35)}
        fill = {u: ("V", OB - 4 + k) for k, u in enumerate(VALUES_AT)}
        fill |= {u: ("Q", a, c) for a, units in QUERIES_AT.items() for c, u in enumerate(units)}
        fill |= {u: ("Y", a, k) for a, units in PROJECTIONS_AT.items() for k, u in enumerate(units)}
        uses += [fill[u] for u in sorted(fill)] + [("Y", KV - 1, OT_TILES - 1)]
        at = {use: n for n, use in enumerate(uses)}
        USES = len(uses)

        var_ready, std_ready, dve_own = sem("var2"), sem("std2"), sem("own2")
        xn_ready = sem("xn2_ready")
        big_done = sem("big_done")
        big_free = [sem("big_free0"), sem("big_free1")]
        scored, peaked, exp_done, normed = sem("scored"), sem("peaked"), sem("exp2_done"), sem("normed")
        p_turned, pt_ready, pv_done, o_ready = sem("p_turned"), sem("pt_ready"), sem("pv2_done"), sem("o_ready")
        block = stack.enter_context(nc.Block())

        @block.sync
        def _(sp):
            with sp.Fori(1, OCTETS) as o:
                sp.wait_ge(big_done, o * USES - (USES - at[("V", OB - 1)] - 1))
                for c in range(CH):
                    sp.dma_start(ht[:, c, :, 0, :], ctx_t[bass.ds(o, 1), :, c].rearrange("o p (b t) -> (o p) b t", b=OB))\
                      .then_inc(ctx_in, 16)

        @block.scalar
        def _(act):
            act.wait_ge(var_ready, 1)
            nc.scalar.activation(rstd[:, :], rstd[:, :], ACT.Sqrt).then_inc(std_ready, 1)

            def big(o, use):
                n = at[use]
                act.wait_ge(big_done, o * USES + n + 1)
                return big_ps[n % 2], big_free[n % 2]

            def take_queries(o, a, c):
                ps, free = big(o, ("Q", a, c))
                nc.scalar.activation(qt[:, a % 2, :, c, :], ps[0:HD1, :], ACT.Copy, scale=HD1 ** -0.5)
                nc.scalar.activation(qt[c * PIECE:(c + 1) * PIECE, a % 2, :, HC, :], ps[HD1:P, :], ACT.Copy,
                                     scale=HD1 ** -0.5).then_inc(free, 1)

            with act.Fori(0, OCTETS) as o:
                for k in range(OT_TILES):
                    ps, free = big(o, ("T", k))
                    nc.scalar.copy(ht[:, :, 2 * k:2 * k + 2, 1, :], ps[:, :].rearrange("p (c b t) -> p c b t", c=CH, b=2)).then_inc(free, 1)
                for k in range(2 * HC):
                    ps, free = big(o, ("K", k))
                    c, half = k // 2, slice(k % 2 * 4, k % 2 * 4 + 4)
                    nc.scalar.copy(kt[:, c, half, :], ps[0:HD1, :])
                    nc.scalar.copy(kt[c * PIECE:(c + 1) * PIECE, HC, half, :], ps[HD1:P, :]).then_inc(free, 1)
                for c in range(HC):
                    take_queries(o, 0, c)
                for u in range(UNITS + 3):
                    if u < UNITS:
                        act.wait_ge(peaked, o * UNITS + u + 1)
                        if u >= 3:
                            act.wait_ge(p_turned, o * UNITS + u - 2)
                        for g2 in range(2):
                            nc.scalar.activation(probs[:, u % 3, g2, :], s_ps[u % 2][:, g2 * P:(g2 + 1) * P], ACT.Exp,
                                                 bias=npeak[:, u % 3, g2:g2 + 1],
                                                 accum_out=total[:, u % 3, g2:g2 + 1]).then_inc(exp_done, 1)
                    if u >= 3:
                        w = u - 3
                        act.wait_ge(p_turned, o * UNITS + w + 1)
                        if w >= 2:
                            act.wait_ge(pv_done, o * UNITS + w - 1)
                        nc.scalar.copy(probs_t[:, w % 2, :], p_ps[w % 2][:, 0:2 * P]).then_inc(pt_ready, 1)
                    if fill.get(u, "Y")[0] == "Q":
                        take_queries(o, *fill[u][1:])

        @block.tensor
        def _(pe):
            pe.sem_inc(big_free[0], 1)
            pe.sem_inc(big_free[1], 1)

            def big(o, use):
                n = at[use]
                pe.wait_ge(big_free[n % 2], o * (USES // 2) + (n // 2 + 1))
                return big_ps[n % 2]

            def values(o, b):
                pe.wait_ge(wv_in, 16)
                ps = big(o, ("V", b))
                for c in range(CH):
                    last = nc.tensor.matmul(ps[:, 0:KV * HD1], ht[:, c, b], wv_sb[:, c, :],
                                            start=(c == 0), stop=(c == CH - 1))
                last.then_inc(big_done, 1)

            def queries(o, a, k):
                pe.wait_ge(wq_in, 16)
                ps = big(o, ("Q", a, k))
                for c in range(CH):
                    last = nc.tensor.matmul(ps[:, :], wq_sb[:, c, (a * HC + k) * P:(a * HC + k + 1) * P], ht[:, c, :, 1, :],
                                            start=(c == 0), stop=(c == CH - 1))
                last.then_inc(big_done, 1)

            def project(o, a, k):
                pe.wait_ge(o_ready, o * UNITS + (OB * a + 2 * k + 2))
                pe.wait_ge(wo_in, 16)
                ps = big(o, ("Y", a, k))
                for c in range(HC):
                    last = nc.tensor.matmul(ps[:, :], ot[:, a % 2, c, k * P:(k + 1) * P], wo_sb[:, a * HC + c, :],
                                            start=(c == 0), stop=(c == HC - 1))
                last.then_inc(big_done, 1)

            with pe.Fori(0, OCTETS) as o:
                for k in range(OT_TILES):
                    pe.wait_ge(xn_ready, o * OT_TILES + k + 1)
                    ps = big(o, ("T", k))
                    for c in range(CH):
                        last = nc.tensor.transpose(ps[:, c * P:(c + 1) * P], xn[:, k % 2, c * P:(c + 1) * P], ident[:, :])
                    last.then_inc(big_done, 1)
                pe.wait_ge(ctx_in, o * (16 * CH) + 16 * CH)
                pe.wait_ge(wk_in, 16)
                for k in range(2 * HC):
                    ps = big(o, ("K", k))
                    if k == 1:
                        pe.wait_ge(big_free[1], o * (USES // 2) + 3)
                    for c in range(CH):
                        last = nc.tensor.matmul(ps[:, :], wk_sb[:, c, k // 2 * P:(k // 2 + 1) * P],
                                                ht[:, c, k % 2 * 4:k % 2 * 4 + 4], start=(c == 0), stop=(c == CH - 1))
                    last.then_inc(big_done, 1)
                for b in range(OB - 4):
                    values(o, b)
                for c in range(HC):
                    queries(o, 0, c)
                for u in range(UNITS + 4):
                    a, b = u // OB, u % OB
                    if u < UNITS:
                        if b == 0:
                            first = at[("Q", a, HC - 2)], at[("Q", a, HC - 1)]
                            for n in first:
                                pe.wait_ge(big_free[n % 2], o * (USES // 2) + n // 2 + 2)
                        if u >= 2:
                            pe.wait_ge(exp_done, o * (2 * UNITS) + 2 * (u - 1))
                        for g2 in range(2):
                            last = nc.tensor.matmul(s_ps[u % 2][:, g2 * P:(g2 + 1) * P],
                                                    qt[:, a % 2, b, 2 * g2:2 * g2 + 2],
                                                    kt[:, a, b], start=True, stop=True)
                        last.then_inc(scored, 1)
                    if u in fill:
                        {"V": values, "Q": queries, "Y": project}[fill[u][0]](o, *fill[u][1:])
                    if u >= 3 and u - 3 < UNITS:
                        w = u - 3
                        pe.wait_ge(normed, o * UNITS + w + 1)
                        if w >= 2:
                            pe.wait_ge(pt_ready, o * UNITS + w - 1)
                        for g2 in range(2):
                            last = nc.tensor.transpose(p_ps[w % 2][:, g2 * P:(g2 + 1) * P], probs[:, w % 3, g2, :], ident[:, :])
                        last.then_inc(p_turned, 1)
                    if u >= 4:
                        w = u - 4
                        pe.wait_ge(pt_ready, o * UNITS + w + 1)
                        if w >= 2:
                            pe.wait_ge(o_ready, o * UNITS + w - 1)
                        nc.tensor.matmul(o_ps[w % 2][0:HD1, 0:2 * P], v[:, w % OB, w // OB * HD1:(w // OB + 1) * HD1],
                                         probs_t[:, w % 2, :], start=True, stop=True).then_inc(pv_done, 1)
                project(o, KV - 1, OT_TILES - 1)

        @block.vector
        def _(dve):
            own = Own(dve, dve_own)
            deviations(nc, dve, own, mv, rstd, var_ready, std_ready)

            def big(o, use):
                n = at[use]
                dve.wait_ge(big_done, o * USES + n + 1)
                return big_ps[n % 2], big_free[n % 2]

            def take_values(o, b):
                ps, free = big(o, ("V", b))
                nc.vector.tensor_copy(v[:, b, :], ps[:, 0:KV * HD1]).then_inc(free, 1)

            def add(o, a, k):
                ps, free = big(o, ("Y", a, k))
                row = X[:, bass.ds(o * OT_TILES + k, 1), :].rearrange("p o d -> p (o d)")
                nc.vector.scalar_tensor_tensor(row, ps[:, :], tg[:, 2:3], row, ALU.mult, ALU.add).then_inc(free, 1)

            with dve.Fori(0, OCTETS) as o:
                own.enter(o, UNITS + OT_TILES)
                for k in range(OT_TILES):
                    if k >= 2:
                        dve.wait_ge(big_done, o * USES + k - 1)
                    t = o * OT_TILES + k
                    nc.vector.tensor_scalar(xn[:, k % 2, :], X[:, bass.ds(t, 1), :].rearrange("p o d -> p (o d)"),
                                            mv[:, bass.ds(t, 1), 0:1].rearrange("p o d -> p (o d)"),
                                            rstd[:, bass.ds(t, 1)], ALU.subtract, ALU.mult).then_inc(xn_ready, 1)
                for b in range(OB - 4):
                    take_values(o, b)
                for u in range(UNITS + 4):
                    if u < UNITS:
                        dve.wait_ge(scored, o * UNITS + u + 1)
                        nc.vector.tensor_reduce(npeak[:, u % 3, :], s_ps[u % 2][:, 0:2 * P].rearrange("p (g s) -> p g s", g=2),
                                                AX_X, ALU.max, negate=True).then_inc(peaked, 1)
                    if 1 <= u <= UNITS:
                        w = u - 1
                        dve.wait_ge(exp_done, o * (2 * UNITS) + 2 * (w + 1))
                        own.done(nc.vector.reciprocal(total[:, w % 3, :], total[:, w % 3, :]))
                        nc.vector.tensor_tensor(probs[:, w % 3], probs[:, w % 3],
                                                total[:, w % 3, :].unsqueeze(2).to_broadcast([P, 2, P]),
                                                ALU.mult).then_inc(normed, 1)
                    if fill.get(u, "Q")[0] == "Y":
                        add(o, *fill[u][1:])
                    if fill.get(u, "Q")[0] == "V":
                        take_values(o, *fill[u][1:])
                    if u >= 4:
                        w = u - 4
                        a, b = w // OB, w % OB
                        dve.wait_ge(pv_done, o * UNITS + w + 1)
                        if b == 0 and a >= 2:
                            dve.wait_ge(big_done, o * USES + at[("Y", a - 2, OT_TILES - 1)] + 1)
                        heads = o_ps[w % 2][:, 0:2 * P].rearrange("p (g q) -> p g q", g=G)
                        t = slice(b * TOK, (b + 1) * TOK)
                        nc.vector.tensor_copy(ot[0:HD1, a % 2, :, t], heads[0:HD1, 0:HC])
                        for c in range(HC):
                            last = nc.vector.tensor_copy(ot[HD1:P, a % 2, c, t], heads[c * PIECE:(c + 1) * PIECE, HC])
                        last.then_inc(o_ready, 1)
                for k in range(OT_TILES):
                    if k == OT_TILES - 1:
                        add(o, KV - 1, k)
                    n, t = at[("Y", KV - 1, k)], o * OT_TILES + k
                    dve.wait_ge(big_free[n % 2], o * (USES // 2) + n // 2 + 2)
                    own.mark(nc.vector.bn_stats(bn[:, bass.ds(t, 1), :].rearrange("p o d -> p (o d)"),
                                                X[:, bass.ds(t, 1), :].rearrange("p o d -> p (o d)")))
                own.leave(OCTETS)
            own.wait()
            for t in range(TILES):
                own.mark(nc.vector.bn_aggr(mv[:, t, :], bn[:, t, :]))


def route(nc, X, tg, ident, bn, mv, rstd, wr, te, slot_of, tok_of, gs, xn_rows, table, rw, rows, tri_in, tok_ids, wr_in, w_s, b3, xt, b_sb, b_in, b_here):
    stack = ExitStack()
    with stack:
        def sb(name, shape, dtype=F32):
            return stack.enter_context(nc.sbuf_tensor(name, shape, dtype))

        def sem(name):
            return stack.enter_context(nc.semaphore(name))

        def banks(name, n=2):
            return [stack.enter_context(nc.psum_tensor(f"{name}{s}", [P, DIM], F32)) for s in range(n)]

        T, E, GS = TILES, E1, E1 // EGROUPS
        STEPS = SHARED * OCTETS
        GATES_FROM = STEPS - OCTETS
        COUNT_AT = 3
        rw_sb = sb("rw_sb", [P, CH, E])
        rows_sb = sb("rows_sb", [P, ROWS])
        row, at = {}, 0
        for name, n in ROW_PARTS:
            row[name] = rows_sb[:, at:at + n]
            at += n
        tri = sb("tri", [P, P])
        ones = sb("ones", [P, P])
        tab_sb = sb("tab_sb", [MAX_TILES, P])
        ids = sb("ids", [P, T])
        w_sb = sb("w_sb", [P, SHARED, W_COLS])
        w12_sb = w_sb[:, :, 0:W3].rearrange("p s (c k n) -> p s c k n", c=CH, k=2)
        b3_sb = sb("b3_sb", [E + 1, DIM])
        act_sb, h_sb = sb("act_sb", [P, 2, DIM]), sb("h_sb", [P, 2, DIM])
        xn_0 = sb("xn3", [P, 2, DIM])
        xn = [xn_0[:, 0, :], xn_0[:, 1, :], h_sb[:, 0, :], h_sb[:, 1, :]]
        gates = sb("gates", [P, T, E + 1])
        gt = sb("gt", [E + 1, DIM])
        scores, work, among, best1, best2, left, pos = (
            sb(n, [P, T, E]) for n in ("scores", "work", "among3", "best1", "best2", "left", "pos"))
        top, gtop, gwork, gamong, keep = (sb("top3", [P, T]), sb("gtop", [P, T, EGROUPS]), sb("gwork", [P, T, EGROUPS]),
                                          sb("gamong", [P, T, EGROUPS]), sb("keep", [P, T, EGROUPS]))
        before = sb("before", [P, T + 1, E])
        square = sb("square", [P, E, E])
        tiles_of, ends, starts = sb("tiles_of", [P, E]), sb("ends", [P, E]), sb("starts", [P, E])
        te_f = sb("te_f", [1, MAX_TILES])
        te_work = sb("te_work", [1, MAX_TILES, E])
        def item(k, j):
            return 4 * k + j + max(0, k - GATES_FROM + 1)

        a_ps, b_ps, y_ps, count_ps = banks("a_ps"), banks("b_ps"), banks("y_ps", 3), banks("count_ps", 1)[0]
        t_ps, lt_ps, l_ps = a_ps, b_ps, y_ps
        lt_sb = act_sb[0:E]
        prefix_ps, total_ps, tab_ps = count_ps[:, 0:T * E], count_ps[:, T * E:2 * T * E], count_ps[:, 0:MAX_TILES]

        w_in, ids_in, ws_in = sem("w3_in"), sem("ids_in"), sem("ws_in")
        var_ready, std_ready, dve_own = sem("var3"), sem("std3"), sem("own3")
        xn_ready, rows_out = sem("xn3_ready"), [sem(f"xn_rows_out{k}") for k in range(4)]
        turned, xt_ready, wr_here = sem("turned3"), sem("xt3_ready"), sem("wr_here")
        lt_done, lt_ready = sem("lt_done"), sem("lt_ready")
        logits_done, logits_out, shifted, exp_done = sem("logits_done"), sem("logits_out"), sem("shifted3"), sem("exp3")
        ones_ready, picks_ready, counted, gates_ready = sem("ones_ready"), sem("picks_ready"), sem("counted"), sem("gates_ready")
        zeroed, slots_ready, scattered, tab_in = sem("zeroed"), sem("slots_ready"), sem("scattered"), sem("tab_in")
        tab_turned, gates_turned, gt_ready = sem("tab_turned"), sem("gates_turned"), sem("gt_ready")
        up_done, silu_done, h_ready, y_done, added = sem("up_done"), sem("silu_done"), sem("h_ready"), sem("y_done"), sem("added3")
        block = stack.enter_context(nc.Block())

        @block.sync
        def _(sp):
            for dst, src in ((rw_sb, rw), (rows_sb, rows), (tri, tri_in), (b3_sb, b3)):
                sp.dma_start(dst[:], src).then_inc(w_in, 16)
            sp.dma_start(ids[:], tok_ids).then_inc(ids_in, 16)
            sp.wait_ge(ones_ready, 1)
            sp.dma_start(table.rearrange("(i p) o -> i (p o)", p=P), tab_sb[:]).then_inc(zeroed, 16)
            sp.dma_start(w_sb[:], w_s).then_inc(ws_in, 16)
            for n in range(T):
                sp.wait_ge(xn_ready, n + 1)
                sp.dma_start(xn_rows[n * P:(n + 1) * P, :], xn[n % 4]).then_inc(rows_out[n % 4], 16)
            for k in range(4):
                sp.wait_ge(rows_out[k], 16 * (T // 4))
            sp.wait_ge(scattered, 16 * 2 * T)
            sp.dma_start(tab_sb[:], table.rearrange("(i p) o -> i (p o)", p=P)).then_inc(tab_in, 16)
            sp.wait_ge(up_done, 2 * STEPS)
            sp.dma_start(b_sb, b_in).then_inc(b_here, 16)

        @block.gpsimd
        def _(pool):
            pool.wait_ge(zeroed, 16)
            pool.wait_ge(ids_in, 16)
            for k in range(2):
                pool.wait_ge(slots_ready, k + 1)
                for n in range(T):
                    nc.gpsimd.indirect_dma_start(
                        table, bass.IndirectOffsetOnAxis(ap=slot_of[:, k, n:n + 1], axis=0), ids[:, n:n + 1], None)\
                        .then_inc(scattered, 16)

        @block.scalar
        def _(act):
            act.wait_ge(var_ready, 1)
            nc.scalar.activation(rstd[:, :], rstd[:, :], ACT.Sqrt).then_inc(std_ready, 1)
            for n in range(T + 1):
                if n < T:
                    act.wait_ge(turned, n + 1)
                    nc.scalar.copy(xt[:, :, n * P:(n + 1) * P], t_ps[n % 2][:, :].rearrange("p (c t) -> p c t", c=CH))\
                      .then_inc(xt_ready, 1)
                if n >= 4 and n % 4 == 0:
                    q = n // 4 - 1
                    act.wait_ge(lt_done, q + 1)
                    if q >= 2:
                        act.wait_ge(logits_done, q - 1)
                    nc.scalar.copy(lt_sb[:, q % 2, :], lt_ps[q % 2][0:E, :]).then_inc(lt_ready, 1)
            for part in range(4):
                act.dma_start(wr[:, 4 * part:4 * part + 4, :], wr_in[4 * part:4 * part + 4].rearrange("e p n -> p e n"))\
                   .then_inc(wr_here, 16)
            act.wait_ge(shifted, 1)
            nc.scalar.activation(work[:], work[:], ACT.Exp).then_inc(exp_done, 1)
            for k in range(STEPS):
                act.wait_ge(up_done, 2 * k + 1)
                if k >= 2:
                    act.wait_ge(h_ready, k - 1)
                nc.scalar.activation(act_sb[:, k % 2, :], a_ps[k % 2][:, :], ACT.Silu,
                                     bias=w_sb[:, k // OCTETS, B1:B1 + 1]).then_inc(silu_done, 1)
                q = k - GATES_FROM
                if q >= 0:
                    act.wait_ge(gates_turned, q + 1)
                    if q >= 1:
                        act.wait_ge(y_done, 4 * k)
                    nc.scalar.copy(gt[:, :], y_ps[item(k, -1) % 3][0:E + 1, :]).then_inc(gt_ready, 1)

        @block.tensor
        def _(pe):
            pe.wait_ge(w_in, 64)
            for n in range(T + 2):
                s = n % 2
                if n < T:
                    pe.wait_ge(xn_ready, n + 1)
                    if n >= 2:
                        pe.wait_ge(xt_ready, n - 1)
                    for c in range(CH):
                        last = nc.tensor.transpose(t_ps[s][:, c * P:(c + 1) * P], xn[n % 4][:, c * P:(c + 1) * P], ident[:, :])
                    last.then_inc(turned, 1)
                if n >= 4 and n % 4 == 0:
                    q = n // 4 - 1
                    pe.wait_ge(xt_ready, 4 * q + 4)
                    if q >= 2:
                        pe.wait_ge(lt_ready, q - 1)
                    for c in range(CH):
                        last = nc.tensor.matmul(lt_ps[q % 2][0:E, :], rw_sb[:, c, :], xt[:, c, q * DIM:(q + 1) * DIM],
                                                start=(c == 0), stop=(c == CH - 1))
                    last.then_inc(lt_done, 1)
                if n >= 5 and n % 4 == 1:
                    q = n // 4 - 1
                    pe.wait_ge(lt_ready, q + 1)
                    if q >= 2:
                        pe.wait_ge(logits_out, q - 1)
                    for j in range(4):
                        last = nc.tensor.transpose(l_ps[q % 2][:, j * E:(j + 1) * E], lt_sb[:, q % 2, j * P:(j + 1) * P],
                                                   ident[0:E, 0:E])
                    last.then_inc(logits_done, 1)
            pe.wait_ge(ws_in, 16)

            def up(k):
                s, q = k // OCTETS, k % OCTETS
                if k >= 2:
                    pe.wait_ge(h_ready, k - 1)
                for half, banks_of in enumerate((a_ps, b_ps)):
                    for c in range(CH):
                        last = nc.tensor.matmul(banks_of[k % 2][:, :], w12_sb[:, s, c, half, :],
                                                xt[:, c, q * DIM:(q + 1) * DIM], start=(c == 0), stop=(c == CH - 1))
                    last.then_inc(up_done, 1)

            up(0)
            for k in range(STEPS):
                if k + 1 < STEPS:
                    up(k + 1)
                if k == COUNT_AT:
                    pe.wait_ge(picks_ready, 1)
                    flat = among[:].rearrange("p t e -> p (t e)")
                    nc.tensor.matmul(prefix_ps, tri[:, :], flat, start=True, stop=True).then_inc(counted, 1)
                    nc.tensor.matmul(total_ps, ones[:, :], flat, start=True, stop=True).then_inc(counted, 1)
                q = k - GATES_FROM
                if q == 0:
                    pe.wait_ge(gates_ready, 1)
                if q >= 0:
                    pe.wait_ge(added, 4 * k - 2)
                    for j in range(4):
                        last = nc.tensor.transpose(y_ps[item(k, -1) % 3][0:E + 1, j * P:(j + 1) * P],
                                                   gates[:, 4 * q + j, :], ident[:, :])
                    last.then_inc(gates_turned, 1)
                pe.wait_ge(h_ready, k + 1)
                if k == 0:
                    pe.wait_ge(logits_out, T // 4)
                for j in range(4):
                    y = y_ps[item(k, j) % 3][:, :]
                    before_it = 4 * k + j + 1 - (3 if q < 0 or j == 3 else 2)
                    if before_it >= 1:
                        pe.wait_ge(added, before_it)
                    if q >= 0 and j == 0:
                        pe.wait_ge(gt_ready, q + 1)
                    last = nc.tensor.matmul(y, h_sb[:, k % 2, j * P:(j + 1) * P], w_sb[:, k // OCTETS, W3:B1],
                                            start=True, stop=(q < 0))
                    if q >= 0:
                        last = nc.tensor.matmul(y, gt[:, j * P:(j + 1) * P], b3_sb[:, :], start=False, stop=True)
                    last.then_inc(y_done, 1)
            pe.wait_ge(slots_ready, 2)
            pe.wait_ge(tab_in, 16)
            nc.tensor.transpose(tab_ps, tab_sb[:, :], ident[0:MAX_TILES, 0:MAX_TILES]).then_inc(tab_turned, 1)
            pe.wait_ge(wr_here, 64)

        @block.vector
        def _(dve):
            own = Own(dve, dve_own)
            V = nc.vector

            def over(a, n):
                return a.unsqueeze(2).to_broadcast([P, a.shape[1], n])

            def hidden(k):
                dve.wait_ge(silu_done, k + 1)
                dve.wait_ge(up_done, 2 * k + 2)
                if k >= 2:
                    dve.wait_ge(y_done, 4 * (k - 1))
                V.scalar_tensor_tensor(h_sb[:, k % 2, :], b_ps[k % 2][:, :], w_sb[:, k // OCTETS, B2:B2 + 1],
                                       act_sb[:, k % 2, :], ALU.add, ALU.mult).then_inc(h_ready, 1)

            def add(k):
                for j in range(4):
                    tile = k % OCTETS * 4 + j
                    dve.wait_ge(y_done, 4 * k + j + 1)
                    V.scalar_tensor_tensor(X[:, tile, :], y_ps[item(k, j) % 3][:, :], tg[:, 3:4], X[:, tile, :], ALU.mult, ALU.add)\
                     .then_inc(added, 1)

            def pick(out, values, mark, best, order, n):
                own.done(V.tensor_reduce(best, values, AX_X, ALU.max))
                own.done(V.tensor_tensor(mark, values, over(best, n), ALU.is_equal))
                own.done(V.tensor_tensor(mark, mark, order.unsqueeze(1).to_broadcast([P, T, n]), ALU.mult))
                own.done(V.tensor_reduce(best, mark, AX_X, ALU.max))
                own.done(V.tensor_tensor(out, mark, over(best, n), ALU.is_equal))

            own.mark(V.memset(gates[:], 1.0))
            own.mark(V.memset(ones[:], 1.0))
            own.mark(V.memset(before[:, 0, :], 0.0))
            V.memset(tab_sb[:], 0.0).then_inc(ones_ready, 1)
            deviations(nc, dve, own, mv, rstd, var_ready, std_ready)
            dve.wait_ge(w_in, 64)
            normalise(nc, xn[0], X, 0, mv, rstd).then_inc(xn_ready, 1)
            for n in range(T + 1):
                if n + 1 < T:
                    k = n + 1
                    if k >= 4:
                        dve.wait_ge(turned, k - 3)
                        dve.wait_ge(rows_out[k % 4], 16 * (k // 4))
                    normalise(nc, xn[k % 4], X, k, mv, rstd).then_inc(xn_ready, 1)
                if n >= 6 and (n % 4 == 2 or n == T):
                    q = (n + 1) // 4 - 1
                    dve.wait_ge(logits_done, q + 1)
                    V.tensor_tensor(work[:, 4 * q:4 * q + 4, :], l_ps[q % 2][:, 0:4 * E].rearrange("p (t e) -> p t e", e=E),
                                    row["router_b"].unsqueeze(1).to_broadcast([P, 4, E]), ALU.add).then_inc(logits_out, 1)
            dve.wait_ge(logits_out, T // 4)
            for k in (2, 3):
                dve.wait_ge(rows_out[k], 16 * (T // 4))
            own.done(V.tensor_reduce(top[:], work[:], AX_X, ALU.max))
            V.tensor_tensor(work[:], work[:], over(top[:], E), ALU.subtract).then_inc(shifted, 1)
            dve.wait_ge(exp_done, 1)
            own.done(V.tensor_reduce(top[:], work[:], AX_X, ALU.add))
            own.done(V.reciprocal(top[:], top[:]))
            own.done(V.tensor_tensor(work[:], work[:], over(top[:], E), ALU.mult))
            own.done(V.tensor_tensor(scores[:], work[:], row["router_bias"].unsqueeze(1).to_broadcast([P, T, E]), ALU.add))
            own.done(V.tensor_reduce(gwork[:], scores[:].rearrange("p t (g e) -> p t g e", g=EGROUPS), AX_X, ALU.max))
            hidden(0)
            pick(keep[:], gwork[:], gamong[:], top[:], row["order_g"], EGROUPS)
            own.done(V.scalar_tensor_tensor(gwork[:], keep[:], -1e30, gwork[:], ALU.mult, ALU.add))
            pick(gtop[:], gwork[:], gamong[:], top[:], row["order_g"], EGROUPS)
            own.done(V.tensor_tensor(keep[:], keep[:], gtop[:], ALU.add))
            hidden(1)
            own.done(V.tensor_scalar(gwork[:], keep[:], 1.0, 1e30, ALU.subtract, ALU.mult))
            four = lambda a: a.rearrange("p t (g e) -> p (t g) e", g=EGROUPS)
            flat = lambda a: over(a.rearrange("p t g -> p (t g)"), GS)
            own.done(V.tensor_tensor(four(left[:]), four(scores[:]), flat(keep[:]), ALU.mult))
            own.done(V.tensor_tensor(four(left[:]), four(left[:]), flat(gwork[:]), ALU.add))
            add(0)
            pick(best1[:], left[:], among[:], top[:], row["order"], E)
            hidden(2)
            own.done(V.scalar_tensor_tensor(left[:], best1[:], -2e30, left[:], ALU.mult, ALU.add))
            pick(best2[:], left[:], among[:], top[:], row["order"], E)
            V.tensor_tensor(among[:], best1[:], best2[:], ALU.add).then_inc(picks_ready, 1)
            add(1)
            hidden(3)
            add(2)
            dve.wait_ge(picks_ready, 1)
            V.tensor_tensor(gates[:, :, 0:E], among[:], scores[:], ALU.mult).then_inc(gates_ready, 1)
            for k, best in enumerate((best1, best2)):
                own.done(V.tensor_tensor(work[:], best[:], scores[:], ALU.mult))
                own.done(V.tensor_reduce(top[:], work[:], AX_X, ALU.add))
                own.done(V.tensor_scalar(gs[:, k, :], top[:], tg[:, 3:4], None, ALU.mult))
            dve.wait_ge(counted, 2)
            for t in range(T):
                own.done(V.tensor_tensor(before[:, t + 1, :], total_ps[:, t * E:(t + 1) * E], before[:, t, :], ALU.add))
            hidden(4)
            add(3)
            own.done(V.tensor_tensor(square[:], over(before[:, T, :], E), row["steps"].unsqueeze(1).to_broadcast([P, E, E]),
                                     ALU.is_gt))
            own.done(V.tensor_reduce(tiles_of[:], square[:], AX_X, ALU.add))
            own.done(V.tensor_tensor(square[:], row["upto"].rearrange("p (a b) -> p a b", a=E),
                                     tiles_of[:].unsqueeze(1).to_broadcast([P, E, E]), ALU.mult))
            own.done(V.tensor_reduce(ends[:], square[:], AX_X, ALU.add))
            own.done(V.tensor_tensor(starts[:], ends[:], tiles_of[:], ALU.subtract))
            own.done(V.tensor_tensor(pos[:].rearrange("p t e -> p (t e)"), prefix_ps,
                                     before[:, 0:T, :].rearrange("p t e -> p (t e)"), ALU.add))
            own.done(V.scalar_tensor_tensor(pos[:], starts[:].unsqueeze(1).to_broadcast([P, T, E]), float(P), pos[:],
                                            ALU.mult, ALU.add))
            for k, best in enumerate((best1, best2)):
                own.done(V.tensor_tensor(work[:], best[:], pos[:], ALU.mult))
                own.done(V.tensor_reduce(top[:], work[:], AX_X, ALU.add))
                V.tensor_copy(slot_of[:, k, :], top[:]).then_inc(slots_ready, 1)
                dve.wait_ge(slots_ready, k + 1)
            own.done(V.tensor_tensor(te_work[:], ends[0:1, :].unsqueeze(1).to_broadcast([1, MAX_TILES, E]),
                                     row["tile"][0:1, :].unsqueeze(2).to_broadcast([1, MAX_TILES, E]), ALU.is_le))
            own.done(V.tensor_reduce(te_f[:], te_work[:], AX_X, ALU.add))
            own.done(V.tensor_scalar(te[:], te_f[:], float(E - 1), None, ALU.min))
            for k in range(5, STEPS):
                hidden(k)
                add(k - 1)
            add(STEPS - 1)
            dve.wait_ge(tab_turned, 1)
            own.mark(V.tensor_copy(tok_of[:], tab_ps))


def routed(nc, X, out, ident, wr, te, slot_of, tok_of, gs, xn_rows, y_rows, b_sb, b_here):
    stack = ExitStack()
    with stack:
        def sb(name, shape):
            return stack.enter_context(nc.sbuf_tensor(name, shape, F32))

        def sem(name):
            return stack.enter_context(nc.semaphore(name))

        def banks(name):
            return [stack.enter_context(nc.psum_tensor(f"{name}{s}", [P, DIM], F32)) for s in range(2)]

        DEEP = 4
        xg = sb("xg", [P, DEEP, DIM])
        xgt = sb("xgt", [P, 2, CH, P])
        up_sb, silu_sb, h_sb = sb("up_sb", [P, 2, 2 * INTER]), sb("silu_sb", [P, 2, INTER]), sb("h5_sb", [P, 2, INTER])
        ht_sb = sb("ht5_sb", [P, 2, P])
        y_sb = sb("y_sb", [P, 4, DIM])
        back = sb("back5", [P, 4, DIM])
        t_ps, u_ps, ht_ps, y_ps = banks("t5_ps"), banks("u5_ps"), banks("ht5_ps"), banks("y5_ps")
        gathered = [sem(f"gathered{s}") for s in range(DEEP)]
        turned, xgt_ready, up_done, biased, silu_done = sem("turned5"), sem("xgt_ready"), sem("up5_done"), sem("biased"), sem("silu5")
        h_ready, h_turned, ht_ready, down_done, y_ready = sem("h5_ready"), sem("h5_turned"), sem("ht5_ready"), sem("down_done"), sem("y5_ready")
        y_out = [sem(f"y_out{s}") for s in range(4)]
        backed = [sem(f"backed{s}") for s in range(4)]
        combined, stored = sem("combined"), sem("stored")
        block = stack.enter_context(nc.Block())

        def in_steps(engine, step):
            for i in range(8):
                step(i, i)
            with engine.Fori(2, MAX_TILES // 4) as r:
                for j in range(4):
                    step(r * 4 + j, 8 + j)
            for i in range(MAX_TILES, MAX_TILES + 3):
                step(i, i)

        @block.sync
        def _(sp):
            with sp.Fori(0, MAX_TILES // 4) as r:
                for s in range(4):
                    sp.wait_ge(y_ready, r * 4 + s + 1)
                    sp.dma_start(y_rows[bass.ds((r * 4 + s) * P, P), :], y_sb[:, s, :]).then_inc(y_out[s], 16)
            for n in range(TILES):
                sp.wait_ge(combined, 2 * n + 2)
                sp.dma_start(out[n], X[:, n, :]).then_inc(stored, 16)
            sp.wait_ge(stored, 16 * TILES)

        @block.gpsimd
        def _(pool):
            for i in range(MAX_TILES):
                if i >= DEEP:
                    pool.wait_ge(turned, i - DEEP + 1)
                nc.gpsimd.indirect_dma_start(xg[:, i % DEEP, :], None, xn_rows,
                                             bass.IndirectOffsetOnAxis(ap=tok_of[:, i:i + 1], axis=0))\
                    .then_inc(gathered[i % DEEP], 16)
            for s in range(4):
                pool.wait_ge(y_out[s], 16 * (MAX_TILES // 4))
            for m in range(2 * TILES):
                n, k = m // 2, m % 2
                if m >= 4:
                    pool.wait_ge(combined, m - 3)
                nc.gpsimd.indirect_dma_start(back[:, m % 4, :], None, y_rows,
                                             bass.IndirectOffsetOnAxis(ap=slot_of[:, k, n:n + 1], axis=0))\
                    .then_inc(backed[m % 4], 16)

        @block.scalar
        def _(act):
            def step(i, n):
                if n < MAX_TILES:
                    act.wait_ge(turned, i + 1)
                    if n >= 2:
                        act.wait_ge(up_done, i - 1)
                    nc.scalar.copy(xgt[:, n % 2], t_ps[n % 2][:, :]).then_inc(xgt_ready, 1)
                if 1 <= n <= MAX_TILES:
                    m = n - 1
                    act.wait_ge(biased, i)
                    if m >= 2:
                        act.wait_ge(h_ready, i - 2)
                    nc.scalar.activation(silu_sb[:, m % 2, :], up_sb[:, m % 2, 0:INTER], ACT.Silu).then_inc(silu_done, 1)
                if 2 <= n <= MAX_TILES + 1:
                    m = n - 2
                    act.wait_ge(h_turned, i - 1)
                    if m >= 2:
                        act.wait_ge(down_done, i - 3)
                    nc.scalar.copy(ht_sb[:, m % 2, :], ht_ps[m % 2][:, 0:P]).then_inc(ht_ready, 1)
                if n >= 3:
                    m = n - 3
                    act.wait_ge(down_done, i - 2)
                    if m >= 4:
                        act.wait_ge(y_out[m % 4], (i - 3 - m % 4) * 4)
                    nc.scalar.copy(y_sb[:, m % 4, :], y_ps[m % 2][:, :]).then_inc(y_ready, 1)

            in_steps(act, step)

        @block.tensor
        def _(pe):
            def expert(i):
                return pe.value_load(te[0:1, bass.ds(i, 1)], min_val=0, max_val=E1 - 1)

            def step(i, n):
                if n < MAX_TILES:
                    pe.wait_ge(gathered[n % DEEP], (i - n % DEEP) * (16 // DEEP) + 16)
                    if n >= 2:
                        pe.wait_ge(xgt_ready, i - 1)
                    for c in range(CH):
                        last = nc.tensor.transpose(t_ps[n % 2][:, c * P:(c + 1) * P], xg[:, n % DEEP, c * P:(c + 1) * P],
                                                   ident[:, :])
                    last.then_inc(turned, 1)
                if 1 <= n <= MAX_TILES:
                    m = n - 1
                    e = expert(i - 1)
                    pe.wait_ge(xgt_ready, i)
                    if m >= 2:
                        pe.wait_ge(biased, i - 2)
                    for c in range(CH):
                        last = nc.tensor.matmul(u_ps[m % 2][:, 0:2 * INTER], xgt[:, m % 2, c, :],
                                                wr[:, bass.ds(e, 1), c * 2 * INTER:(c + 1) * 2 * INTER],
                                                start=(c == 0), stop=(c == CH - 1))
                    last.then_inc(up_done, 1)
                if 2 <= n <= MAX_TILES + 1:
                    m = n - 2
                    pe.wait_ge(h_ready, i - 1)
                    if m >= 2:
                        pe.wait_ge(ht_ready, i - 3)
                    nc.tensor.transpose(ht_ps[m % 2][:, 0:P], h_sb[:, m % 2, :], ident[:, :]).then_inc(h_turned, 1)
                if n >= 3:
                    m = n - 3
                    e = expert(i - 3)
                    pe.wait_ge(ht_ready, i - 2)
                    if m >= 2:
                        pe.wait_ge(y_ready, i - 4)
                    nc.tensor.matmul(y_ps[m % 2][:, :], ht_sb[:, m % 2, :], wr[:, bass.ds(e, 1), W3:B1],
                                     start=True, stop=True).then_inc(down_done, 1)

            in_steps(pe, step)

        @block.vector
        def _(dve):
            dve.wait_ge(b_here, 16)

            def step(i, n):
                if n >= MAX_TILES:
                    return
                e = dve.value_load(te[0:1, bass.ds(i, 1)], min_val=0, max_val=E1 - 1)
                if n >= 2:
                    dve.wait_ge(silu_done, i - 1)
                dve.wait_ge(up_done, i + 1)
                nc.vector.tensor_tensor(up_sb[:, n % 2, :], u_ps[n % 2][:, 0:2 * INTER],
                                        b_sb[:, bass.ds(e, 1), :].rearrange("p e n -> p (e n)"), ALU.add).then_inc(biased, 1)
                dve.wait_ge(silu_done, i + 1)
                if n >= 2:
                    dve.wait_ge(h_turned, i - 1)
                nc.vector.tensor_tensor(h_sb[:, n % 2, :], silu_sb[:, n % 2, :], up_sb[:, n % 2, INTER:2 * INTER],
                                        ALU.mult).then_inc(h_ready, 1)

            in_steps(dve, step)
            for m in range(2 * TILES):
                n, k = m // 2, m % 2
                dve.wait_ge(backed[m % 4], 16 * (m // 4 + 1))
                nc.vector.scalar_tensor_tensor(X[:, n, :], back[:, m % 4, :], gs[:, k, n:n + 1], X[:, n, :],
                                               ALU.mult, ALU.add).then_inc(combined, 1)
                dve.wait_ge(combined, m + 1)


def flamingo_gated_kernel(nc, x, ctx, ctx_t, gates4, w_qkvo, b_qkvo, ident_in, route_a, bw, desc, wq, wk, wv, wo,
                          rw, rows, tri, tok_ids, w_routed, w_shared, b_routed, b3, out):
    with ExitStack() as stack:
        def sb(name, shape, dtype=F32):
            return stack.enter_context(nc.sbuf_tensor(name, shape, dtype))

        X = sb("X", [P, TILES, DIM])
        tg = sb("tg", [P, 4])
        ident = sb("ident", [P, P])
        bn, mv, rstd = sb("bn", [P, TILES, 6]), sb("mv", [P, TILES, 2]), sb("rstd", [P, TILES])
        window_attention(nc, X, x, ctx, w_qkvo, b_qkvo, gates4, ident_in, tg, ident, bn, mv, rstd)
        with ExitStack() as weights_stack:
            shapes = (("wk_sb", [P, CH, KV * HD1], wk), ("wv_sb", [P, CH, KV * HD1], wv),
                      ("wq_sb", [P, CH, QH * HD1], wq), ("wo_sb", [P, KV * HC, DIM], wo))
            weights = [(weights_stack.enter_context(nc.sbuf_tensor(name, shape, F32)), src)
                       for name, shape, src in shapes]
            weights_in = [weights_stack.enter_context(nc.semaphore(f"{name}_in")) for name, _, _ in shapes]
            ht = weights_stack.enter_context(nc.sbuf_tensor("ht", [P, CH, OB, 2, TOK], F32))
            ctx_in = weights_stack.enter_context(nc.semaphore("ctx_in"))
            top1_lora(nc, X, route_a, bw, desc, tg, ident, bn, mv, rstd, weights, weights_in, ht, ctx_t, ctx_in)
            latent_attention(nc, X, ht, ctx_t, ctx_in, [w for w, _ in weights], weights_in, tg, ident, bn, mv, rstd)
        wr = sb("wr", [P, E1, W_COLS - 2])
        te = sb("te", [1, MAX_TILES], U32)
        slot_of = sb("slot_of", [P, 2, TILES], U32)
        tok_of = sb("tok_of", [P, MAX_TILES], U32)
        gs = sb("gs", [P, 2, TILES])
        xt = sb("xt", [P, CH, TILES * P])
        b_sb = xt[:, 0:2, :].rearrange("p c (e n) -> p (c e) n", n=2 * INTER)
        b_here = stack.enter_context(nc.semaphore("b_here"))
        xn_rows = nc.dram_tensor("xn_rows", (TILES * P, DIM), F32, kind="Internal").ap()
        y_rows = nc.dram_tensor("y_rows", (MAX_TILES * P, DIM), F32, kind="Internal").ap()
        table = nc.dram_tensor("table", (MAX_TILES * P, 1), F32, kind="Internal").ap()
        route(nc, X, tg, ident, bn, mv, rstd, wr, te, slot_of, tok_of, gs, xn_rows, table, rw, rows, tri, tok_ids,
              w_routed, w_shared, b3, xt, b_sb, b_routed, b_here)
        routed(nc, X, out, ident, wr, te, slot_of, tok_of, gs, xn_rows, y_rows, b_sb, b_here)


def laid_out(i):
    import numpy as np
    a = {k: np.asarray(v) for k, v in i.items()}

    def by_chunk(w):
        return w.reshape(-1, P, w.shape[1]).transpose(1, 0, 2)

    def twice(w):
        z = np.zeros((P, P), np.float32)
        z[:TOK, :TOK] = z[TOK:, TOK:] = w.T
        return z

    o = {}
    o["x"] = a["x"].reshape(TILES, P, DIM)
    o["ctx"] = a["ctx_4096"].reshape(TILES, P, DIM)
    o["ctx_t"] = a["ctx_4096"].reshape(OCTETS, DIM, CH, P).transpose(0, 3, 2, 1)
    g = np.stack([a["g_xattn"][0], a["g_ffn"][0], a["g_xattn"][1], a["g_ffn"][1]])
    o["gates4"] = np.broadcast_to(g, (P, 4))
    o["w_qkvo"] = np.stack([twice(a[f"L0_xattn_W{k}"]) for k in "qkvo"], axis=1)
    o["b_qkvo"] = np.stack([np.tile(a[f"L0_xattn_b{k}"], 2) for k in "qkvo"], axis=1)
    o["ident_in"] = np.eye(P, dtype=np.float32)
    o["route_a"] = by_chunk(np.concatenate([a["L0_ffn_route_w"], a["L0_ffn_A"].reshape(-1, DIM)]).T)
    o["bw"] = a["L0_ffn_Bw"].transpose(0, 2, 1).reshape(P, DIM)
    o["desc"] = np.broadcast_to(np.arange(LORA_E, 0, -1, dtype=np.float32), (P, LORA_E))
    piece = np.arange(PIECE)
    order = np.concatenate([np.r_[c * HD1:(c + 1) * HD1, HC * HD1 + c * PIECE + piece] for c in range(HC)])
    packed = np.concatenate([k * G * HD1 + order for k in range(KV)])
    o["wq"], o["wk"], o["wv"] = (by_chunk(w.T) for w in (a["L1_xattn_Wq"][packed], a["L1_xattn_Wk"][order], a["L1_xattn_Wv"]))
    o["wo"] = by_chunk(a["L1_xattn_Wo"].T[packed])
    o["rw"] = by_chunk(a["L1_ffn_router_w"])
    parts = {"router_b": a["L1_ffn_router_b"], "router_bias": a["L1_ffn_router_bias"],
             "order": np.arange(E1, 0, -1), "order_g": np.arange(EGROUPS, 0, -1), "steps": np.arange(E1) * P,
             "upto": np.tril(np.ones((E1, E1))).ravel(), "tile": np.arange(MAX_TILES)}
    o["rows"] = np.broadcast_to(np.concatenate([parts[k].astype(np.float32) for k, _ in ROW_PARTS]), (P, ROWS))
    o["tri"] = np.triu(np.ones((P, P), np.float32), 1)
    o["tok_ids"] = np.arange(TILES * P, dtype=np.float32).reshape(TILES, P).T

    def up(k):
        routed = a[f"L1_ffn_ew{k}"].reshape(E1, CH, P, INTER).transpose(0, 2, 1, 3)
        shared = a[f"L1_ffn_sw{k}"].reshape(CH, P, SHARED, INTER).transpose(2, 1, 0, 3)
        return np.concatenate([routed, shared])

    w12 = np.stack([up(1), up(2)], axis=3).reshape(EXPERTS, P, W3)
    w3 = np.concatenate([a["L1_ffn_ew3"], a["L1_ffn_sw3"].reshape(SHARED, INTER, DIM)])
    b12 = np.stack([np.concatenate([a[f"L1_ffn_eb{k}"], a[f"L1_ffn_sb{k}"].reshape(SHARED, INTER)])
                    for k in (1, 2)], axis=2)
    o["w_routed"] = np.concatenate([w12, w3], axis=2)[:E1]
    o["w_shared"] = np.concatenate([w12, w3, b12], axis=2)[E1:].transpose(1, 0, 2)
    b_routed = np.concatenate([a["L1_ffn_eb1"], a["L1_ffn_eb2"]], axis=1)
    o["b_routed"] = np.broadcast_to(b_routed, (P, E1, 2 * INTER))
    o["b3"] = np.concatenate([a["L1_ffn_eb3"], a["L1_ffn_sb3"][None]])
    return {k: np.ascontiguousarray(v) for k, v in o.items()}


def kernel(**inputs):
    import concourse.bacc as bacc
    from concourse.bass_utils import run_bass_kernel_spmd

    arrays = laid_out(inputs)
    nc = bacc.Bacc("TRN2", target_bir_lowering=False, num_devices=1)
    args = {k: nc.dram_tensor(f"in_{k}", v.shape, mybir.dt.from_np(v.dtype), kind="ExternalInput").ap()
            for k, v in arrays.items()}
    out = nc.dram_tensor("out_0", (TILES, P, DIM), F32, kind="ExternalOutput").ap()
    flamingo_gated_kernel(nc, out=out, **args)
    got = run_bass_kernel_spmd(nc, [{f"in_{k}": v for k, v in arrays.items()}], core_ids=[0])
    return got.results[0]["out_0"].reshape(BATCH, TOK, DIM)
```
